# Optimizing a Trainium2 kernel written in Bass

```python
import numpy as np
import jax
import jax.numpy as jnp

def _softmax(x, axis=-1):
    return jax.nn.softmax(x, axis=axis)

def _gelu(x):
    return jax.nn.gelu(x, approximate=True)

def _silu(x):
    return jax.nn.silu(x)

def _sigmoid(x):
    return jax.nn.sigmoid(x)

def _layernorm(x, axis=-1, eps=1e-05):
    m = jnp.mean(x, axis=axis, keepdims=True)
    v = jnp.var(x, axis=axis, keepdims=True)
    return (x - m) / jnp.sqrt(v + eps)

def _scatter_add(tgt, idx, src, axis=0):
    return tgt.at[idx].add(src)

def _segment_sum(src, seg, n):
    return jax.ops.segment_sum(src, seg, n)
kernel_name = 'mk_flamingo_gated_d4_seqx_r8_fefd38'

def setup_inputs(seed: int=0):
    np.random.seed(seed)
    _w = jnp.asarray

    def _rec_inputs():
        import jax
        import jax.numpy as jnp
        _rk = jax.random.key(seed)
        x = -0.0003929 + 0.9999 * jax.random.normal(jax.random.fold_in(_rk, 1), (2, 512, 128), jnp.float32)
        _lenS = 512 - jax.random.randint(jax.random.fold_in(_rk, 7), (2,), 0, max(1, 512 // 4) + 1, jnp.int32)
        _lenS2 = 154 - jax.random.randint(jax.random.fold_in(_rk, 8), (2,), 0, max(1, 154 // 4) + 1, jnp.int32)
        _ctx_768P = jax.random.normal(jax.random.fold_in(_rk, 11), (2, 16, 96), jnp.float32)
        _ctx_768c = jax.random.dirichlet(jax.random.fold_in(_rk, 511), 0.3 * jnp.ones((16,), jnp.float32), (2, 154))
        _ctx_768t = jnp.einsum('bsk,bkd->bsd', _ctx_768c, _ctx_768P)
        _ctx_768t = _ctx_768t * jax.lax.rsqrt(jnp.mean(jnp.square(_ctx_768t)) + 1e-12) * 0.953939
        ctx_768 = -0.00055796 + 0.999787 * (_ctx_768t + 0.3 * jax.random.normal(jax.random.fold_in(_rk, 611), (2, 154, 96), jnp.float32))
        _g = jax.random.normal(jax.random.fold_in(_rk, 9001), (2, 4), jnp.float32)
        _g = jnp.sign(_g) * jnp.maximum(jnp.abs(_g), 1.0) + (_g == 0) * 1.0
        g_xattn = _g[0]
        g_ffn = _g[1]
        return (x, ctx_768, g_xattn, g_ffn)
    x, ctx_768, g_xattn, g_ffn = _rec_inputs()

    def _L0_xattn_setup():
        import jax, jax.numpy as jnp
        import numpy as np
        IMAGE_DIM = 128
        TEXT_DIM = 96
        NUM_HEADS = 16
        HEAD_DIM = IMAGE_DIM // NUM_HEADS
        key = jax.random.key(seed)
        ks = jax.random.split(key, 14)
        B, N, M = (4, 512, 64)
        s_img = 1.0 / np.sqrt(IMAGE_DIM)
        s_txt = 1.0 / np.sqrt(TEXT_DIM)
        s_ff = 1.0 / np.sqrt(2 * IMAGE_DIM)
        return {'x': jax.random.normal(ks[0], (B, N, IMAGE_DIM), jnp.float32), 'y': jax.random.normal(ks[1], (B, M, TEXT_DIM), jnp.float32), 'Wq': jax.random.normal(ks[2], (IMAGE_DIM, IMAGE_DIM), jnp.float32) * s_img, 'bq': jax.random.normal(ks[3], (IMAGE_DIM,), jnp.float32) * s_img, 'Wk': jax.random.normal(ks[4], (TEXT_DIM, IMAGE_DIM), jnp.float32) * s_txt, 'bk': jax.random.normal(ks[5], (IMAGE_DIM,), jnp.float32) * s_txt, 'Wv': jax.random.normal(ks[6], (TEXT_DIM, IMAGE_DIM), jnp.float32) * s_txt, 'bv': jax.random.normal(ks[7], (IMAGE_DIM,), jnp.float32) * s_txt, 'W1': jax.random.normal(ks[8], (IMAGE_DIM, 2 * IMAGE_DIM), jnp.float32) * s_img, 'b1': jax.random.normal(ks[9], (2 * IMAGE_DIM,), jnp.float32) * s_img, 'W2': jax.random.normal(ks[10], (2 * IMAGE_DIM, IMAGE_DIM), jnp.float32) * s_ff, 'b2': jax.random.normal(ks[11], (IMAGE_DIM,), jnp.float32) * s_ff}
    _L0_xattn_all = _L0_xattn_setup()
    _L0_xattn_in = {k: v for k, v in _L0_xattn_all.items() if k in ('Wq', 'bq', 'Wk', 'bk', 'Wv', 'bv', 'W1', 'b1', 'W2', 'b2')}
    del _L0_xattn_all

    def _L0_ffn_setup():
        import jax, jax.numpy as jnp
        import numpy as np
        K = 4
        ROUTED_SCALING = 1.0
        NORM_TOPK = True

        def _gate(hidden_states, router_w, router_bias):
            logits = jnp.einsum('bsh,he->bse', hidden_states, router_w).astype(jnp.float32)
            scores = jax.nn.softmax(logits, axis=-1)
            corrected = scores + router_bias
            _, top_k_indices = jax.lax.top_k(corrected, K)
            top_k_weights = jnp.take_along_axis(scores, top_k_indices, axis=-1)
            if NORM_TOPK:
                top_k_weights = top_k_weights / (top_k_weights.sum(-1, keepdims=True) + 1e-20)
            top_k_weights = top_k_weights * ROUTED_SCALING
            return (top_k_weights.astype(hidden_states.dtype), top_k_indices)
        key = jax.random.key(seed)
        ks = jax.random.split(key, 9)
        B, S, H, E, I, IS = (2, 128, 128, 8, 64, 256)
        sc = 0.02
        return {'hidden_states': jax.random.normal(ks[0], (B, S, H), jnp.float32), 'router_w': jax.random.normal(ks[1], (H, E), jnp.float32) * sc, 'router_bias': jnp.zeros((), jnp.float32), 'gate_w': jax.random.normal(ks[2], (E, H, I), jnp.float32) * sc, 'up_w': jax.random.normal(ks[3], (E, H, I), jnp.float32) * sc, 'down_w': jax.random.normal(ks[4], (E, I, H), jnp.float32) * sc, 's_gate_w': jax.random.normal(ks[5], (H, IS), jnp.float32) * sc, 's_up_w': jax.random.normal(ks[6], (H, IS), jnp.float32) * sc, 's_down_w': jax.random.normal(ks[7], (IS, H), jnp.float32) * sc}
    _L0_ffn_all = _L0_ffn_setup()
    _L0_ffn_in = {k: v for k, v in _L0_ffn_all.items() if k in ('router_w', 'router_bias', 'gate_w', 'up_w', 'down_w', 's_gate_w', 's_up_w', 's_down_w')}
    del _L0_ffn_all

    def _L1_xattn_setup():
        import jax, jax.numpy as jnp
        import numpy as np
        import math
        E = 128
        EV = 128
        FFN = 512
        DINO = 96
        B, S, P = (64, 64, 32)

        def bitnet_linear(x, W, b):
            w_scale = jnp.maximum(jnp.mean(jnp.abs(W)), 1e-05)
            qW = jnp.sign(W) * (jnp.abs(W) > 0.5 * w_scale).astype(W.dtype)
            i_scale = jnp.maximum(jnp.max(jnp.abs(x)), 1e-08) / 127.0
            qx = jnp.clip(jnp.round(x / i_scale), -128.0, 127.0)
            out = jnp.einsum('...i,oi->...o', qx, qW) * (w_scale * i_scale)
            return out + b
        key = jax.random.key(seed)
        ks = iter(jax.random.split(key, 32))

        def lin_w(fin, fout):
            return jax.random.normal(next(ks), (fout, fin), jnp.float32) * math.sqrt(2.0 / fin)
        return {'text_embeddings': jax.random.normal(next(ks), (B, S, E), jnp.float32), 'dinov2_features': jax.random.normal(next(ks), (B, P, DINO), jnp.float32), 'W_d2v': lin_w(DINO, EV), 'b_d2v': jnp.zeros((EV,), jnp.float32), 'W_img': lin_w(EV, E), 'b_img': jnp.zeros((E,), jnp.float32), 'W_txt': lin_w(E, E), 'b_txt': jnp.zeros((E,), jnp.float32), 'W_att0': lin_w(E, E // 2), 'b_att0': jnp.zeros((E // 2,), jnp.float32), 'W_att1': lin_w(E, E // 2), 'b_att1': jnp.zeros((E // 2,), jnp.float32), 'W_f1': lin_w(2 * E, FFN), 'b_f1': jnp.zeros((FFN,), jnp.float32), 'W_f2': lin_w(FFN, E), 'b_f2': jnp.zeros((E,), jnp.float32)}
    _L1_xattn_all = _L1_xattn_setup()
    _L1_xattn_in = {k: v for k, v in _L1_xattn_all.items() if k in ('W_d2v', 'b_d2v', 'W_img', 'b_img', 'W_txt', 'b_txt', 'W_att0', 'b_att0', 'W_att1', 'b_att1', 'W_f1', 'b_f1', 'W_f2', 'b_f2')}
    del _L1_xattn_all

    def _L1_ffn_setup():
        import math
        import jax, jax.numpy as jnp
        import numpy as np
        NUM_EXPERTS = 8
        CAPACITY_FACTOR = 1.5
        key = jax.random.key(seed)
        ks = jax.random.split(key, 4)
        B, T, D, F, E = (4, 256, 128, 512, NUM_EXPERTS)
        scale = 0.02
        return {'x': jax.random.normal(ks[0], (B, T, D), dtype=jnp.float32), 'router_w': jax.random.normal(ks[1], (E, D), dtype=jnp.float32) * scale, 'w1': jax.random.normal(ks[2], (E, D, F), dtype=jnp.float32) * scale, 'b1': jnp.zeros((E, F), dtype=jnp.float32), 'w2': jax.random.normal(ks[3], (E, F, D), dtype=jnp.float32) * scale, 'b2': jnp.zeros((E, D), dtype=jnp.float32)}
    _L1_ffn_all = _L1_ffn_setup()
    _L1_ffn_in = {k: v for k, v in _L1_ffn_all.items() if k in ('router_w', 'w1', 'b1', 'w2', 'b2')}
    del _L1_ffn_all

    def _L2_xattn_setup():
        import jax, jax.numpy as jnp
        import numpy as np
        N_HEADS = 16
        key = jax.random.key(seed)
        ks = jax.random.split(key, 8)
        b, l, m = (8, 128, 128)
        d_embed, d_cross = (128, 96)
        s_q = 1.0 / np.sqrt(d_embed)
        s_kv = 1.0 / np.sqrt(d_cross)
        return {'x': jax.random.normal(ks[0], (b, l, d_embed), jnp.float32), 'y': jax.random.normal(ks[1], (b, m, d_cross), jnp.float32), 'Wq': jax.random.normal(ks[2], (d_embed, d_embed), jnp.float32) * s_q, 'bq': jax.random.normal(ks[3], (d_embed,), jnp.float32) * 0.01, 'Wkv': jax.random.normal(ks[4], (2 * d_embed, d_cross), jnp.float32) * s_kv, 'bkv': jax.random.normal(ks[5], (2 * d_embed,), jnp.float32) * 0.01, 'Wo': jax.random.normal(ks[6], (d_embed, d_embed), jnp.float32) * s_q, 'bo': jax.random.normal(ks[7], (d_embed,), jnp.float32) * 0.01}
    _L2_xattn_all = _L2_xattn_setup()
    _L2_xattn_in = {k: v for k, v in _L2_xattn_all.items() if k in ('Wq', 'bq', 'Wkv', 'bkv', 'Wo', 'bo')}
    del _L2_xattn_all

    def _L2_ffn_setup():
        import jax, jax.numpy as jnp
        import numpy as np
        B, S, D = (4, 512, 128)
        E, F_EXP = (16, 256)
        F_C = 2.0
        F_SH = 256
        key = jax.random.key(seed)
        ks = jax.random.split(key, 8)
        s = 0.02
        return {'hidden_states': jax.random.normal(ks[0], (B, S, D), jnp.float32), 'gate_w': jax.random.normal(ks[1], (E, D), jnp.float32) * s, 'Wg': jax.random.normal(ks[2], (E, F_EXP, D), jnp.float32) * s, 'Wu': jax.random.normal(ks[3], (E, F_EXP, D), jnp.float32) * s, 'Wd': jax.random.normal(ks[4], (E, D, F_EXP), jnp.float32) * s, 'Ws_g': jax.random.normal(ks[5], (F_SH, D), jnp.float32) * s, 'Ws_u': jax.random.normal(ks[6], (F_SH, D), jnp.float32) * s, 'Ws_d': jax.random.normal(ks[7], (D, F_SH), jnp.float32) * s}
    _L2_ffn_all = _L2_ffn_setup()
    _L2_ffn_in = {k: v for k, v in _L2_ffn_all.items() if k in ('gate_w', 'Wg', 'Wu', 'Wd', 'Ws_g', 'Ws_u', 'Ws_d')}
    del _L2_ffn_all

    def _L3_xattn_setup():
        import jax, jax.numpy as jnp
        import numpy as np
        HEADS = 16
        DIM_HEAD = 64
        key = jax.random.key(seed)
        ks = jax.random.split(key, 7)
        b, n, m = (2, 256, 128)
        query_dim, context_dim = (128, 96)
        inner = HEADS * DIM_HEAD
        s_q = 1.0 / np.sqrt(query_dim)
        s_c = 1.0 / np.sqrt(context_dim)
        s_i = 1.0 / np.sqrt(inner)
        return {'x': jax.random.normal(ks[0], (b, n, query_dim), jnp.float32), 'context': jax.random.normal(ks[1], (b, m, context_dim), jnp.float32), 'Wq': jax.random.normal(ks[2], (query_dim, inner), jnp.float32) * s_q, 'Wk': jax.random.normal(ks[3], (context_dim, inner), jnp.float32) * s_c, 'Wv': jax.random.normal(ks[4], (context_dim, inner), jnp.float32) * s_c, 'Wo': jax.random.normal(ks[5], (inner, query_dim), jnp.float32) * s_i, 'bo': jax.random.normal(ks[6], (query_dim,), jnp.float32) * 0.01}
    _L3_xattn_all = _L3_xattn_setup()
    _L3_xattn_in = {k: v for k, v in _L3_xattn_all.items() if k in ('Wq', 'Wk', 'Wv', 'Wo', 'bo')}
    del _L3_xattn_all

    def _L3_ffn_setup():
        import jax, jax.numpy as jnp
        import numpy as np
        D = 128
        H = 96
        E = 8
        K = 2
        NS = 2
        ROUTE_SCALE = 1.0

        def _gated_mlp(x, w1, w2):
            h = x @ w1.T
            y, g = jnp.split(h, 2, axis=-1)
            return y * jax.nn.silu(g) @ w2.T
        key = jax.random.key(seed)
        ks = jax.random.split(key, 6)
        s = 0.02
        return {'x': jax.random.normal(ks[0], (2, 128, D), jnp.float32), 'gate_w': jax.random.normal(ks[1], (E, D), jnp.float32) * s, 'W1': jax.random.normal(ks[2], (E, 2 * H, D), jnp.float32) * s, 'W2': jax.random.normal(ks[3], (E, D, H), jnp.float32) * s, 'Ws1': jax.random.normal(ks[4], (2 * NS * H, D), jnp.float32) * s, 'Ws2': jax.random.normal(ks[5], (D, NS * H), jnp.float32) * s}
    _L3_ffn_all = _L3_ffn_setup()
    _L3_ffn_in = {k: v for k, v in _L3_ffn_all.items() if k in ('gate_w', 'W1', 'W2', 'Ws1', 'Ws2')}
    del _L3_ffn_all
    return {'x': x, 'ctx_768': ctx_768, 'g_xattn': g_xattn, 'g_ffn': g_ffn, 'L0_xattn_Wq': _L0_xattn_in['Wq'], 'L0_xattn_bq': _L0_xattn_in['bq'], 'L0_xattn_Wk': _L0_xattn_in['Wk'], 'L0_xattn_bk': _L0_xattn_in['bk'], 'L0_xattn_Wv': _L0_xattn_in['Wv'], 'L0_xattn_bv': _L0_xattn_in['bv'], 'L0_xattn_W1': _L0_xattn_in['W1'], 'L0_xattn_b1': _L0_xattn_in['b1'], 'L0_xattn_W2': _L0_xattn_in['W2'], 'L0_xattn_b2': _L0_xattn_in['b2'], 'L0_ffn_router_w': _L0_ffn_in['router_w'], 'L0_ffn_router_bias': _L0_ffn_in['router_bias'], 'L0_ffn_gate_w': _L0_ffn_in['gate_w'], 'L0_ffn_up_w': _L0_ffn_in['up_w'], 'L0_ffn_down_w': _L0_ffn_in['down_w'], 'L0_ffn_s_gate_w': _L0_ffn_in['s_gate_w'], 'L0_ffn_s_up_w': _L0_ffn_in['s_up_w'], 'L0_ffn_s_down_w': _L0_ffn_in['s_down_w'], 'L1_xattn_W_d2v': _L1_xattn_in['W_d2v'], 'L1_xattn_b_d2v': _L1_xattn_in['b_d2v'], 'L1_xattn_W_img': _L1_xattn_in['W_img'], 'L1_xattn_b_img': _L1_xattn_in['b_img'], 'L1_xattn_W_txt': _L1_xattn_in['W_txt'], 'L1_xattn_b_txt': _L1_xattn_in['b_txt'], 'L1_xattn_W_att0': _L1_xattn_in['W_att0'], 'L1_xattn_b_att0': _L1_xattn_in['b_att0'], 'L1_xattn_W_att1': _L1_xattn_in['W_att1'], 'L1_xattn_b_att1': _L1_xattn_in['b_att1'], 'L1_xattn_W_f1': _L1_xattn_in['W_f1'], 'L1_xattn_b_f1': _L1_xattn_in['b_f1'], 'L1_xattn_W_f2': _L1_xattn_in['W_f2'], 'L1_xattn_b_f2': _L1_xattn_in['b_f2'], 'L1_ffn_router_w': _L1_ffn_in['router_w'], 'L1_ffn_w1': _L1_ffn_in['w1'], 'L1_ffn_b1': _L1_ffn_in['b1'], 'L1_ffn_w2': _L1_ffn_in['w2'], 'L1_ffn_b2': _L1_ffn_in['b2'], 'L2_xattn_Wq': _L2_xattn_in['Wq'], 'L2_xattn_bq': _L2_xattn_in['bq'], 'L2_xattn_Wkv': _L2_xattn_in['Wkv'], 'L2_xattn_bkv': _L2_xattn_in['bkv'], 'L2_xattn_Wo': _L2_xattn_in['Wo'], 'L2_xattn_bo': _L2_xattn_in['bo'], 'L2_ffn_gate_w': _L2_ffn_in['gate_w'], 'L2_ffn_Wg': _L2_ffn_in['Wg'], 'L2_ffn_Wu': _L2_ffn_in['Wu'], 'L2_ffn_Wd': _L2_ffn_in['Wd'], 'L2_ffn_Ws_g': _L2_ffn_in['Ws_g'], 'L2_ffn_Ws_u': _L2_ffn_in['Ws_u'], 'L2_ffn_Ws_d': _L2_ffn_in['Ws_d'], 'L3_xattn_Wq': _L3_xattn_in['Wq'], 'L3_xattn_Wk': _L3_xattn_in['Wk'], 'L3_xattn_Wv': _L3_xattn_in['Wv'], 'L3_xattn_Wo': _L3_xattn_in['Wo'], 'L3_xattn_bo': _L3_xattn_in['bo'], 'L3_ffn_gate_w': _L3_ffn_in['gate_w'], 'L3_ffn_W1': _L3_ffn_in['W1'], 'L3_ffn_W2': _L3_ffn_in['W2'], 'L3_ffn_Ws1': _L3_ffn_in['Ws1'], 'L3_ffn_Ws2': _L3_ffn_in['Ws2']}

def reference(x, ctx_768, g_xattn, g_ffn, L0_xattn_Wq, L0_xattn_bq, L0_xattn_Wk, L0_xattn_bk, L0_xattn_Wv, L0_xattn_bv, L0_xattn_W1, L0_xattn_b1, L0_xattn_W2, L0_xattn_b2, L0_ffn_router_w, L0_ffn_router_bias, L0_ffn_gate_w, L0_ffn_up_w, L0_ffn_down_w, L0_ffn_s_gate_w, L0_ffn_s_up_w, L0_ffn_s_down_w, L1_xattn_W_d2v, L1_xattn_b_d2v, L1_xattn_W_img, L1_xattn_b_img, L1_xattn_W_txt, L1_xattn_b_txt, L1_xattn_W_att0, L1_xattn_b_att0, L1_xattn_W_att1, L1_xattn_b_att1, L1_xattn_W_f1, L1_xattn_b_f1, L1_xattn_W_f2, L1_xattn_b_f2, L1_ffn_router_w, L1_ffn_w1, L1_ffn_b1, L1_ffn_w2, L1_ffn_b2, L2_xattn_Wq, L2_xattn_bq, L2_xattn_Wkv, L2_xattn_bkv, L2_xattn_Wo, L2_xattn_bo, L2_ffn_gate_w, L2_ffn_Wg, L2_ffn_Wu, L2_ffn_Wd, L2_ffn_Ws_g, L2_ffn_Ws_u, L2_ffn_Ws_d, L3_xattn_Wq, L3_xattn_Wk, L3_xattn_Wv, L3_xattn_Wo, L3_xattn_bo, L3_ffn_gate_w, L3_ffn_W1, L3_ffn_W2, L3_ffn_Ws1, L3_ffn_Ws2):
    import jax
    import jax.numpy as jnp

    def _L0_xattn_ref(x, y, Wq, bq, Wk, bk, Wv, bv, W1, b1, W2, b2):
        import jax, jax.numpy as jnp
        import numpy as np
        IMAGE_DIM = 128
        TEXT_DIM = 96
        NUM_HEADS = 16
        HEAD_DIM = IMAGE_DIM // NUM_HEADS
        B, N, _ = x.shape
        M = y.shape[1]
        q = (x @ Wq + bq).reshape(B, N, NUM_HEADS, HEAD_DIM)
        k = (y @ Wk + bk).reshape(B, M, NUM_HEADS, HEAD_DIM)
        v = (y @ Wv + bv).reshape(B, M, NUM_HEADS, HEAD_DIM)
        scale = 1.0 / np.sqrt(HEAD_DIM)
        scores = jnp.einsum('bnhd,bmhd->bhnm', q, k) * scale
        attn = jax.nn.softmax(scores, axis=-1)
        out = jnp.einsum('bhnm,bmhd->bnhd', attn, v).reshape(B, N, IMAGE_DIM)
        h = jax.nn.relu(out @ W1 + b1)
        return h @ W2 + b2

    def _L0_ffn_ref(hidden_states, router_w, router_bias, gate_w, up_w, down_w, s_gate_w, s_up_w, s_down_w):
        import jax, jax.numpy as jnp
        import numpy as np
        K = 4
        ROUTED_SCALING = 1.0
        NORM_TOPK = True

        def _gate(hidden_states, router_w, router_bias):
            logits = jnp.einsum('bsh,he->bse', hidden_states, router_w).astype(jnp.float32)
            scores = jax.nn.softmax(logits, axis=-1)
            corrected = scores + router_bias
            _, top_k_indices = jax.lax.top_k(corrected, K)
            top_k_weights = jnp.take_along_axis(scores, top_k_indices, axis=-1)
            if NORM_TOPK:
                top_k_weights = top_k_weights / (top_k_weights.sum(-1, keepdims=True) + 1e-20)
            top_k_weights = top_k_weights * ROUTED_SCALING
            return (top_k_weights.astype(hidden_states.dtype), top_k_indices)
        B, S, H = hidden_states.shape
        tk_w, tk_i = _gate(hidden_states, router_w, router_bias)
        hf = hidden_states.reshape(-1, H)
        tk_w = tk_w.reshape(-1, K)
        tk_i = tk_i.reshape(-1, K)
        gate_all = jnp.einsum('nh,ehi->nei', hf, gate_w)
        up_all = jnp.einsum('nh,ehi->nei', hf, up_w)
        act = jax.nn.silu(gate_all) * up_all
        down_all = jnp.einsum('nei,eih->neh', act, down_w)
        sel = jnp.take_along_axis(down_all, tk_i[:, :, None], axis=1)
        routed = (sel * tk_w[:, :, None]).sum(axis=1).reshape(B, S, H)
        g = jnp.einsum('bsh,hm->bsm', hidden_states, s_gate_w)
        u = jnp.einsum('bsh,hm->bsm', hidden_states, s_up_w)
        shared = jnp.einsum('bsm,mh->bsh', jax.nn.silu(g) * u, s_down_w)
        return routed + shared

    def _L1_xattn_ref(text_embeddings, dinov2_features, W_d2v, b_d2v, W_img, b_img, W_txt, b_txt, W_att0, b_att0, W_att1, b_att1, W_f1, b_f1, W_f2, b_f2):
        import jax, jax.numpy as jnp
        import numpy as np
        import math
        E = 128
        EV = 128
        FFN = 512
        DINO = 96
        B, S, P = (64, 64, 32)

        def bitnet_linear(x, W, b):
            w_scale = jnp.maximum(jnp.mean(jnp.abs(W)), 1e-05)
            qW = jnp.sign(W) * (jnp.abs(W) > 0.5 * w_scale).astype(W.dtype)
            i_scale = jnp.maximum(jnp.max(jnp.abs(x)), 1e-08) / 127.0
            qx = jnp.clip(jnp.round(x / i_scale), -128.0, 127.0)
            out = jnp.einsum('...i,oi->...o', qx, qW) * (w_scale * i_scale)
            return out + b
        b, s, e = text_embeddings.shape
        vis = bitnet_linear(dinov2_features, W_d2v, b_d2v)
        image_embeds = bitnet_linear(vis, W_img, b_img)
        fused = bitnet_linear(text_embeddings, W_txt, b_txt)
        inv_sqrt_e = 1.0 / math.sqrt(e)
        for Wa, ba in ((W_att0, b_att0), (W_att1, b_att1)):
            kv = bitnet_linear(image_embeds, Wa, ba)
            k = jnp.concatenate([kv, kv], axis=-1)
            scores = jnp.einsum('bse,bpe->bsp', fused, k) * inv_sqrt_e
            attn = jax.nn.softmax(scores, axis=-1)
            fused = fused + 0.1 * jnp.einsum('bsp,bpe->bse', attn, k)
        avg_img = jnp.mean(image_embeds, axis=1, keepdims=True)
        concatenated = jnp.concatenate([fused, jnp.broadcast_to(avg_img, (b, s, e))], axis=-1)
        h = jax.nn.relu(bitnet_linear(concatenated, W_f1, b_f1))
        return bitnet_linear(h, W_f2, b_f2)

    def _L1_ffn_ref(x, router_w, w1, b1, w2, b2):
        import math
        import jax, jax.numpy as jnp
        import numpy as np
        NUM_EXPERTS = 8
        CAPACITY_FACTOR = 1.5
        B, T, D = x.shape
        E = router_w.shape[0]
        N = B * T
        C = max(math.ceil(CAPACITY_FACTOR * N / E), 1)
        x_flat = x.reshape(N, D)
        logits = x_flat @ router_w.T
        probs = jax.nn.softmax(logits, axis=-1)
        chosen_e = jnp.argmax(probs, axis=-1)
        chosen_p = jnp.max(probs, axis=-1)
        onehot = jax.nn.one_hot(chosen_e, E, dtype=jnp.float32)
        pos = jnp.take_along_axis(jnp.cumsum(onehot, axis=0), chosen_e[:, None], axis=1)[:, 0] - 1.0
        pos = pos.astype(jnp.int32)
        kept = pos < C
        pos_c = jnp.clip(pos, 0, C - 1)
        buf = jnp.zeros((E, C, D), dtype=x.dtype).at[chosen_e, pos_c].add(x_flat * kept[:, None].astype(x.dtype))
        h = jax.nn.gelu(jnp.einsum('ecd,edf->ecf', buf, w1) + b1[:, None, :], approximate=False)
        eo = jnp.einsum('ecf,efd->ecd', h, w2) + b2[:, None, :]
        y = eo[chosen_e, pos_c] * (chosen_p * kept.astype(x.dtype))[:, None]
        return y.reshape(B, T, D)

    def _L2_xattn_ref(x, y, Wq, bq, Wkv, bkv, Wo, bo):
        import jax, jax.numpy as jnp
        import numpy as np
        N_HEADS = 16
        b, l, d = x.shape
        m = y.shape[1]
        h = N_HEADS
        dh = d // h
        q = (jnp.einsum('bld,ed->ble', x, Wq) + bq).reshape(b, l, h, dh)
        kv = (jnp.einsum('bmc,ec->bme', y, Wkv) + bkv).reshape(b, m, h, 2 * dh)
        k, v = (kv[..., :dh], kv[..., dh:])
        scale = 1.0 / jnp.sqrt(jnp.asarray(dh, x.dtype))
        att = jax.nn.softmax(jnp.einsum('blhd,bmhd->blmh', q, k) * scale, axis=2)
        out = jnp.einsum('blmh,bmhd->blhd', att, v).reshape(b, l, d)
        return jnp.einsum('bld,ed->ble', out, Wo) + bo

    def _L2_ffn_ref(hidden_states, gate_w, Wg, Wu, Wd, Ws_g, Ws_u, Ws_d):
        import jax, jax.numpy as jnp
        import numpy as np
        B, S, D = (4, 512, 128)
        E, F_EXP = (16, 256)
        F_C = 2.0
        F_SH = 256
        b, s, d = hidden_states.shape
        e = gate_w.shape[0]
        cap = int(s * F_C / e)
        logits = jnp.einsum('bsd,ed->bse', hidden_states, gate_w)
        scores = jax.nn.softmax(logits, axis=-1).transpose(0, 2, 1)
        topk_w, topk_idx = jax.lax.top_k(scores, cap)
        x_tok = jnp.take_along_axis(hidden_states[:, None, :, :], topk_idx[..., None], axis=2)
        g = jnp.einsum('becd,efd->becf', x_tok, Wg)
        u = jnp.einsum('becd,efd->becf', x_tok, Wu)
        h = jax.nn.gelu(g, approximate=False) * u
        eo = jnp.einsum('becf,edf->becd', h, Wd) * topk_w[..., None]
        offs = (jnp.arange(b) * s)[:, None, None]
        flat_idx = (topk_idx + offs).reshape(-1)
        flat = jnp.zeros((b * s, d), hidden_states.dtype)
        flat = flat.at[flat_idx].add(eo.reshape(-1, d))
        out = flat.reshape(b, s, d)
        gs = jnp.einsum('bsd,fd->bsf', hidden_states, Ws_g)
        us = jnp.einsum('bsd,fd->bsf', hidden_states, Ws_u)
        shared = jnp.einsum('bsf,df->bsd', jax.nn.gelu(gs, approximate=False) * us, Ws_d)
        return out + shared

    def _L3_xattn_ref(x, context, Wq, Wk, Wv, Wo, bo):
        import jax, jax.numpy as jnp
        import numpy as np
        HEADS = 16
        DIM_HEAD = 64
        b, n, _ = x.shape
        h, d = (HEADS, DIM_HEAD)
        scale = d ** (-0.5)
        q = (x @ Wq).reshape(b, n, h, d).transpose(0, 2, 1, 3)
        k = (context @ Wk).reshape(b, -1, h, d).transpose(0, 2, 1, 3)
        v = (context @ Wv).reshape(b, -1, h, d).transpose(0, 2, 1, 3)
        sim = jnp.einsum('bhid,bhjd->bhij', q, k) * scale
        attn = jax.nn.softmax(sim, axis=-1)
        out = jnp.einsum('bhij,bhjd->bhid', attn, v)
        out = out.transpose(0, 2, 1, 3).reshape(b, n, h * d)
        return out @ Wo + bo

    def _L3_ffn_ref(x, gate_w, W1, W2, Ws1, Ws2):
        import jax, jax.numpy as jnp
        import numpy as np
        D = 128
        H = 96
        E = 8
        K = 2
        NS = 2
        ROUTE_SCALE = 1.0

        def _gated_mlp(x, w1, w2):
            h = x @ w1.T
            y, g = jnp.split(h, 2, axis=-1)
            return y * jax.nn.silu(g) @ w2.T
        x_shape = x.shape
        xf = x.reshape(-1, D)
        T = xf.shape[0]
        scores = jax.nn.softmax((xf @ gate_w.T).astype(jnp.float32), axis=-1)
        top_vals, top_idx = jax.lax.top_k(scores, K)
        weights = (top_vals * ROUTE_SCALE).astype(x.dtype)
        w_dense = jnp.zeros((T, E), x.dtype).at[jnp.arange(T)[:, None], top_idx].set(weights)
        h = jnp.einsum('td,ehd->teh', xf, W1)
        y, g = jnp.split(h, 2, axis=-1)
        eo = jnp.einsum('teh,edh->ted', y * jax.nn.silu(g), W2)
        z = jnp.einsum('te,ted->td', w_dense, eo)
        z = z + _gated_mlp(xf, Ws1, Ws2)
        return z.reshape(x_shape)
    x = x + jnp.tanh(g_xattn[0]) * _L0_xattn_ref(_layernorm(x, axis=-1), ctx_768, L0_xattn_Wq, L0_xattn_bq, L0_xattn_Wk, L0_xattn_bk, L0_xattn_Wv, L0_xattn_bv, L0_xattn_W1, L0_xattn_b1, L0_xattn_W2, L0_xattn_b2)
    x = x + jnp.tanh(g_ffn[0]) * _L0_ffn_ref(_layernorm(x, axis=-1), L0_ffn_router_w, L0_ffn_router_bias, L0_ffn_gate_w, L0_ffn_up_w, L0_ffn_down_w, L0_ffn_s_gate_w, L0_ffn_s_up_w, L0_ffn_s_down_w)
    x = x + jnp.tanh(g_xattn[1]) * _L1_xattn_ref(_layernorm(x, axis=-1), ctx_768, L1_xattn_W_d2v, L1_xattn_b_d2v, L1_xattn_W_img, L1_xattn_b_img, L1_xattn_W_txt, L1_xattn_b_txt, L1_xattn_W_att0, L1_xattn_b_att0, L1_xattn_W_att1, L1_xattn_b_att1, L1_xattn_W_f1, L1_xattn_b_f1, L1_xattn_W_f2, L1_xattn_b_f2)
    x = x + jnp.tanh(g_ffn[1]) * _L1_ffn_ref(_layernorm(x, axis=-1), L1_ffn_router_w, L1_ffn_w1, L1_ffn_b1, L1_ffn_w2, L1_ffn_b2)
    x = x + jnp.tanh(g_xattn[2]) * _L2_xattn_ref(_layernorm(x, axis=-1), ctx_768, L2_xattn_Wq, L2_xattn_bq, L2_xattn_Wkv, L2_xattn_bkv, L2_xattn_Wo, L2_xattn_bo)
    x = x + jnp.tanh(g_ffn[2]) * _L2_ffn_ref(_layernorm(x, axis=-1), L2_ffn_gate_w, L2_ffn_Wg, L2_ffn_Wu, L2_ffn_Wd, L2_ffn_Ws_g, L2_ffn_Ws_u, L2_ffn_Ws_d)
    x = x + jnp.tanh(g_xattn[3]) * _L3_xattn_ref(_layernorm(x, axis=-1), ctx_768, L3_xattn_Wq, L3_xattn_Wk, L3_xattn_Wv, L3_xattn_Wo, L3_xattn_bo)
    x = x + jnp.tanh(g_ffn[3]) * _L3_ffn_ref(_layernorm(x, axis=-1), L3_ffn_gate_w, L3_ffn_W1, L3_ffn_W2, L3_ffn_Ws1, L3_ffn_Ws2)
    return x

_drawn_inputs = setup_inputs


def setup_inputs(seed=0):
    import zlib

    import numpy as np

    out = dict(_drawn_inputs(seed))
    spreads = {'L1_xattn_b_d2v': (0.0, 0.274),
     'L1_xattn_b_img': (0.0, 0.1),
     'L1_xattn_b_txt': (0.0, 0.1),
     'L1_xattn_b_att0': (0.0, 0.8),
     'L1_xattn_b_att1': (0.0, 0.8),
     'L1_xattn_b_f1': (0.0, 0.1),
     'L1_xattn_b_f2': (0.0, 0.1),
     'L1_ffn_b1': (0.0, 0.8),
     'L1_ffn_b2': (0.0, 0.615)}
    factors = {'g_ffn': 8.0,
     'L0_xattn_bq': 5.132,
     'L0_xattn_bk': 64.0,
     'L0_ffn_router_w': 8.0,
     'L0_ffn_gate_w': 8.0,
     'L0_ffn_up_w': 8.0,
     'L0_ffn_down_w': 8.0,
     'L0_ffn_s_gate_w': 7.191,
     'L0_ffn_s_up_w': 6.999,
     'L0_ffn_s_down_w': 7.139,
     'L1_xattn_W_att0': 3.007,
     'L1_xattn_W_att1': 2.81,
     'L1_ffn_router_w': 4.065,
     'L1_ffn_w1': 8.0,
     'L1_ffn_w2': 7.452,
     'L2_xattn_bq': 33.392,
     'L2_xattn_bkv': 8.0,
     'L2_xattn_bo': 8.0,
     'L2_ffn_gate_w': 8.0,
     'L2_ffn_Wg': 8.0,
     'L2_ffn_Wu': 8.0,
     'L2_ffn_Wd': 8.0,
     'L2_ffn_Ws_g': 8.0,
     'L2_ffn_Ws_u': 8.0,
     'L2_ffn_Ws_d': 8.0,
     'L3_xattn_bo': 38.32,
     'L3_ffn_gate_w': 8.0,
     'L3_ffn_W1': 8.0,
     'L3_ffn_W2': 8.0,
     'L3_ffn_Ws1': 8.0,
     'L3_ffn_Ws2': 8.0}
    for name, (base, spread) in spreads.items():
        noise = np.random.default_rng([zlib.crc32(name.encode()), seed]).standard_normal(out[name].shape)
        drawn = base * np.exp(spread * noise) if base else spread * noise
        out[name] = jnp.asarray(drawn.astype(out[name].dtype))
    for name, factor in factors.items():
        out[name] = (out[name] * factor).astype(out[name].dtype)
    return out
```

```python
from contextlib import ExitStack

import concourse.bass as bass
from concourse import mybir

ALU = mybir.AluOpType
ACT = mybir.ActivationFunctionType
AX = mybir.AxisListType
F32 = mybir.dt.float32
BF16 = mybir.dt.bfloat16
U32 = mybir.dt.uint32

P = 128
B, S, D = 2, 512, 128
N = B * S
NT = N // P
TB = S // P
M, DC = 154, 96
MR = M - P
NK = B * M
H = 16
HP = 32
HG = P // HP
NG = H // HG
WIN = 128
EPS = 1e-5
E8 = 8
CAP = 192
NSLOT = E8 * CAP
CT = CAP // 2
E16, CAP2 = 16, 64
MAGIC = 12582912.0
NRING = 6


PACK = {
    "const": [("ident", 128), ("ones", 128), ("head_rows", 16), ("rem_rows", 4), ("earlier", 64),
              ("slot_no", 1), ("neg_half", 8), ("expert_base", 64), ("dummy_row", 8)],
    "ctx": [("ctxT", NK), ("ctx_rem", B * P)],
    "L0x": [("Wk", 128), ("Wv", 128), ("Wq", 128), ("W1", 256), ("W2", 256), ("bq", 1), ("bk", 1), ("b1", 2)],
    "L0f": [("Wr", 8), ("gate", 512), ("up", 512), ("sgate", 256), ("sup", 256), ("down", 512), ("sdown", 256)],
    "L1x": [("d2v", 128), ("img", 128), ("att0", 128), ("att1", 128), ("txt", 128), ("f1", 1024), ("f2", 512),
            ("b_d2v", 1), ("b_img", 1), ("b_att0", 1), ("b_att1", 1), ("b_txt", 1), ("b_f1", 4)],
    "L1f": [("Wr", 8), ("w1", 8 * 512), ("w2", 8 * 512), ("b1", 32)],
    "L2x": [("Wk", 128), ("Wv", 128), ("Wq", 128), ("Wo", 128), ("bq", 1), ("bk", 1)],
    "L2f": [("Wr", 16), ("sg", 256), ("su", 256), ("sd", 256), ("g", 4096), ("u", 4096), ("d", 4096)],
    "L3x": [("Wk", 1024), ("Wv", 1024), ("Wq", 1024), ("Wo", 1024)],
    "L3f": [("Wr", 8), ("gate", 960), ("up", 960), ("down", 1280)],
    "sel": [("ident", 128), ("ones", 128), ("upto", 128), ("minus_max", 16 * 128), ("L0f", 4 * 128), ("L3f", 8 * 96),
            ("slot", 16 * 128), ("score", 16 * 128), ("slot_iota", 1024)],
    "rows": [("g", 8), ("rb", 1), ("L0_bv", 128), ("L0_b2", 128), ("L1_bf2", 128), ("L1_b2", 1024),
             ("L2_bv", 128), ("L2_bo", 128), ("L3_bo", 128)],
}
WIDTH = {group: sum(n for _, n in items) for group, items in PACK.items()}


def columns(group, name):
    at = 0
    for part, n in PACK[group]:
        if part == name:
            return at, at + n
        at += n
    raise KeyError(name)


EARLY = ["L0x", "L0f", "L1x", "L1f", "L2x", "L2f"]
PLACE, ARENA = {}, 0
for _g in EARLY:
    PLACE[_g] = ARENA
    ARENA += WIDTH[_g]
PLACE["L3x"] = PLACE["L1f"]
PLACE["L3f"] = PLACE["L1f"] + WIDTH["L3x"]
assert WIDTH["L3x"] + WIDTH["L3f"] <= WIDTH["L1f"]
ARENA_SIZE = 11500


class Banks:

    def __init__(self, labels):
        self.at = {label: (i % NRING, i // NRING) for i, label in enumerate(labels)}
        assert len(self.at) == len(labels)


def attention_prep_jobs(L, nchunk):
    jobs = [(L, "k", c) for c in range(nchunk)]
    for b in range(B):
        for half in range(nchunk if nchunk == 1 else 2):
            jobs += [(L, "v", b, half), (L, "vr", b, half)]
    return jobs


def attention_jobs(L, nchunk):
    jobs = [(L, "q", c, b) for c in range(nchunk) for b in range(B)]
    jobs += [(L, "s", t, p) for t in range(TB) for p in range(H // 2)]
    jobs += [(L, "nmT", 0)]
    late = [(L, "s", t, p) for t in range(TB, NT) for p in range(H // 2)] + [(L, "nmT", 1)]
    steps = [(b, g) for b in range(B) for g in range(NG)]

    def scores_T(b, g):
        return [(L, "st", b, g, j) for j in range(HG)] + [(L, "sr", b, g)]

    def values(b, g):
        return [(L, "pv", b, g, i) for i in range(TB if nchunk > 1 else 1)]

    jobs += late
    jobs += scores_T(*steps[0])
    for n, (b, g) in enumerate(steps):
        if n + 1 < len(steps):
            jobs += scores_T(*steps[n + 1])
        if n and nchunk > 1:
            jobs += [(L, "oT", *steps[n - 1], c) for c in range(2)]
        jobs += values(b, g)
    last = steps[-1:] if nchunk > 1 else [(b, 0) for b in range(B)]
    return jobs + [(L, "oT", b, g, c) for b, g in last for c in range(2 if nchunk > 1 else 1)]


def norm_jobs(k):
    return [("xnT", k, b) for b in range(B)]


def moe_jobs(L, chunks, routed):
    jobs = [(L, "logits")]
    shared = [(c, b) for c in range(routed, chunks) for b in range(B)]
    first = [(c, b) for c in range(routed) for b in range(B)]
    for c, b in shared:
        jobs += [(L, "g", c, b), (L, "u", c, b)]
    jobs += [(L, "wT", b) for b in range(B)]
    for c, b in first:
        jobs += [(L, "g", c, b), (L, "u", c, b), (L, "w", c, b)]
    return jobs


AMAX = ["ctx", "vis", "img", "x", "cat", "h"]


def amax_jobs(name):
    return [("L1x", "amT", name), ("L1x", "amB", name)]


def l1x_prep_jobs():
    jobs = [("L1x", "wsum")] + amax_jobs("ctx") + [("L1x", "vis")] + amax_jobs("vis") + [("L1x", "img")]
    jobs += amax_jobs("img") + [("L1x", "kv", a) for a in range(2)]
    jobs += [("L1x", "kvT", a, b) for a in range(2) for b in range(B)]
    return jobs


def l1x_jobs():
    jobs = amax_jobs("x") + [("L1x", "txt", b) for b in range(B)]
    for a in range(2):
        jobs += [("L1x", "s", a, t) for t in range(0, NT, 2)]
        for b in range(B):
            jobs += [("L1x", "pT", a, b, 0), ("L1x", "pT", a, b, 1), ("L1x", "o", a, b)]
    jobs += amax_jobs("cat") + [("L1x", "f1", c, b) for c in range(4) for b in range(B)]
    return jobs + amax_jobs("h")


def l1f_jobs():
    jobs = [("L1f", "logits"), ("L1f", "count")] + [("L1f", "xgT", j) for j in range(3)]
    for kind, e in l1f_jobs_order():
        jobs += [("L1f", "h", e, c) for c in range(2)] if kind == "h" else [("L1f", "eo", e)]
    return jobs


def l2f_jobs():
    jobs = [("L2f", "logits"), ("L2f", "pT")]
    jobs += [("L2f", x, c, b) for c in range(2) for b in range(B) for x in ("sg", "su")]
    jobs += [("L2f", "slots")] + [("L2f", "stT")]
    jobs += [("L2f", "xg", b, half) for b in range(B) for half in range(2)]
    for k in range(E16 // 2):
        jobs += [("L2f", "gu", 2 * k), ("L2f", "gu", 2 * k + 1)]
        jobs += [("L2f", "bs", k, b, x) for b in range(B) for x in (0, 1)]
        jobs += [("L2f", "eo", k - 1)] if k else []
    return jobs + [("L2f", "eo", E16 // 2 - 1)]


ALL = ["L0x", "L0f", "L1x", "L1f", "L2x", "L2f", "L3x", "L3f"]
SUBLAYERS = 8


def all_jobs():
    jobs = attention_prep_jobs("L0x", 1) + norm_jobs(0) + attention_jobs("L0x", 1) + [("L0x", "h", c, b) for c in range(2) for b in range(B)]
    jobs += norm_jobs(1) + moe_jobs("L0f", 6, 4)
    jobs += l1x_prep_jobs() + norm_jobs(2) + l1x_jobs()
    jobs += norm_jobs(3) + l1f_jobs()
    jobs += attention_prep_jobs("L2x", 1) + norm_jobs(4) + attention_jobs("L2x", 1)
    jobs += norm_jobs(5) + l2f_jobs()
    jobs += attention_prep_jobs("L3x", 8) + norm_jobs(6) + attention_jobs("L3x", 8)
    jobs += norm_jobs(7) + moe_jobs("L3f", 10, 8)
    return jobs


class Core:

    def __init__(self, nc, ctx, dram, out):
        self.nc, self.dram, self.out = nc, dram, out
        self.banks = Banks(all_jobs())

        def sb(name, shape, dt=F32):
            return ctx.enter_context(nc.sbuf_tensor(name, shape, dt))

        def sem(name):
            return ctx.enter_context(nc.semaphore(name))

        self.bank_filled = [sem(f"bank_filled{i}") for i in range(NRING)]
        self.bank_drained = [sem(f"bank_drained{i}") for i in range(NRING)]
        self.loaded = {g: sem(f"loaded_{g}") for g in PACK}
        self.x_ready = sem("x_ready")
        self.projected = sem("projected")
        self.x_loaded = sem("x_loaded")
        self.out_stored = sem("out_stored")
        self.vector_step = sem("vector_step")
        self.scalar_step = sem("scalar_step")
        self.pool_step = sem("pool_step")
        self.var_ready = sem("var_ready")
        self.rstd_ready = sem("rstd_ready")
        self.normed = sem("normed")
        self.acc_filled = sem("acc_filled")
        self.residual_done = sem("residual_done")
        self.bias_ready = sem("bias_ready")
        self.gates_ready = sem("gates_ready")
        self.zeroed = sem("zeroed")
        self.kbd_ready = sem("kbd_ready")
        self.v_ready = sem("v_ready")
        self.nm_ready = sem("nm_ready")
        self.o_ready = sem("o_ready")
        self.l_ready = sem("l_ready")
        self.exp_ready = sem("exp_ready")
        self.w_ready = sem("w_ready")
        self.h_ready = sem("h_ready")
        self.am_ready = sem("am_ready")
        self.q_ready = sem("q_ready")
        self.l1_bias = sem("l1_bias")
        self.p_exp = sem("p_exp")
        self.p_norm = sem("p_norm")
        self.f_ready = sem("f_ready")
        self.slots_ready = sem("slots_ready")
        self.scattered = sem("scattered")
        self.slots_loaded = sem("slots_loaded")
        self.eo_stored = sem("eo_stored")
        self.y_loaded = sem("y_loaded")
        self.dram_zeroed = sem("dram_zeroed")
        self.parts_ready = sem("parts_ready")
        self.gather_sel = sem("gather_sel")
        self.scatter_sel = sem("scatter_sel")
        self.act_copied = sem("act_copied")

        self.ps = [ctx.enter_context(nc.psum_tensor(f"ring{i}", [P, 512], F32)) for i in range(NRING)]
        self.acc = [ctx.enter_context(nc.psum_tensor(f"acc{i}", [P, 512], F32)) for i in range(2)]

        self.packed = {g: sb(f"w_{g}", [P, WIDTH[g]], BF16 if g == "sel" else F32)
                       for g in ("const", "ctx", "sel", "rows")}
        self.mem = sb("mem", [P, ARENA + ARENA_SIZE])
        for g, at in PLACE.items():
            self.packed[g] = self.mem[:, at:at + WIDTH[g]]
        self.x = sb("x", [P, NT, D])
        self.xb = sb("xb", [P, NT, D])
        self.xn = sb("xn", [P, NT, D])
        self.xnT = sb("xnT", [P, N])
        self.stats = sb("stats", [P, NT, 6])
        self.mv = sb("mv", [P, NT, 2])
        self.rstd = sb("rstd", [P, NT])
        self.gates = sb("gates", [P, 8])
        self.small = sb("small", [P, 1024])
        self.nm = sb("nm", [P, NT, H])
        self.mpad = sb("mpad", [P, NT, P], BF16)
        self.nmT = sb("nmT", [P, N], BF16)
        self.bqs = sb("bqs", [P, 1])
        self.flag = sb("flag", [P, 4])
        self.den = sb("den", [P, 16])
        self.onehot = sb("onehot", [P, 64], BF16)
        self.gp = sb("gp", [P, NT])
        self.idx = sb("idx", [P, NT], U32)
        self.top8 = sb("top8", [P, 8])
        self.slots = nc.dram_tensor("slots", (ROWS1, D), F32).ap()
        self.eo_rows = nc.dram_tensor("eo_rows", (ROWS1, D), F32).ap()
        self.rt = sb("rt", [P, 5, 128])
        self.cmp = self.xb[:, :, :].rearrange("p t d -> p (t d)").rearrange("p (a b) -> p a b", a=2)
        self.m8 = sb("m8", [P, NT])
        self.s8 = sb("s8", [P, NT])
        self.r8 = sb("r8", [P, NT])
        self.am = sb("am", [P, 8])
        self.m1 = sb("m1", [P, 1])
        self.sc = sb("sc", [P, 12])
        self.ws = sb("ws", [P, 8])
        self.wabs = sb("wabs", [P, 8])
        self.thr = sb("thr", [P, 16])
        self.comb = sb("comb", [P, 8])
        self.avg = sb("avg", [P, 2])
        self.avgq = sb("avgq", [P, 2], BF16)
        self.hm = sb("hm", [P, 4])
        self.l1s = sb("l1s", [P, 3, NT])

    def cols(self, at, shape, dt=F32):
        n = 1
        for d in shape:
            n *= d
        words = n if dt != BF16 else n // 2
        v = self.mem[:, at:at + words]
        if dt != F32:
            v = v.bitcast(dt)
        if len(shape) == 2:
            v = v.rearrange("p (a b) -> p a b", a=shape[0])
        if len(shape) == 3:
            v = v.rearrange("p (a b c) -> p a b c", a=shape[0], b=shape[1])
        if len(shape) == 4:
            v = v.rearrange("p (a b c d) -> p a b c d", a=shape[0], b=shape[1], c=shape[2])
        return v

    def w(self, group, name):
        a, b = columns(group, name)
        return self.packed[group][:, a:b]

    def bank(self, label):
        return self.ps[self.banks.at[label][0]]

    def filled(self, eng, label):
        b, use = self.banks.at[label]
        eng.wait_ge(self.bank_filled[b], use + 1)
        return self.ps[b]

    def drained(self, eng, label):
        b, use = self.banks.at[label]
        eng.wait_ge(self.bank_drained[b], use + 1)

    def open(self, pe, label):
        b, use = self.banks.at[label]
        if use:
            pe.wait_ge(self.bank_drained[b], use)
        return self.ps[b]

    def fill(self, label, ins):
        ins.then_inc(self.bank_filled[self.banks.at[label][0]], 1)

    def drain(self, label, ins):
        b, use = self.banks.at[label]
        ins.then_inc(self.bank_drained[b], 1)
        return self.bank_drained[b], use + 1


class Chain:

    def __init__(self, core, eng, own):
        self.core, self.eng, self.own, self.n, self.counts = core, eng, own, 0, {}
        self.last = None

    def did(self, ins, sem=None):
        sem = self.own if sem is None else sem
        ins.then_inc(sem, 1)
        key = str(sem)
        self.counts[key] = self.counts.get(key, 0) + 1
        self.last = (sem, self.counts[key])

    def drain(self, label, ins):
        self.last = self.core.drain(label, ins)

    def settle(self):
        self.eng.wait_ge(*self.last)


def bc(ap, axis, shape):
    return ap.unsqueeze(axis).to_broadcast([P, *shape])


def norm_vector(k, v, n, bias=None):
    nc = k.nc
    for t in range(NT):
        v.did(nc.vector.bn_stats(k.stats[:, t, :], k.x[:, t, :]))
    v.settle()
    for t in range(NT - 1):
        v.did(nc.vector.bn_aggr(k.mv[:, t, :], k.stats[:, t, :]))
    v.did(nc.vector.bn_aggr(k.mv[:, NT - 1, :], k.stats[:, NT - 1, :]), k.var_ready)
    if bias is not None:
        if n == 0:
            v.eng.wait_ge(k.gates_ready, 1)
            v.eng.wait_ge(k.loaded["rows"], 16)
        v.did(nc.vector.scalar_tensor_tensor(
            out=k.xb[:, :, :], in0=bc(bias, 1, [NT, D]), scalar=k.gates[:, n:n + 1], in1=k.x[:, :, :],
            op0=ALU.mult, op1=ALU.add))
    v.eng.wait_ge(k.rstd_ready, n + 1)
    for t in range(NT):
        v.did(nc.vector.tensor_scalar(k.xn[:, t, :], k.x[:, t, :], k.mv[:, t, 0:1], k.rstd[:, t:t + 1],
                                      ALU.subtract, ALU.mult), k.normed)


def norm_pool(k, g, n):
    nc = k.nc
    g.eng.wait_ge(k.var_ready, n + 1)
    g.did(nc.gpsimd.tensor_scalar_add(k.rstd[:, :], k.mv[:, :, 1], EPS))
    g.settle()
    g.did(nc.gpsimd.tensor_tensor(k.rstd[:, :], k.rstd[:, :], k.w("const", "neg_half"), ALU.pow), k.rstd_ready)


def norm_tensor(k, pe, n):
    for b in range(B):
        ps = k.open(pe, ("xnT", n, b))
        for i in range(TB):
            t = b * TB + i
            pe.wait_ge(k.normed, n * NT + t + 1)
            last = k.nc.tensor.transpose(ps[:, i * P:(i + 1) * P], k.xn[:, t, :], k.w("const", "ident"))
        k.fill(("xnT", n, b), last)


def norm_scalar(k, a, n):
    for b in range(B):
        ps = k.filled(a.eng, ("xnT", n, b))
        a.drain(("xnT", n, b), k.nc.scalar.activation(k.xnT[:, b * S:(b + 1) * S], ps[:, :], ACT.Copy))


def wait_xnT(k, eng, n, b):
    k.drained(eng, ("xnT", n, b))


def residual_vector(k, v, n, base, gate=None):
    for c in range(2):
        v.eng.wait_ge(k.acc_filled, 2 * acc_use(n) + c + 1)
        cs = slice(c * TB, (c + 1) * TB)
        v.did(k.nc.vector.scalar_tensor_tensor(
            out=k.x[:, cs, :], in0=k.acc[c][:, :].rearrange("p (t d) -> p t d", t=TB),
            scalar=k.gates[:, n:n + 1] if gate is None else gate, in1=base[:, cs, :], op0=ALU.mult, op1=ALU.add), k.residual_done)
    v.settle()


ACC_USERS = [0, 1, 2, 4, 5, 6, 7]


def acc_use(n):
    return ACC_USERS.index(n)


def open_acc(k, pe, n):
    if acc_use(n):
        pe.wait_ge(k.residual_done, 2 * acc_use(n))


class Attention:

    def __init__(self, k, L, n):
        self.L, self.n = L, n
        self.dh = 64 if L == "L3x" else 8
        self.nchunk = H * self.dh // P
        self.hpc = H // self.nchunk
        self.dv = self.dh + 1
        self.scale = float(self.dh) ** -0.5
        self.use = {"L0x": 0, "L2x": 1, "L3x": 2}[L]
        self.rw = max(WIN, HG * self.dv)
        dead = PLACE["L2f"] if L != "L2x" else PLACE["L0x"]
        first = PLACE["L2f"] if L == "L0x" else PLACE["L0x"]
        self.kbd = k.cols(first, [B, H, 160])
        at = ARENA
        self.vm = k.cols(at, [B, H, WIN])
        at += B * H * WIN
        self.vr = k.cols(at, [B, NG, self.rw])
        at += B * NG * self.rw
        self.pt = k.cols(at, [2, HG + 1, S])
        at += 2 * (HG + 1) * S
        if self.nchunk == 1:
            self.qT = k.cols(at, [1, N])
            self.o = k.xn
            self.oT = k.xnT
            self.kT = k.small[:, 0:NK]
            self.h = k.cols(dead + 5120, [2, N]) if L == "L0x" else None
        else:
            self.qT = k.cols(PLACE["L2f"], [self.nchunk, N])
            self.o = k.cols(PLACE["L2f"] + 8192, [2, TB, HG * self.dh])
            self.oT = k.cols(PLACE["L2f"] + 8192 + 2048, [2, 2, S])
        self.nm = k.nm


def attention_prep_tensor(k, pe, A):
    nc, L = k.nc, A.L
    pe.wait_ge(k.loaded["ctx"], 16)
    pe.wait_ge(k.loaded[L], 16)
    ctxT = k.w("ctx", "ctxT")
    for c in range(A.nchunk):
        ps = k.open(pe, (L, "k", c))
        k.fill((L, "k", c), nc.tensor.matmul(ps[:, 0:NK], k.w(L, "Wk")[:, c * P:(c + 1) * P], ctxT,
                                             start=True, stop=True))
    inner = H * A.dh
    for b in range(B):
        for half in range(max(1, inner // 512)):
            cs = slice(half * 512, min(inner, (half + 1) * 512))
            n = min(inner, 512)
            for kind, keys in (("v", ctxT[:, b * M:b * M + P]), ("vr", k.w("ctx", "ctx_rem")[:, b * P:(b + 1) * P])):
                ps = k.open(pe, (L, kind, b, half))
                k.fill((L, kind, b, half), nc.tensor.matmul(ps[:, 0:n], keys, k.w(L, "Wv")[:, cs], start=True, stop=True))


def attention_prep_pool(k, g, A):
    nc = k.nc
    if A.L != "L0x":
        g.eng.wait_ge(k.x_ready, A.n)
    if A.nchunk > 1:
        g.did(nc.gpsimd.memset(A.kbd[:, :, :, :], 0.0))
    else:
        g.did(nc.gpsimd.memset(A.kbd[:, :, :, M:160], 0.0))
    g.did(nc.gpsimd.memset(A.vm[:, :, :, :], 0.0))
    g.did(nc.gpsimd.memset(A.vr[:, :, :], 0.0))
    if A.L == "L0x":
        g.did(nc.gpsimd.memset(k.mpad[:, :, :], 0.0))
    g.settle()
    g.did(nc.gpsimd.memset(A.vm[:, :, :, A.dh:A.dh + 1], 1.0), k.zeroed)


def attention_prep_vector(k, v, A):
    nc, L = k.nc, A.L
    v.eng.wait_ge(k.loaded["const"], 16)
    v.eng.wait_ge(k.loaded["rows"], 16)
    v.eng.wait_ge(k.zeroed, {0: 1, 1: 3, 2: 4}[A.use])
    head_rows = k.w("const", "head_rows")
    if A.nchunk == 1:
        v.did(nc.vector.tensor_scalar(k.bqs[:, 0:1], k.w(L, "bq"), A.scale, None, ALU.mult), k.bias_ready)
        ps = k.filled(v.eng, (L, "k", 0))
        v.drain((L, "k", 0), nc.vector.tensor_scalar(A.kT, ps[:, 0:NK], k.w(L, "bk"), None, ALU.add))
        v.settle()
        for b in range(B):
            v.did(nc.vector.tensor_tensor(
                A.kbd[:, b, :, 0:M], bc(A.kT[:, b * M:(b + 1) * M], 1, [H, M]), bc(head_rows, 2, [H, M]), ALU.mult),
                k.kbd_ready)
    else:
        for c in range(A.nchunk):
            ps = k.filled(v.eng, (L, "k", c))
            src = ps[:, 0:NK].rearrange("p (b m) -> p b m", b=B)
            v.did(nc.vector.tensor_copy(A.kbd[0:64, :, 2 * c, 0:M], src[0:64]))
            v.drain((L, "k", c), nc.vector.tensor_copy(A.kbd[64:128, :, 2 * c + 1, 0:M], src[64:128]))
    inner = H * A.dh
    halves = max(1, inner // 512)
    nh = H // halves
    rem = k.w("const", "rem_rows")
    for b in range(B):
        for half in range(halves):
            hs = slice(half * nh, (half + 1) * nh)
            ps = k.filled(v.eng, (L, "v", b, half))
            src = ps[:, 0:nh * A.dh].rearrange("p (h d) -> p h d", h=nh)
            dst = A.vm[:, b, hs, 0:A.dh]
            if A.nchunk == 1:
                bv = k.w("rows", L[:2] + "_bv").rearrange("p (h d) -> p h d", h=nh)
                v.drain((L, "v", b, half), nc.vector.tensor_tensor(dst, src, bv, ALU.add))
            else:
                v.drain((L, "v", b, half), nc.vector.tensor_copy(dst, src))
            ps = k.filled(v.eng, (L, "vr", b, half))
            if A.nchunk == 1:
                v.drain((L, "vr", b, half), nc.vector.tensor_tensor(
                    k.small[:, 512:640], ps[:, 0:128], k.w("rows", L[:2] + "_bv"), ALU.add))
                v.settle()
                for g in range(NG):
                    dst = A.vr[:, b, g, 0:HG * A.dv].rearrange("p (j d) -> p j d", j=HG)
                    src = k.small[:, 512 + g * 32:512 + (g + 1) * 32].rearrange("p (j d) -> p j d", j=HG)
                    v.did(nc.vector.tensor_tensor(dst[:, :, 0:A.dh], src, bc(rem, 2, [HG, A.dh]), ALU.mult))
                    v.did(nc.vector.tensor_copy(dst[:, :, A.dh:A.dh + 1], rem.unsqueeze(2)))
                v.settle()
            else:
                for g in range(2 * half, 2 * half + 2):
                    dst = A.vr[:, b, g, 0:HG * A.dv].rearrange("p (j d) -> p j d", j=HG)
                    at = (g - 2 * half) * HG * A.dh
                    src = ps[:, at:at + HG * A.dh].rearrange("p (j d) -> p j d", j=HG)
                    ins = nc.vector.tensor_tensor(dst[:, :, 0:A.dh], src, bc(rem, 2, [HG, A.dh]), ALU.mult)
                    v.did(ins) if g == 2 * half else v.drain((L, "vr", b, half), ins)
                    v.did(nc.vector.tensor_copy(dst[:, :, A.dh:A.dh + 1], rem.unsqueeze(2)))
    v.did(nc.vector.tensor_copy(k.flag[:, 0:1], rem[:, 0:1]), k.v_ready)


def attention_scalar_q(k, a, A):
    nc, L = k.nc, A.L
    if A.nchunk == 1:
        a.eng.wait_ge(k.bias_ready, {0: 1, 1: 3}[A.use])
    for c in range(A.nchunk):
        for b in range(B):
            ps = k.filled(a.eng, (L, "q", c, b))
            dst = A.qT[:, c, b * S:(b + 1) * S]
            if A.nchunk == 1:
                ins = nc.scalar.activation(dst, ps[:, :], ACT.Identity, bias=k.bqs[:, 0:1], scale=A.scale)
            else:
                ins = nc.scalar.activation(dst, ps[:, :], ACT.Copy, scale=A.scale)
            a.drain((L, "q", c, b), ins)


def attention_tensor(k, pe, A):
    nc, L = k.nc, A.L
    for c in range(A.nchunk):
        for b in range(B):
            wait_xnT(k, pe, A.n, b)
            ps = k.open(pe, (L, "q", c, b))
            k.fill((L, "q", c, b), nc.tensor.matmul(ps[:, :], k.w(L, "Wq")[:, c * P:(c + 1) * P],
                                                    k.xnT[:, b * S:(b + 1) * S], start=True, stop=True))
    if A.nchunk == 1:
        pe.wait_ge(k.kbd_ready, B * (A.use + 1))
    pe.wait_ge(k.v_ready, A.use + 1)

    def scores(t):
        b = t // TB
        for p in range(H // 2):
            c = 2 * p // A.hpc
            k.drained(pe, (L, "q", c, b))
            ps = k.open(pe, (L, "s", t, p))
            k.fill((L, "s", t, p), nc.tensor.matmul(
                ps[:, 0:2 * M], A.qT[:, c, t * P:(t + 1) * P],
                A.kbd[:, b, 2 * p:2 * p + 2, 0:M], start=True, stop=True))

    def minus_max(b):
        ps = k.open(pe, (L, "nmT", b))
        pe.wait_ge(k.nm_ready, 2 * A.use + b + 1)
        view = ps[:, :].bitcast(BF16)
        for i in range(TB):
            last = nc.tensor.transpose(view[:, i * P:(i + 1) * P], k.mpad[:, b * TB + i, :], k.w("sel", "ident"))
        k.fill((L, "nmT", b), last)

    def scores_T(b, g):
        k.drained(pe, (L, "nmT", b))
        queries = slice(b * S, (b + 1) * S)
        for j in range(HG):
            h = HG * g + j
            ps = k.open(pe, (L, "st", b, g, j))
            nc.tensor.matmul(ps[:, :], A.kbd[:, b, h, 0:P], A.qT[:, h // A.hpc, queries], start=True, stop=False)
            k.fill((L, "st", b, g, j), nc.tensor.matmul(
                ps[:, :], k.w("sel", "minus_max")[:, h * P:(h + 1) * P], k.nmT[:, queries], start=False, stop=True))
        ps = k.open(pe, (L, "sr", b, g))
        for j in range(HG):
            h = HG * g + j
            rows = slice(HP * j, HP * (j + 1))
            nc.tensor.matmul(ps[rows, :], A.kbd[:, b, h, P:160], A.qT[:, h // A.hpc, queries], start=True, stop=False)
            last = nc.tensor.matmul(ps[rows, :], k.w("sel", "minus_max")[:, h * P:h * P + HP], k.nmT[:, queries],
                                    start=False, stop=True)
        k.fill((L, "sr", b, g), last)

    def values(b, g):
        step = b * NG + g
        for j in range(HG):
            k.drained(pe, (L, "st", b, g, j))
        k.drained(pe, (L, "sr", b, g))
        pt = A.pt[:, step % 2]
        for i in range(TB):
            q = slice(i * P, (i + 1) * P)
            single = A.nchunk == 1
            if not single or i == 0:
                ps = k.open(pe, (L, "pv", b, g, i))
            at = i * HG * A.dv if single else 0
            for j in range(HG):
                a = at + j * A.dv
                nc.tensor.matmul(ps[:, a:a + WIN], pt[:, j, q], A.vm[:, b, HG * g + j, :],
                                 start=(j == 0 and (i == 0 or not single)), stop=False, skip_group_check=True)
            last = nc.tensor.matmul(ps[:, at:at + A.rw], pt[:, HG, q], A.vr[:, b, g, :], start=False,
                                    stop=(not single or i == TB - 1), skip_group_check=True)
            if not single:
                k.fill((L, "pv", b, g, i), last)
        if A.nchunk == 1:
            k.fill((L, "pv", b, g, 0), last)

    for t in range(TB):
        scores(t)
    minus_max(0)
    for t in range(TB, NT):
        scores(t)
    minus_max(1)
    def turn(n):
        b, g = steps[n]
        for c in range(2):
            ps = k.open(pe, (L, "oT", b, g, c))
            pe.wait_ge(k.o_ready, 2 + n + 1)
            for i in range(TB):
                last = nc.tensor.transpose(ps[:, i * P:(i + 1) * P], A.o[:, n % 2, i, c * P:(c + 1) * P], k.w("const", "ident"))
            k.fill((L, "oT", b, g, c), last)

    def project(n):
        b, g = steps[n]
        for c in range(2):
            k.drained(pe, (L, "oT", b, g, c))
        for i in range(TB):
            for c in range(2):
                chunk = 2 * g + c
                last = nc.tensor.matmul(
                    k.acc[b][:, i * D:(i + 1) * D], A.oT[:, n % 2, c, i * P:(i + 1) * P],
                    k.w(L, "Wo")[:, chunk * D:(chunk + 1) * D], start=(chunk == 0 and i == 0),
                    stop=(chunk == 7 and i == TB - 1), skip_group_check=True)
        last.then_inc(k.projected if g < NG - 1 else k.acc_filled, 1)

    steps = [(b, g) for b in range(B) for g in range(NG)]
    scores_T(*steps[0])
    if A.nchunk > 1:
        open_acc(k, pe, A.n)
    for n, (b, g) in enumerate(steps):
        if n + 1 < len(steps):
            scores_T(*steps[n + 1])
        if n and A.nchunk > 1:
            turn(n - 1)
        values(b, g)
        if n and A.nchunk > 1:
            project(n - 1)
    if A.nchunk > 1:
        turn(len(steps) - 1)
        project(len(steps) - 1)
        return
    for b in range(B):
        pe.wait_ge(k.o_ready, A.use + 1)
        ps = k.open(pe, (L, "oT", b, 0, 0))
        for i in range(TB):
            last = nc.tensor.transpose(ps[:, i * P:(i + 1) * P], A.o[:, b * TB + i, :], k.w("const", "ident"))
        k.fill((L, "oT", b, 0, 0), last)
    open_acc(k, pe, A.n)
    if L == "L0x":
        for c in range(2):
            for b in range(B):
                k.drained(pe, (L, "oT", b, 0, 0))
                ps = k.open(pe, (L, "h", c, b))
                k.fill((L, "h", c, b), nc.tensor.matmul(ps[:, :], k.w(L, "W1")[:, c * P:(c + 1) * P],
                                                        A.oT[:, b * S:(b + 1) * S], start=True, stop=True))
        for b in range(B):
            for c in range(2):
                k.drained(pe, (L, "h", c, b))
            for i in range(TB):
                t = b * TB + i
                for c in range(2):
                    last = nc.tensor.matmul(k.acc[b][:, i * D:(i + 1) * D], A.h[:, c, t * P:(t + 1) * P],
                                            k.w(L, "W2")[:, c * D:(c + 1) * D], start=(c == 0), stop=(c == 1))
            last.then_inc(k.acc_filled, 1)
    else:
        for b in range(B):
            k.drained(pe, (L, "oT", b, 0, 0))
            for i in range(TB):
                t = b * TB + i
                last = nc.tensor.matmul(k.acc[b][:, i * D:(i + 1) * D], A.oT[:, t * P:(t + 1) * P], k.w(L, "Wo"),
                                        start=True, stop=True)
            last.then_inc(k.acc_filled, 1)


def projected(k, n):
    b, g = divmod(n, NG)
    if g < NG - 1:
        return k.projected, b * (NG - 1) + g + 1
    return k.acc_filled, 2 * acc_use(6) + b + 1


def attention_scalar(k, a, A):
    nc, L = k.nc, A.L

    def turned(n):
        b, g = divmod(n, NG)
        if n >= 2:
            a.eng.wait_ge(*projected(k, n - 2))
        for c in range(2):
            ps = k.filled(a.eng, (L, "oT", b, g, c))
            a.drain((L, "oT", b, g, c), nc.scalar.activation(A.oT[:, n % 2, c, :], ps[:, :], ACT.Copy))

    for b in range(B):
        ps = k.filled(a.eng, (L, "nmT", b))
        a.drain((L, "nmT", b), nc.scalar.activation(k.nmT[:, b * S:(b + 1) * S], ps[:, :].bitcast(BF16)[:, 0:S], ACT.Copy))
    for b in range(B):
        for g in range(NG):
            step = b * NG + g
            if step >= 2:
                bb, gg = divmod(step - 2, NG)
                k.filled(a.eng, (L, "pv", bb, gg, 0 if A.nchunk == 1 else TB - 1))
            for j in range(HG + 1):
                label = (L, "st", b, g, j) if j < HG else (L, "sr", b, g)
                ps = k.filled(a.eng, label)
                a.drain(label, nc.scalar.activation(A.pt[:, step % 2, j, :], ps[:, :], ACT.Exp))
            if A.nchunk > 1 and step >= 2:
                turned(step - 2)
    if A.nchunk > 1:
        turned(B * NG - 2)
        turned(B * NG - 1)
    else:
        for b in range(B):
            ps = k.filled(a.eng, (L, "oT", b, 0, 0))
            a.drain((L, "oT", b, 0, 0), nc.scalar.activation(A.oT[:, b * S:(b + 1) * S], ps[:, :], ACT.Copy))
    if L == "L0x":
        for c in range(2):
            for b in range(B):
                ps = k.filled(a.eng, (L, "h", c, b))
                a.drain((L, "h", c, b), nc.scalar.activation(A.h[:, c, b * S:(b + 1) * S], ps[:, :], ACT.Relu,
                                                             bias=k.w(L, "b1")[:, c:c + 1]))


def attention_vector(k, v, A):
    nc, L = k.nc, A.L
    for b in range(B):
        for t in range(b * TB, (b + 1) * TB):
            for p in range(H // 2):
                ps = k.filled(v.eng, (L, "s", t, p))
                v.drain((L, "s", t, p), nc.vector.tensor_reduce(
                    k.nm[:, t, 2 * p:2 * p + 2], ps[:, 0:2 * M].rearrange("p (h m) -> p h m", h=2),
                    axis=AX.X, op=ALU.max, negate=True))
        v.settle()
        ts = slice(b * TB, (b + 1) * TB)
        v.did(nc.vector.tensor_copy(k.mpad[:, ts, 0:H], k.nm[:, ts, :]))
        v.settle()
        v.did(nc.vector.tensor_tensor(k.mpad[:, ts, H:2 * H], k.nm[:, ts, :], k.mpad[:, ts, 0:H], ALU.subtract), k.nm_ready)
    for b in range(B):
        for g in range(NG):
            if A.nchunk == 1:
                ps = k.filled(v.eng, (L, "pv", b, g, 0))
                src = ps[:, 0:TB * HG * A.dv].rearrange("p (i j d) -> p i j d", i=TB, j=HG)
                r = k.den[:, 0:TB * HG]
                v.settle()
                v.did(nc.vector.reciprocal(r.rearrange("p (i j) -> p i j", i=TB), src[:, :, :, A.dh]))
                v.settle()
                dst = A.o[:, b * TB:(b + 1) * TB, g * HG * A.dh:(g + 1) * HG * A.dh].rearrange("p i (j d) -> p i j d", j=HG)
                v.drain((L, "pv", b, g, 0), nc.vector.tensor_tensor(
                    dst, src[:, :, :, 0:A.dh],
                    r.rearrange("p (i j) -> p i j", i=TB).unsqueeze(3).to_broadcast([P, TB, HG, A.dh]), ALU.mult))
            else:
                step = b * NG + g
                for i in range(TB):
                    ps = k.filled(v.eng, (L, "pv", b, g, i))
                    src = ps[:, 0:HG * A.dv].rearrange("p (j d) -> p j d", j=HG)
                    r = k.den[:, HG * i:HG * (i + 1)]
                    if i == 0:
                        v.settle()
                    v.did(nc.vector.reciprocal(r, src[:, :, A.dh]))
                    v.settle()
                    if step >= 2 and i == 0:
                        k.filled(v.eng, (L, "oT", *divmod(step - 2, NG), 1))
                    v.drain((L, "pv", b, g, i), nc.vector.tensor_tensor(
                        A.o[:, step % 2, i, :].rearrange("p (j d) -> p j d", j=HG), src[:, :, 0:A.dh],
                        r.unsqueeze(2).to_broadcast([P, HG, A.dh]), ALU.mult))
                v.did(nc.vector.tensor_copy(k.flag[:, 1:2], k.flag[:, 0:1]), k.o_ready)
    if A.nchunk == 1:
        v.did(nc.vector.tensor_copy(k.flag[:, 1:2], k.flag[:, 0:1]), k.o_ready)


def done(k, v):
    v.settle()
    v.did(k.nc.vector.tensor_copy(k.flag[:, 2:3], k.flag[:, 0:1]), k.x_ready)


class Moe:

    def __init__(self, k, L, n, width, chunks, routed):
        self.L, self.n, self.width, self.chunks, self.routed = L, n, width, chunks, routed
        self.topk = 4 if L == "L0f" else 2
        self.use = 0 if L == "L0f" else 1
        self.h = k.cols(ARENA, [chunks, N])
        self.sg = k.small[:, 0:1024].rearrange("p (a b) -> p a b", a=2)

    def part(self, k, kind, c):
        w = D if kind == "down" else self.width
        if self.L == "L0f" and c >= self.routed:
            kind, c = {"gate": "sgate", "up": "sup", "down": "sdown"}[kind], c - self.routed
        return k.w(self.L, kind)[:, c * w:(c + 1) * w]


ROUTERS = ["L0f", "L1f", "L2f", "L3f"]


def logits_tensor(k, pe, L, n, experts=E8):
    ps = k.open(pe, (L, "logits"))
    pe.wait_ge(k.loaded[L], 16)
    for t in range(NT):
        wait_xnT(k, pe, n, t // TB)
        last = k.nc.tensor.matmul(ps[:, t * experts:(t + 1) * experts], k.xnT[:, t * P:(t + 1) * P], k.w(L, "Wr"),
                                  start=True, stop=True)
    k.fill((L, "logits"), last)


def softmax_scalar(k, a, L, experts=E8):
    a.eng.wait_ge(k.l_ready, ROUTERS.index(L) + 1)
    w = NT * experts
    a.did(k.nc.scalar.activation(k.rt[:, 0, 0:w], k.rt[:, 0, 0:w], ACT.Exp), k.exp_ready)


def softmax_vector(k, v, L, experts=E8):
    nc = k.nc
    w = NT * experts
    ps = k.filled(v.eng, (L, "logits"))
    three = lambda ap: ap.rearrange("p (t e) -> p t e", t=NT)
    src = three(ps[:, 0:w])
    ex = three(k.rt[:, 0, 0:w])
    v.did(nc.vector.tensor_reduce(k.m8[:, :], src, axis=AX.X, op=ALU.max, negate=True))
    v.settle()
    v.drain((L, "logits"), nc.vector.tensor_tensor(ex, src, bc(k.m8[:, :], 2, [NT, experts]), ALU.add))
    v.settle()
    v.did(nc.vector.tensor_copy(k.flag[:, 3:4], k.flag[:, 0:1]), k.l_ready)
    v.eng.wait_ge(k.exp_ready, ROUTERS.index(L) + 1)
    v.did(nc.vector.tensor_reduce(k.s8[:, :], ex, axis=AX.X, op=ALU.add))
    v.settle()
    v.did(nc.vector.reciprocal(k.r8[:, :], k.s8[:, :]))
    v.settle()
    v.did(nc.vector.tensor_tensor(three(k.rt[:, 1, 0:w]), ex, bc(k.r8[:, :], 2, [NT, experts]), ALU.mult))
    v.settle()


def rank_vector(k, v, scores):
    nc = k.nc
    s = scores.rearrange("p (t e) -> p t e", t=NT)
    four = lambda ap: ap.rearrange("p (t e f) -> p t e f", t=NT, e=E8)
    other = s.unsqueeze(2).to_broadcast([P, NT, E8, E8])
    own = s.unsqueeze(3).to_broadcast([P, NT, E8, E8])
    gt, eq = four(k.cmp[:, 0, :]), four(k.cmp[:, 1, :])
    v.did(nc.vector.tensor_tensor(gt, other, own, ALU.is_gt))
    v.did(nc.vector.tensor_tensor(eq, other, own, ALU.is_equal))
    v.settle()
    earlier = k.w("const", "earlier").unsqueeze(1).to_broadcast([P, NT, 64])
    flat = lambda ap: ap.rearrange("p (t e) -> p t e", t=NT)
    v.did(nc.vector.tensor_tensor(flat(k.cmp[:, 1, :]), flat(k.cmp[:, 1, :]), earlier, ALU.mult))
    v.settle()
    v.did(nc.vector.tensor_tensor(k.cmp[:, 0, :], k.cmp[:, 0, :], k.cmp[:, 1, :], ALU.add))
    v.settle()
    v.did(nc.vector.tensor_reduce(k.rt[:, 3, 0:64], k.cmp[:, 0, :].rearrange("p (c f) -> p c f", f=E8), axis=AX.X, op=ALU.add))
    v.settle()


def three_parts(k, v, src, dst, tmp, last_sem):
    nc = k.nc
    v.did(nc.vector.tensor_copy(dst[0], src))
    v.settle()
    v.did(nc.vector.tensor_tensor(tmp[0], src, dst[0], ALU.subtract))
    v.settle()
    v.did(nc.vector.tensor_copy(dst[1], tmp[0]))
    v.settle()
    v.did(nc.vector.tensor_tensor(dst[2], tmp[0], dst[1], ALU.subtract), last_sem)


def moe_vector(k, v, A):
    nc, L = k.nc, A.L
    softmax_vector(k, v, L)
    probs, w = k.rt[:, 1, 0:64], k.rt[:, 2, 0:64]
    scores = probs
    if L == "L0f":
        scores = k.rt[:, 4, 0:64]
        v.did(nc.vector.tensor_scalar(scores, probs, k.w("rows", "rb"), None, ALU.add))
        v.settle()
    rank_vector(k, v, scores)
    v.did(nc.vector.scalar_tensor_tensor(out=w, in0=k.rt[:, 3, 0:64], scalar=float(A.topk), in1=probs,
                                         op0=ALU.is_lt, op1=ALU.mult))
    v.settle()
    three = lambda ap: ap.rearrange("p (t e) -> p t e", t=NT)
    if L == "L0f":
        v.did(nc.vector.tensor_reduce(k.s8[:, :], three(w), axis=AX.X, op=ALU.add))
        v.settle()
        v.did(nc.vector.tensor_scalar(k.s8[:, :], k.s8[:, :], 1e-20, None, ALU.add))
        v.settle()
        v.did(nc.vector.reciprocal(k.r8[:, :], k.s8[:, :]))
        v.settle()
        v.did(nc.vector.tensor_tensor(three(w), three(w), bc(k.r8[:, :], 2, [NT, E8]), ALU.mult))
        v.settle()
    parts = [k.mpad[:, :, 8 * i:8 * (i + 1)] for i in range(3)]
    three_parts(k, v, three(w), parts, [three(k.rt[:, 3, 0:64])], k.w_ready)

    def hidden(c, b):
        r = slice(0, A.width)
        cs = slice(b * S, (b + 1) * S)
        turn = order.index((c, b))
        k.drained(v.eng, (L, "g", c, b))
        ps = k.filled(v.eng, (L, "u", c, b))
        v.drain((L, "u", c, b), nc.vector.tensor_tensor(A.h[r, c, cs], A.sg[r, turn % 2, :], ps[r, :], ALU.mult))
        if c < A.routed:
            v.settle()
            ps = k.filled(v.eng, (L, "w", c, b))
            v.drain((L, "w", c, b), nc.vector.tensor_tensor(A.h[r, c, cs], A.h[r, c, cs], ps[r, :], ALU.mult))

    order = moe_order(A)
    for c, b in order:
        hidden(c, b)


def moe_order(A):
    return [(c, b) for c in range(A.routed, A.chunks) for b in range(B)] + [(c, b) for c in range(A.routed) for b in range(B)]


def moe_scalar(k, a, A):
    nc, L = k.nc, A.L
    softmax_scalar(k, a, L)
    order = moe_order(A)
    shared = 2 * (A.chunks - A.routed)
    for turn, (c, b) in enumerate(order):
        if turn == shared:
            for bb in range(B):
                ps = k.filled(a.eng, (L, "wT", bb))
                a.drain((L, "wT", bb), nc.scalar.activation(k.nmT[:, bb * S:(bb + 1) * S], ps[:, :].bitcast(BF16)[:, 0:S], ACT.Copy))
        if turn >= 2:
            k.drained(a.eng, (L, "u", *order[turn - 2]))
        ps = k.filled(a.eng, (L, "g", c, b))
        a.drain((L, "g", c, b), nc.scalar.activation(A.sg[0:A.width, turn % 2, :], ps[0:A.width, :], ACT.Silu))


def moe_tensor(k, pe, A):
    nc, L = k.nc, A.L
    logits_tensor(k, pe, L, A.n)
    order = moe_order(A)
    shared = 2 * (A.chunks - A.routed)
    for turn, (c, b) in enumerate(order):
        if turn == shared:
            for bb in range(B):
                ps = k.open(pe, (L, "wT", bb))
                pe.wait_ge(k.w_ready, ROUTERS.index(L) + 1)
                for i in range(TB):
                    last = nc.tensor.transpose(ps[:, :].bitcast(BF16)[:, i * P:(i + 1) * P], k.mpad[:, bb * TB + i, :],
                                               k.w("sel", "ident"))
                k.fill((L, "wT", bb), last)
        cs = slice(b * S, (b + 1) * S)
        for kind, name in (("g", "gate"), ("u", "up")):
            ps = k.open(pe, (L, kind, c, b))
            k.fill((L, kind, c, b), nc.tensor.matmul(ps[0:A.width, :], A.part(k, name, c), k.xnT[:, cs], start=True, stop=True))
        if c < A.routed:
            ps = k.open(pe, (L, "w", c, b))
            k.drained(pe, (L, "wT", b))
            k.fill((L, "w", c, b), nc.tensor.matmul(ps[0:A.width, :], k.w("sel", L)[:, c * A.width:(c + 1) * A.width],
                                                    k.nmT[:, cs], start=True, stop=True))
    open_acc(k, pe, A.n)
    for b in range(B):
        for c in range(A.chunks):
            k.drained(pe, (L, "w" if c < A.routed else "u", c, b))
        for i in range(TB):
            t = b * TB + i
            for c in range(A.chunks):
                last = nc.tensor.matmul(k.acc[b][:, i * D:(i + 1) * D], A.h[0:A.width, c, t * P:(t + 1) * P],
                                        A.part(k, "down", c)[0:A.width], start=(c == 0), stop=(c == A.chunks - 1))
        last.then_inc(k.acc_filled, 1)


def moe_pool(k, g):
    pass


WEIGHTS1 = [("d2v", 1, 128 * 96), ("img", 1, 128 * 128), ("att0", 1, 128 * 128), ("att1", 1, 128 * 128),
            ("txt", 1, 128 * 128), ("f1", 8, 512 * 256), ("f2", 4, 128 * 512)]


class L1x:

    def __init__(self, k):
        self.wq = k.cols(PLACE["L0x"], [17 * P], BF16)
        self.hq = k.cols(PLACE["L0x"] + 1088, [4, N], BF16)
        at = ARENA
        self.tmp = k.cols(at, [2, N])
        at += 2 * N
        self.xq = k.cols(at, [N], BF16)
        at += N // 2
        self.fused = k.cols(at, [N])
        at += N
        self.kT = k.cols(at, [2, B, 256])
        at += 1024
        self.kv = k.cols(at, [2, B, 2, P])
        at += 1024
        self.p = k.cols(at, [NT, 256])
        self.pT = k.cols(at + 2048, [B, 2, S])
        self.h = k.cols(at, [4, N])
        self.f8 = k.l1s

    def weight(self, name):
        at = 0
        for n, blocks, _ in WEIGHTS1:
            if n == name:
                return self.wq[:, at:at + blocks * P]
            at += blocks * P


def amax_vector(k, v, name, src):
    nc, i = k.nc, AMAX.index(name)
    if src is not None:
        v.did(nc.vector.tensor_reduce(k.am[:, 0:1], src, axis=AX.X, op=ALU.max, apply_absolute_value=True))
    v.settle()
    v.did(nc.vector.tensor_copy(k.am[:, 4:5], k.am[:, 0:1]), k.am_ready)
    ps = k.filled(v.eng, ("L1x", "amT", name))
    v.drain(("L1x", "amT", name), nc.vector.tensor_reduce(k.m1[0:1, 0:1], ps[0:1, 0:P], axis=AX.X, op=ALU.max))
    ps = k.filled(v.eng, ("L1x", "amB", name))
    v.drain(("L1x", "amB", name), nc.vector.tensor_scalar(k.sc[:, 2 * i:2 * i + 1], ps[:, 0:1], 1e-8, 1.0 / 127.0, ALU.max, ALU.mult))
    v.settle()
    v.did(nc.vector.reciprocal(k.sc[:, 2 * i + 1:2 * i + 2], k.sc[:, 2 * i:2 * i + 1]))
    v.settle()


def amax_tensor(k, pe, name):
    nc = k.nc
    ps = k.open(pe, ("L1x", "amT", name))
    pe.wait_ge(k.am_ready, AMAX.index(name) + 1)
    k.fill(("L1x", "amT", name), nc.tensor.transpose(ps[0:1, 0:P], k.am[:, 4:5], k.w("const", "ident")))
    ps = k.open(pe, ("L1x", "amB", name))
    k.drained(pe, ("L1x", "amT", name))
    k.fill(("L1x", "amB", name), nc.tensor.matmul(ps[:, 0:1], k.w("const", "ones")[0:1, :], k.m1[0:1, 0:1], start=True, stop=True))


def quantise_vector(k, v, name, src, dst, tmp, sem=None):
    nc, i = k.nc, AMAX.index(name)
    v.did(nc.vector.tensor_scalar(tmp, src, k.sc[:, 2 * i + 1:2 * i + 2], MAGIC, ALU.mult, ALU.add))
    v.settle()
    v.did(nc.vector.tensor_scalar(dst, tmp, MAGIC, 127.0, ALU.subtract, ALU.min), sem)


def scale_vector(k, v, weight, name):
    w = [n for n, _, _ in WEIGHTS1].index(weight)
    i = AMAX.index(name)
    v.did(k.nc.vector.tensor_tensor(k.comb[:, w:w + 1], k.ws[:, w:w + 1], k.sc[:, 2 * i:2 * i + 1], ALU.mult))
    v.settle()
    return k.comb[:, w:w + 1]


def l1x_pool(k, g):
    nc, T = k.nc, L1x(k)
    g.eng.wait_ge(k.x_ready, 2)
    g.did(nc.gpsimd.memset(T.kT[:, :, :, M:256], 0.0))
    g.did(nc.gpsimd.memset(T.p[:, :, M:256], 0.0), k.zeroed)


def l1x_prep_vector(k, v):
    nc, T = k.nc, L1x(k)
    v.eng.wait_ge(k.loaded["L1x"], 16)
    at = 0
    for i, (name, blocks, _) in enumerate(WEIGHTS1):
        last = nc.vector.tensor_reduce(k.wabs[:, i:i + 1], k.w("L1x", name), axis=AX.X, op=ALU.add, apply_absolute_value=True)
        v.did(last, k.q_ready if i == 6 else None)
    ps = k.filled(v.eng, ("L1x", "wsum"))
    for a, b, count in ((0, 1, 128 * 96), (1, 5, 128 * 128), (5, 6, 512 * 256), (6, 7, 128 * 512)):
        ins = nc.vector.tensor_scalar(k.ws[:, a:b], ps[:, a:b], 1.0 / count, 1e-5, ALU.mult, ALU.max)
        v.did(ins) if b < 7 else v.drain(("L1x", "wsum"), ins)
    v.settle()
    v.did(nc.vector.tensor_scalar(k.thr[:, 0:7], k.ws[:, 0:7], 0.5, None, ALU.mult))
    v.did(nc.vector.tensor_scalar(k.thr[:, 8:15], k.ws[:, 0:7], -0.5, None, ALU.mult))
    v.settle()
    for i, (name, blocks, _) in enumerate(WEIGHTS1):
        below = T.tmp[:, i % 2, 0:blocks * P // 2].bitcast(BF16)
        if i >= 2:
            v.settle()
        v.did(nc.vector.tensor_scalar(below, k.w("L1x", name), k.thr[:, 8 + i:9 + i], None, ALU.is_lt))
        v.settle()
        v.did(nc.vector.scalar_tensor_tensor(out=T.weight(name), in0=k.w("L1x", name), scalar=k.thr[:, i:i + 1],
                                             in1=below, op0=ALU.is_gt, op1=ALU.subtract))
    small = T.tmp[:, 0, 0:NK]
    amax_vector(k, v, "ctx", k.w("ctx", "ctxT"))
    quantise_vector(k, v, "ctx", k.w("ctx", "ctxT"), T.xq[:, 0:NK], small, k.q_ready)
    act = T.tmp[:, 1, 0:NK]
    for label, name in (("vis", "d2v"), ("img", "img")):
        s = scale_vector(k, v, name, "ctx" if label == "vis" else "vis")
        ps = k.filled(v.eng, ("L1x", label))
        v.drain(("L1x", label), nc.vector.tensor_scalar(act, ps[:, 0:NK], s, k.w("L1x", "b_" + name), ALU.mult, ALU.add))
        v.settle()
        amax_vector(k, v, label, act)
        if label == "img":
            v.did(nc.vector.tensor_reduce(k.avg[:, 0:2], act.rearrange("p (b m) -> p b m", b=B), axis=AX.X, op=ALU.add))
            v.settle()
            v.did(nc.vector.tensor_scalar(k.avg[:, 0:2], k.avg[:, 0:2], 1.0 / M, None, ALU.mult))
        quantise_vector(k, v, label, act, T.xq[:, 0:NK], small, k.q_ready)
    v.eng.wait_ge(k.zeroed, 2)
    for r in range(2):
        s = scale_vector(k, v, f"att{r}", "img")
        ps = k.filled(v.eng, ("L1x", "kv", r))
        v.drain(("L1x", "kv", r), nc.vector.tensor_scalar(
            T.kT[:, r, :, 0:M], ps[:, 0:NK].rearrange("p (b m) -> p b m", b=B), s, k.w("L1x", f"b_att{r}"), ALU.mult, ALU.add))


def l1x_prep_tensor(k, pe):
    nc, T = k.nc, L1x(k)
    ps = k.open(pe, ("L1x", "wsum"))
    pe.wait_ge(k.q_ready, 1)
    k.fill(("L1x", "wsum"), nc.tensor.matmul(ps[:, 0:7], k.w("const", "ones"), k.wabs[:, 0:7], start=True, stop=True))
    for i, (label, name, weight) in enumerate((("vis", "ctx", "d2v"), ("img", "vis", "img"))):
        amax_tensor(k, pe, name)
        ps = k.open(pe, ("L1x", label))
        pe.wait_ge(k.q_ready, 2 + i)
        k.fill(("L1x", label), nc.tensor.matmul(ps[:, 0:NK], T.weight(weight), T.xq[:, 0:NK], start=True, stop=True))
    amax_tensor(k, pe, "img")
    for r in range(2):
        ps = k.open(pe, ("L1x", "kv", r))
        pe.wait_ge(k.q_ready, 4)
        k.fill(("L1x", "kv", r), nc.tensor.matmul(ps[:, 0:NK], T.weight(f"att{r}"), T.xq[:, 0:NK], start=True, stop=True))
    for r in range(2):
        for b in range(B):
            k.drained(pe, ("L1x", "kv", r))
            ps = k.open(pe, ("L1x", "kvT", r, b))
            for half in range(2):
                last = nc.tensor.transpose(ps[:, half * P:(half + 1) * P], T.kT[:, r, b, half * P:(half + 1) * P], k.w("const", "ident"))
            k.fill(("L1x", "kvT", r, b), last)


INV_SQRT = float(D) ** -0.5


def l1x_vector(k, v):
    nc, T = k.nc, L1x(k)
    for b in range(B):
        wait_xnT(k, v.eng, 2, b)
    amax_vector(k, v, "x", k.xnT[:, :])
    quantise_vector(k, v, "x", k.xnT[:, :], T.xq, T.tmp[:, 0, :], k.q_ready)
    s = scale_vector(k, v, "txt", "x")
    for b in range(B):
        ps = k.filled(v.eng, ("L1x", "txt", b))
        v.drain(("L1x", "txt", b), nc.vector.tensor_scalar(T.fused[:, b * S:(b + 1) * S], ps[:, :], s, k.w("L1x", "b_txt"), ALU.mult, ALU.add))
    for r in range(2):
        for t in range(0, NT, 2):
            ps = k.filled(v.eng, ("L1x", "s", r, t))
            v.did(nc.vector.tensor_reduce(k.am[:, 2:4], ps[:, 0:2 * M].rearrange("p (i m) -> p i m", i=2), axis=AX.X, op=ALU.max))
            v.settle()
            v.did(nc.vector.tensor_scalar(k.l1s[:, 0, t:t + 2], k.am[:, 2:4], -INV_SQRT, None, ALU.mult), k.l1_bias)
            v.settle()
        for t in range(0, NT, 2):
            k.drained(v.eng, ("L1x", "s", r, t))
            v.did(nc.vector.reciprocal(k.l1s[:, 2, t:t + 2], k.l1s[:, 1, t:t + 2]))
            v.settle()
            for i in range(t, t + 2):
                v.did(nc.vector.tensor_scalar(T.p[:, i, 0:M], T.p[:, i, 0:M], k.l1s[:, 2, i:i + 1], 0.1, ALU.mult, ALU.mult), k.p_norm)
        for b in range(B):
            ps = k.filled(v.eng, ("L1x", "o", r, b))
            cs = slice(b * S, (b + 1) * S)
            v.drain(("L1x", "o", r, b), nc.vector.tensor_tensor(T.fused[:, cs], T.fused[:, cs], ps[:, :], ALU.add))
        v.settle()
    v.did(nc.vector.tensor_reduce(k.am[:, 2:3], T.fused, axis=AX.X, op=ALU.max, apply_absolute_value=True))
    v.did(nc.vector.tensor_reduce(k.am[:, 3:4], k.avg[:, 0:2], axis=AX.X, op=ALU.max, apply_absolute_value=True))
    v.settle()
    v.did(nc.vector.tensor_reduce(k.am[:, 0:1], k.am[:, 2:4], axis=AX.X, op=ALU.max))
    amax_vector(k, v, "cat", None)
    quantise_vector(k, v, "cat", k.avg[:, 0:2], k.avgq[:, 0:2], k.am[:, 2:4])
    v.settle()
    quantise_vector(k, v, "cat", T.fused, T.xq, T.tmp[:, 0, :], k.q_ready)
    scale_vector(k, v, "f1", "cat")
    v.did(nc.vector.tensor_copy(k.flag[:, 3:4], k.flag[:, 0:1]), k.bias_ready)
    for c in range(4):
        for b in range(B):
            k.drained(v.eng, ("L1x", "f1", c, b))
        v.did(nc.vector.tensor_reduce(k.hm[:, c:c + 1], T.h[:, c, :], axis=AX.X, op=ALU.max))
    v.settle()
    amax_vector(k, v, "h", k.hm[:, 0:4])
    for c in range(4):
        if c >= 2:
            v.settle()
        quantise_vector(k, v, "h", T.h[:, c, :], T.hq[:, c, :], T.tmp[:, c % 2, :], k.q_ready)
    s = scale_vector(k, v, "f2", "h")
    v.did(nc.vector.tensor_tensor(k.comb[:, 7:8], s, k.gates[:, 2:3], ALU.mult))
    v.settle()
    residual_vector(k, v, 2, k.xb, k.comb[:, 7:8])


def l1x_scalar(k, a):
    nc, T = k.nc, L1x(k)
    for r in range(2):
        for t in range(0, NT, 2):
            ps = k.filled(a.eng, ("L1x", "s", r, t))
            a.eng.wait_ge(k.l1_bias, (r * NT + t) // 2 + 1)
            if r:
                k.filled(a.eng, ("L1x", "pT", 0, t // TB, 1))
            for i in range(2):
                ins = nc.scalar.activation(T.p[:, t + i, 0:M], ps[:, i * M:(i + 1) * M], ACT.Exp, bias=k.l1s[:, 0, t + i:t + i + 1],
                                           scale=INV_SQRT, accum_out=k.l1s[:, 1, t + i:t + i + 1])
                a.did(ins) if i == 0 else a.drain(("L1x", "s", r, t), ins)
        for b in range(B):
            if r:
                k.filled(a.eng, ("L1x", "o", 0, b))
            for half in range(2):
                label = ("L1x", "pT", r, b, half)
                ps = k.filled(a.eng, label)
                a.drain(label, nc.scalar.activation(T.pT[:, b, half, :], ps[:, :], ACT.Copy))
    a.eng.wait_ge(k.bias_ready, 2)
    for c in range(4):
        for b in range(B):
            ps = k.filled(a.eng, ("L1x", "f1", c, b))
            a.drain(("L1x", "f1", c, b), nc.scalar.activation(T.h[:, c, b * S:(b + 1) * S], ps[:, :], ACT.Relu,
                                                              bias=k.w("L1x", "b_f1")[:, c:c + 1], scale=k.comb[:, 5:6]))


def l1x_prep_scalar(k, a):
    T = L1x(k)
    for r in range(2):
        for b in range(B):
            ps = k.filled(a.eng, ("L1x", "kvT", r, b))
            a.drain(("L1x", "kvT", r, b), k.nc.scalar.activation(
                T.kv[:, r, b, :, :], ps[:, 0:256].rearrange("p (i d) -> p i d", i=2), ACT.Copy))


def l1x_tensor(k, pe):
    nc, T = k.nc, L1x(k)
    amax_tensor(k, pe, "x")
    pe.wait_ge(k.q_ready, 5)
    for b in range(B):
        ps = k.open(pe, ("L1x", "txt", b))
        k.fill(("L1x", "txt", b), nc.tensor.matmul(ps[:, :], T.weight("txt"), T.xq[:, b * S:(b + 1) * S], start=True, stop=True))
    for r in range(2):
        for t in range(0, NT, 2):
            b = t // TB
            k.drained(pe, ("L1x", "txt", b) if r == 0 else ("L1x", "o", 0, b))
            ps = k.open(pe, ("L1x", "s", r, t))
            for i in range(2):
                last = nc.tensor.matmul(ps[:, i * M:(i + 1) * M], T.fused[:, (t + i) * P:(t + i + 1) * P], T.kT[:, r, b, 0:M], start=True, stop=True)
            k.fill(("L1x", "s", r, t), last)
        for b in range(B):
            for half in range(2):
                ps = k.open(pe, ("L1x", "pT", r, b, half))
                for i in range(TB):
                    t = b * TB + i
                    pe.wait_ge(k.p_norm, r * NT + t + 1)
                    last = nc.tensor.transpose(ps[:, i * P:(i + 1) * P], T.p[:, t, half * P:(half + 1) * P], k.w("const", "ident"))
                k.fill(("L1x", "pT", r, b, half), last)
            ps = k.open(pe, ("L1x", "o", r, b))
            k.drained(pe, ("L1x", "kvT", r, b))
            for half in range(2):
                k.drained(pe, ("L1x", "pT", r, b, half))
                last = nc.tensor.matmul(ps[:, :], T.kv[:, r, b, half, :], T.pT[:, b, half, :], start=(half == 0), stop=(half == 1))
            k.fill(("L1x", "o", r, b), last)
    amax_tensor(k, pe, "cat")
    pe.wait_ge(k.q_ready, 6)
    for c in range(4):
        for b in range(B):
            ps = k.open(pe, ("L1x", "f1", c, b))
            w = T.weight("f1")
            nc.tensor.matmul(ps[:, :], w[:, c * P:(c + 1) * P], T.xq[:, b * S:(b + 1) * S], start=True, stop=False)
            k.fill(("L1x", "f1", c, b), nc.tensor.matmul(ps[:, :], w[:, 512 + c * P:512 + (c + 1) * P],
                                                         k.avgq[:, b:b + 1].to_broadcast([P, S]), start=False, stop=True))
    amax_tensor(k, pe, "h")
    pe.wait_ge(k.q_ready, 10)
    open_acc(k, pe, 2)
    for b in range(B):
        for i in range(TB):
            t = b * TB + i
            for c in range(4):
                last = nc.tensor.matmul(k.acc[b][:, i * D:(i + 1) * D], T.hq[:, c, t * P:(t + 1) * P],
                                        T.weight("f2")[:, c * D:(c + 1) * D], start=(c == 0), stop=(c == 3))
        last.then_inc(k.acc_filled, 1)


ROWS1 = NSLOT + N


class L1f:

    def __init__(self, k):
        at = ARENA
        self.xg = k.cols(at, [12, D])
        at += 12 * D
        self.xgT = k.cols(at, [NSLOT])
        at += NSLOT
        self.h = k.cols(at, [2, 4, CAP])
        at += 2 * 4 * CAP
        self.eo = k.cols(at, [E8, 2, D])
        at += E8 * 2 * D
        self.y = k.cols(at, [NT, D])
        self.zeros = k.cols(PLACE["L2f"] + 12000, [1024])


def l1f_jobs_order():
    for e in range(E8):
        if e == 0:
            yield "h", 0
        if e + 1 < E8:
            yield "h", e + 1
        yield "eo", e


def l1f_vector(k, v):
    nc, T = k.nc, L1f(k)
    softmax_vector(k, v, "L1f")
    probs = k.rt[:, 1, 0:64]
    rank_vector(k, v, probs)
    one = k.rt[:, 2, 0:64]
    three = lambda ap: ap.rearrange("p (t e) -> p t e", t=NT)
    v.did(nc.vector.tensor_scalar(one, k.rt[:, 3, 0:64], 1.0, None, ALU.is_lt))
    v.settle()
    v.did(nc.vector.tensor_copy(k.onehot[:, :], one), k.w_ready)
    v.did(nc.vector.tensor_tensor(k.rt[:, 3, 0:64], one, probs, ALU.mult))
    v.did(nc.vector.tensor_tensor(k.rt[:, 4, 0:64], one, k.w("const", "expert_base"), ALU.mult))
    v.settle()
    v.did(nc.vector.tensor_reduce(k.m8[:, :], three(k.rt[:, 3, 0:64]), axis=AX.X, op=ALU.add))
    v.did(nc.vector.tensor_reduce(k.s8[:, :], three(k.rt[:, 4, 0:64]), axis=AX.X, op=ALU.add))
    v.settle()
    v.did(nc.vector.tensor_scalar(k.gp[:, :], k.m8[:, :], k.gates[:, 3:4], None, ALU.mult))
    ps = k.filled(v.eng, ("L1f", "count"))
    v.drain(("L1f", "count"), nc.vector.tensor_tensor(k.rt[:, 0, 0:64], ps[:, 0:64], one, ALU.mult))
    v.settle()
    v.did(nc.vector.tensor_reduce(k.r8[:, :], three(k.rt[:, 0, 0:64]), axis=AX.X, op=ALU.add))
    v.settle()
    dummy = k.w("const", "dummy_row")
    v.did(nc.vector.tensor_tensor(k.s8[:, :], k.s8[:, :], k.r8[:, :], ALU.add))
    v.settle()
    v.did(nc.vector.tensor_tensor(k.s8[:, :], k.s8[:, :], dummy, ALU.subtract))
    v.settle()
    v.did(nc.vector.scalar_tensor_tensor(out=k.s8[:, :], in0=k.r8[:, :], scalar=float(CAP), in1=k.s8[:, :], op0=ALU.is_le, op1=ALU.mult))
    v.settle()
    v.did(nc.vector.tensor_tensor(k.idx[:, :], k.s8[:, :], dummy, ALU.add), k.slots_ready)
    b2 = k.w("rows", "L1_b2")
    for e in range(E8):
        ps = k.filled(v.eng, ("L1f", "eo", e))
        v.drain(("L1f", "eo", e), nc.vector.tensor_tensor(
            T.eo[0:CT, e, :, :], ps[0:CT, 0:2 * D].rearrange("p (j d) -> p j d", j=2),
            b2[0:CT, e * D:(e + 1) * D].unsqueeze(1).to_broadcast([CT, 2, D]), ALU.add))
    v.eng.wait_ge(k.y_loaded, 16 * NT)
    for t in range(NT):
        v.did(nc.vector.scalar_tensor_tensor(out=k.x[:, t, :], in0=T.y[:, t, :], scalar=k.gp[:, t:t + 1], in1=k.x[:, t, :],
                                             op0=ALU.mult, op1=ALU.add))


def l1f_scalar(k, a):
    nc, T = k.nc, L1f(k)
    softmax_scalar(k, a, "L1f")
    for j in range(3):
        ps = k.filled(a.eng, ("L1f", "xgT", j))
        a.drain(("L1f", "xgT", j), nc.scalar.activation(T.xgT[:, j * 512:(j + 1) * 512], ps[:, :], ACT.Copy))
    b1 = k.w("L1f", "b1")
    for e in range(E8):
        if e >= 2:
            k.filled(a.eng, ("L1f", "eo", e - 2))
        for c in range(2):
            ps = k.filled(a.eng, ("L1f", "h", e, c))
            for i in range(2):
                f = 2 * c + i
                ins = nc.scalar.activation(T.h[:, e % 2, f, :], ps[:, i * CAP:(i + 1) * CAP], ACT.Gelu, bias=b1[:, 4 * e + f:4 * e + f + 1])
                a.did(ins) if i == 0 else a.drain(("L1f", "h", e, c), ins)


def l1f_tensor(k, pe):
    nc, T = k.nc, L1f(k)
    logits_tensor(k, pe, "L1f", 3)
    ps = k.open(pe, ("L1f", "count"))
    pe.wait_ge(k.w_ready, 2)
    nc.tensor.matmul(ps[:, 0:64], k.w("sel", "upto"), k.onehot[:, :], start=True, stop=False, skip_group_check=True)
    for t in range(NT - 1):
        rest = NT - 1 - t
        last = nc.tensor.matmul(ps[:, (t + 1) * E8:64].rearrange("p (t e) -> p t e", t=rest), k.w("sel", "ones"),
                                bc(k.onehot[:, t * E8:(t + 1) * E8], 1, [rest, E8]), start=False, stop=(t == NT - 2),
                                skip_group_check=True)
    k.fill(("L1f", "count"), last)
    pe.wait_ge(k.slots_loaded, 16)
    for j in range(3):
        ps = k.open(pe, ("L1f", "xgT", j))
        for i in range(4):
            last = nc.tensor.transpose(ps[:, i * P:(i + 1) * P], T.xg[:, 4 * j + i, :], k.w("const", "ident"))
        k.fill(("L1f", "xgT", j), last)
    for j in range(3):
        k.drained(pe, ("L1f", "xgT", j))
    w1, w2 = k.w("L1f", "w1"), k.w("L1f", "w2")
    for kind, e in l1f_jobs_order():
        if kind == "h":
            for c in range(2):
                ps = k.open(pe, ("L1f", "h", e, c))
                for i in range(2):
                    f = 2 * c + i
                    last = nc.tensor.matmul(ps[:, i * CAP:(i + 1) * CAP], w1[:, e * 512 + f * P:e * 512 + (f + 1) * P],
                                            T.xgT[:, e * CAP:(e + 1) * CAP], start=True, stop=True)
                k.fill(("L1f", "h", e, c), last)
        else:
            ps = k.open(pe, ("L1f", "eo", e))
            for c in range(2):
                k.drained(pe, ("L1f", "h", e, c))
            for j in range(2):
                for f in range(4):
                    last = nc.tensor.matmul(ps[0:CT, j * D:(j + 1) * D], T.h[:, e % 2, f, j * CT:(j + 1) * CT],
                                            w2[:, (4 * e + f) * D:(4 * e + f + 1) * D], start=(f == 0), stop=(f == 3))
            k.fill(("L1f", "eo", e), last)


def l1f_zero_pool(k, g):
    g.did(k.nc.gpsimd.memset(L1f(k).zeros, 0.0), k.parts_ready)


def l1f_zero_sync(k, sp):
    T = L1f(k)
    sp.wait_ge(k.parts_ready, 1)
    flat = lambda ap, a, b: ap[a:b, :].rearrange("(p r) d -> p (r d)", p=P)
    sp.dma_start(flat(k.slots, 0, 1024), T.zeros).then_inc(k.dram_zeroed, 16)
    sp.dma_start(flat(k.slots, 1024, NSLOT), T.zeros[:, 0:512]).then_inc(k.dram_zeroed, 16)
    sp.dma_start(flat(k.eo_rows, NSLOT, ROWS1), T.zeros).then_inc(k.dram_zeroed, 16)


def l1f_pool(k, g):
    nc, T = k.nc, L1f(k)
    g.eng.wait_ge(k.dram_zeroed, 48)
    g.eng.wait_ge(k.slots_ready, 1)
    g.eng.wait_ge(k.normed, NT * 4)
    for t in range(NT):
        nc.gpsimd.indirect_dma_start(out=k.slots[:, :], out_offset=bass.IndirectOffsetOnAxis(ap=k.idx[:, t:t + 1], axis=0),
                                     in_=k.xn[:, t, :], in_offset=None).then_inc(k.scattered, 16)
    g.eng.wait_ge(k.eo_stored, 16 * 4)
    for t in range(NT):
        nc.gpsimd.indirect_dma_start(out=T.y[:, t, :], out_offset=None, in_=k.eo_rows[:, :],
                                     in_offset=bass.IndirectOffsetOnAxis(ap=k.idx[:, t:t + 1], axis=0)).then_inc(k.y_loaded, 16)


def l1f_sync(k, sp):
    T = L1f(k)
    sp.wait_ge(k.scattered, 16 * NT)
    sp.dma_start(T.xg, k.slots[0:NSLOT, :].rearrange("(j p) d -> p j d", p=P)).then_inc(k.slots_loaded, 16)
    for e in range(0, E8, 2):
        for i in range(2):
            k.drained(sp, ("L1f", "eo", e + i))
        sp.dma_start(k.eo_rows[e * CAP:(e + 2) * CAP, :].rearrange("(e j p) d -> p e j d", e=2, p=CT),
                     T.eo[0:CT, e:e + 2, :, :]).then_inc(k.eo_stored, 16)


class L2f:
    def __init__(self, k):
        at = PLACE["L0x"]
        self.xgT = k.cols(at, [E16, B, CAP2])
        self.hs = k.cols(at + 2048, [2, N])
        self.scb = k.cols(at + 4096, [2, S])
        at = ARENA
        self.selw = k.cols(at, [E16 // 2, B, S])
        self.eo = k.cols(at + 8192, [E16 // 2, B, D])
        self.h = k.cols(at + 10240, [4, 2, P])
        self.sel = k.cols(at, [NT, 1024], BF16)
        self.xp = k.cols(at + 4096, [3, NT * D], BF16)
        self.tmp = k.cols(at + 4096 + 1536, [NT * D])
        self.work = k.cols(at + 4096 + 2560, [S])[0:32]
        self.mask = k.cols(at + 4096 + 3072, [S])[0:32]
        self.cum = k.cols(at + 4096 + 3584, [S])[0:32]
        self.sg = k.small[:, 0:1024].rearrange("p (a b) -> p a b", a=2)
        self.ge = k.cmp[:, :, 0:256]
        self.stT = k.nmT[:, 0:S]


def l2f_pool(k, g):
    nc, T = k.nc, L2f(k)
    g.eng.wait_ge(k.normed, NT * 6)
    src = k.xn[:, :, :].rearrange("p t d -> p (t d)")
    g.did(nc.gpsimd.tensor_copy(T.xp[:, 0, :], src))
    g.settle()
    g.did(nc.gpsimd.tensor_tensor(T.tmp, src, T.xp[:, 0, :], ALU.subtract))
    g.settle()
    g.did(nc.gpsimd.tensor_copy(T.xp[:, 1, :], T.tmp))
    g.settle()
    g.did(nc.gpsimd.tensor_tensor(T.xp[:, 2, :], T.tmp, T.xp[:, 1, :], ALU.subtract), k.parts_ready)


SHARED2 = [(c, b) for c in range(2) for b in range(B)]


def l2f_vector(k, v):
    nc, T = k.nc, L2f(k)
    softmax_vector(k, v, "L2f", E16)
    p2 = k.rt[:, 2, :].rearrange("p (i c) -> p i c", i=TB)
    v.did(nc.vector.tensor_copy(p2.rearrange("p i (b e) -> p b i e", b=B), k.rt[:, 1, :].rearrange("p (b i e) -> p b i e", b=B, i=TB)), k.w_ready)
    v.settle()
    ps = k.filled(v.eng, ("L2f", "pT"))
    v.drain(("L2f", "pT"), nc.vector.tensor_copy(T.work, ps[0:32, :]))
    v.settle()
    for _ in range(CAP2 // 8):
        v.did(nc.vector.max(k.top8[0:32, :], T.work))
        v.settle()
        v.did(nc.vector.match_replace(out=T.work, in_to_replace=k.top8[0:32, :], in_values=T.work, imm_value=-1.0))
        v.settle()
    v.did(nc.vector.tensor_scalar(T.mask, T.work, 0.0, None, ALU.is_lt))
    v.settle()
    v.did(nc.vector.tensor_tensor_scan(T.cum, T.mask, T.mask, 0.0, ALU.add, ALU.max))
    v.settle()
    v.did(nc.vector.tensor_tensor(T.work, T.cum, T.mask, ALU.mult), k.slots_ready)
    for turn, (c, b) in enumerate(SHARED2):
        k.drained(v.eng, ("L2f", "sg", c, b))
        ps = k.filled(v.eng, ("L2f", "su", c, b))
        v.drain(("L2f", "su", c, b), nc.vector.tensor_tensor(T.hs[:, c, b * S:(b + 1) * S], T.sg[:, turn % 2, :], ps[:, :], ALU.mult))
    parts = [k.mpad[:, 0:TB, 32 * i:32 * (i + 1)] for i in range(3)]
    three_parts(k, v, p2, parts, [k.rt[:, 3, :].rearrange("p (i c) -> p i c", i=TB)], None)
    ps = k.filled(v.eng, ("L2f", "slots"))
    v.drain(("L2f", "slots"), nc.vector.tensor_copy(k.mpad[:, 0:TB, 96:128], ps[:, 0:TB * 32].rearrange("p (i c) -> p i c", i=TB)))
    v.settle()
    iota = k.w("sel", "slot_iota").rearrange("p (e c) -> p e c", e=E16)
    for b in range(B):
        for i in range(TB):
            v.did(nc.vector.tensor_tensor(T.sel[:, b * TB + i, :].rearrange("p (e c) -> p e c", e=E16),
                                          bc(k.mpad[:, i, 96 + b * E16:96 + (b + 1) * E16], 2, [E16, CAP2]), iota, ALU.is_equal),
                  k.gather_sel)
    for b in range(B):
        for half in range(2):
            k.filled(v.eng, ("L2f", "xg", b, half))
    for kk in range(E16 // 2):
        for e in (2 * kk, 2 * kk + 1):
            ps = k.filled(v.eng, ("L2f", "gu", e))
            v.eng.wait_ge(k.act_copied, e + 1)
            if e >= 4:
                k.filled(v.eng, ("L2f", "eo", (e - 4) // 2))
            v.drain(("L2f", "gu", e), nc.vector.tensor_tensor(T.h[:, e % 4, :, :].rearrange("p f c -> p (f c)"), T.ge[:, e % 2, :],
                                                              ps[:, 256:512], ALU.mult))
        for b in range(B):
            ps = k.filled(v.eng, ("L2f", "bs", kk, b, 0))
            k.drained(v.eng, ("L2f", "bs", kk, b, 1))
            v.drain(("L2f", "bs", kk, b, 0), nc.vector.scalar_tensor_tensor(
                out=T.selw[:, kk, b, :], in0=ps[:, :], scalar=k.w("const", "slot_no"), in1=T.scb[:, b, :], op0=ALU.is_equal, op1=ALU.mult))


def l2f_scalar(k, a):
    nc, T = k.nc, L2f(k)
    softmax_scalar(k, a, "L2f", E16)
    for turn, (c, b) in enumerate(SHARED2):
        if turn >= 2:
            k.drained(a.eng, ("L2f", "su", *SHARED2[turn - 2]))
        ps = k.filled(a.eng, ("L2f", "sg", c, b))
        a.drain(("L2f", "sg", c, b), nc.scalar.activation(T.sg[:, turn % 2, :], ps[:, :], ACT.Gelu))
    ps = k.filled(a.eng, ("L2f", "stT"))
    a.drain(("L2f", "stT"), nc.scalar.activation(T.stT, ps[:, :].bitcast(BF16)[:, 0:S], ACT.Copy))
    for b in range(B):
        for half in range(2):
            ps = k.filled(a.eng, ("L2f", "xg", b, half))
            a.drain(("L2f", "xg", b, half), nc.scalar.activation(
                T.xgT[:, half * 8:(half + 1) * 8, b, :], ps[:, :].rearrange("p (e c) -> p e c", e=8), ACT.Copy))
    for kk in range(E16 // 2):
        for e in (2 * kk, 2 * kk + 1):
            ps = k.filled(a.eng, ("L2f", "gu", e))
            if e >= 2:
                k.drained(a.eng, ("L2f", "gu", e - 2))
            a.did(nc.scalar.activation(T.ge[:, e % 2, :], ps[:, 0:256], ACT.Gelu), k.act_copied)
        for b in range(B):
            if kk:
                k.drained(a.eng, ("L2f", "bs", kk - 1, b, 0))
            ps = k.filled(a.eng, ("L2f", "bs", kk, b, 1))
            a.drain(("L2f", "bs", kk, b, 1), nc.scalar.activation(T.scb[:, b, :], ps[:, :], ACT.Copy))
        if kk:
            eo_scalar(k, a, T, kk - 1)
    eo_scalar(k, a, T, E16 // 2 - 1)


def eo_scalar(k, a, T, kk):
    ps = k.filled(a.eng, ("L2f", "eo", kk))
    a.drain(("L2f", "eo", kk), k.nc.scalar.activation(T.eo[:, kk, :, :], ps[:, 0:2 * D].rearrange("p (b d) -> p b d", b=B), ACT.Copy))


def l2f_tensor(k, pe):
    nc, T = k.nc, L2f(k)
    logits_tensor(k, pe, "L2f", 5, E16)
    ps = k.open(pe, ("L2f", "pT"))
    pe.wait_ge(k.w_ready, 3)
    for i in range(TB):
        last = nc.tensor.transpose(ps[0:32, i * P:(i + 1) * P], k.rt[:, 2, 32 * i:32 * (i + 1)], k.w("const", "ident"))
    k.fill(("L2f", "pT"), last)
    for c, b in SHARED2:
        for kind in ("sg", "su"):
            ps = k.open(pe, ("L2f", kind, c, b))
            k.fill(("L2f", kind, c, b), nc.tensor.matmul(ps[:, :], k.w("L2f", kind)[:, c * P:(c + 1) * P], k.xnT[:, b * S:(b + 1) * S],
                                                         start=True, stop=True))
    ps = k.open(pe, ("L2f", "slots"))
    pe.wait_ge(k.slots_ready, 2)
    for i in range(TB):
        last = nc.tensor.transpose(ps[:, 32 * i:32 * (i + 1)], T.work[:, i * P:(i + 1) * P], k.w("const", "ident")[0:32, 0:32])
    k.fill(("L2f", "slots"), last)
    ps = k.open(pe, ("L2f", "stT"))
    k.drained(pe, ("L2f", "slots"))
    for i in range(TB):
        last = nc.tensor.transpose(ps[:, :].bitcast(BF16)[:, i * P:(i + 1) * P], k.mpad[:, i, :], k.w("sel", "ident"))
    k.fill(("L2f", "stT"), last)
    pe.wait_ge(k.parts_ready, 2)
    for b in range(B):
        for half in range(2):
            ps = k.open(pe, ("L2f", "xg", b, half))
            for i in range(TB):
                t = b * TB + i
                pe.wait_ge(k.gather_sel, t + 1)
                for part in range(3):
                    last = nc.tensor.matmul(ps[:, :], T.xp[:, part, t * D:(t + 1) * D], T.sel[:, t, half * 512:(half + 1) * 512],
                                            start=(i == 0 and part == 0), stop=(i == TB - 1 and part == 2))
            k.fill(("L2f", "xg", b, half), last)
    k.drained(pe, ("L2f", "stT"))

    def down(kk):
        ps = k.open(pe, ("L2f", "eo", kk))
        for e2 in range(2):
            e = 2 * kk + e2
            k.drained(pe, ("L2f", "gu", e))
            for b in range(B):
                for f in range(2):
                    last = nc.tensor.matmul(ps[64 * e2:64 * (e2 + 1), b * D:(b + 1) * D], T.h[:, e % 4, f, b * CAP2:(b + 1) * CAP2],
                                            k.w("L2f", "d")[:, (2 * e + f) * D:(2 * e + f + 1) * D], start=(f == 0), stop=(f == 1))
        k.fill(("L2f", "eo", kk), last)

    for kk in range(E16 // 2):
        for e in (2 * kk, 2 * kk + 1):
            ps = k.open(pe, ("L2f", "gu", e))
            for b in range(B):
                k.drained(pe, ("L2f", "xg", b, e // 8))
            for j, name in enumerate(("g", "g", "u", "u")):
                at = e * 256 + (j % 2) * P
                last = nc.tensor.matmul(ps[:, j * P:(j + 1) * P], k.w("L2f", name)[:, at:at + P],
                                        T.xgT[:, e, :, :].rearrange("p b c -> p (b c)"), start=True, stop=True)
            k.fill(("L2f", "gu", e), last)
        for b in range(B):
            for x, name in enumerate(("slot", "score")):
                ps = k.open(pe, ("L2f", "bs", kk, b, x))
                at = (b * 8 + kk) * P
                k.fill(("L2f", "bs", kk, b, x), nc.tensor.matmul(ps[:, :], k.w("sel", name)[:, at:at + P], T.stT, start=True, stop=True))
        if kk:
            down(kk - 1)
    down(E16 // 2 - 1)
    open_acc(k, pe, 5)
    for b in range(B):
        for kk in range(E16 // 2):
            k.drained(pe, ("L2f", "bs", kk, b, 0))
            k.drained(pe, ("L2f", "eo", kk))
        for c in range(2):
            k.drained(pe, ("L2f", "su", c, b))
        for i in range(TB):
            t = b * TB + i
            out = k.acc[b][:, i * D:(i + 1) * D]
            for c in range(2):
                nc.tensor.matmul(out, T.hs[:, c, t * P:(t + 1) * P], k.w("L2f", "sd")[:, c * D:(c + 1) * D], start=(c == 0), stop=False)
            for kk in range(E16 // 2):
                last = nc.tensor.matmul(out, T.selw[:, kk, b, i * P:(i + 1) * P], T.eo[:, kk, b, :], start=False, stop=(kk == 7))
        last.then_inc(k.acc_filled, 1)


def build(nc, dram, x_in, out):
    with ExitStack() as ctx:
        k = Core(nc, ctx, dram, out)
        block = ctx.enter_context(nc.Block())
        A0, A2, A3 = (Attention(k, L, n) for L, n in (("L0x", 0), ("L2x", 4), ("L3x", 6)))
        M0 = Moe(k, "L0f", 1, P, 6, 4)
        M3 = Moe(k, "L3f", 7, 96, 10, 8)

        @block.sync
        def _(sp):
            sp.dma_start(k.x[:, :, :], x_in.rearrange("(t p) d -> p t d", p=P)).then_inc(k.x_loaded, 16)
            for g in ("const", "ctx", "L0x", "rows", "sel", "L0f", "L1x", "L1f"):
                dst = k.packed[g][:, :] if g in ("const", "ctx", "sel", "rows") else k.packed[g]
                src = dram[g]
                if g == "rows":
                    src = src.to_broadcast([P, WIDTH[g]])
                sp.dma_start(dst, src).then_inc(k.loaded[g], 16)
            l1f_zero_sync(k, sp)
            sp.wait_ge(k.x_ready, 1)
            for g in ("L2x", "L2f"):
                sp.dma_start(k.packed[g], dram[g]).then_inc(k.loaded[g], 16)
            l1f_sync(k, sp)
            sp.wait_ge(k.x_ready, 4)
            for g in ("L3x", "L3f"):
                sp.dma_start(k.packed[g], dram[g]).then_inc(k.loaded[g], 16)
            sp.wait_ge(k.x_ready, SUBLAYERS)
            sp.dma_start(out.rearrange("(t p) d -> p t d", p=P), k.x[:, :, :]).then_inc(k.out_stored, 16)
            sp.wait_ge(k.out_stored, 16)

        @block.gpsimd
        def _(eng):
            g = Chain(k, eng, k.pool_step)
            l1f_zero_pool(k, g)
            attention_prep_pool(k, g, A0)
            norm_pool(k, g, 0)
            moe_pool(k, g)
            norm_pool(k, g, 1)
            l1x_pool(k, g)
            norm_pool(k, g, 2)
            norm_pool(k, g, 3)
            l1f_pool(k, g)
            attention_prep_pool(k, g, A2)
            norm_pool(k, g, 4)
            norm_pool(k, g, 5)
            l2f_pool(k, g)
            attention_prep_pool(k, g, A3)
            norm_pool(k, g, 6)
            norm_pool(k, g, 7)

        @block.scalar
        def _(eng):
            a = Chain(k, eng, k.scalar_step)
            eng.wait_ge(k.loaded["rows"], 16)
            a.did(nc.scalar.activation(k.gates[:, :], k.w("rows", "g"), ACT.Tanh), k.gates_ready)
            norm_scalar(k, a, 0)
            attention_scalar_q(k, a, A0)
            attention_scalar(k, a, A0)
            norm_scalar(k, a, 1)
            moe_scalar(k, a, M0)
            l1x_prep_scalar(k, a)
            norm_scalar(k, a, 2)
            l1x_scalar(k, a)
            norm_scalar(k, a, 3)
            l1f_scalar(k, a)
            norm_scalar(k, a, 4)
            attention_scalar_q(k, a, A2)
            attention_scalar(k, a, A2)
            norm_scalar(k, a, 5)
            l2f_scalar(k, a)
            norm_scalar(k, a, 6)
            attention_scalar_q(k, a, A3)
            attention_scalar(k, a, A3)
            norm_scalar(k, a, 7)
            moe_scalar(k, a, M3)

        @block.vector
        def _(eng):
            v = Chain(k, eng, k.vector_step)
            eng.wait_ge(k.x_loaded, 16)
            attention_prep_vector(k, v, A0)
            norm_vector(k, v, 0, k.w("rows", "L0_b2"))
            attention_vector(k, v, A0)
            residual_vector(k, v, 0, k.xb)
            done(k, v)
            norm_vector(k, v, 1)
            moe_vector(k, v, M0)
            residual_vector(k, v, 1, k.x)
            done(k, v)
            l1x_prep_vector(k, v)
            norm_vector(k, v, 2, k.w("rows", "L1_bf2"))
            l1x_vector(k, v)
            done(k, v)
            norm_vector(k, v, 3)
            l1f_vector(k, v)
            done(k, v)
            attention_prep_vector(k, v, A2)
            norm_vector(k, v, 4, k.w("rows", "L2_bo"))
            attention_vector(k, v, A2)
            residual_vector(k, v, 4, k.xb)
            done(k, v)
            norm_vector(k, v, 5)
            l2f_vector(k, v)
            residual_vector(k, v, 5, k.x)
            done(k, v)
            attention_prep_vector(k, v, A3)
            norm_vector(k, v, 6, k.w("rows", "L3_bo"))
            attention_vector(k, v, A3)
            residual_vector(k, v, 6, k.xb)
            done(k, v)
            norm_vector(k, v, 7)
            moe_vector(k, v, M3)
            residual_vector(k, v, 7, k.x)
            done(k, v)

        @block.tensor
        def _(pe):
            pe.wait_ge(k.loaded["const"], 16)
            attention_prep_tensor(k, pe, A0)
            norm_tensor(k, pe, 0)
            pe.wait_ge(k.loaded["sel"], 16)
            attention_tensor(k, pe, A0)
            norm_tensor(k, pe, 1)
            moe_tensor(k, pe, M0)
            l1x_prep_tensor(k, pe)
            norm_tensor(k, pe, 2)
            l1x_tensor(k, pe)
            norm_tensor(k, pe, 3)
            l1f_tensor(k, pe)
            attention_prep_tensor(k, pe, A2)
            norm_tensor(k, pe, 4)
            attention_tensor(k, pe, A2)
            norm_tensor(k, pe, 5)
            l2f_tensor(k, pe)
            attention_prep_tensor(k, pe, A3)
            norm_tensor(k, pe, 6)
            attention_tensor(k, pe, A3)
            norm_tensor(k, pe, 7)
            moe_tensor(k, pe, M3)


def layout(np, i, bf16):
    def rows(a):
        out = np.zeros((P, a.shape[1]), a.dtype)
        out[:a.shape[0]] = a
        return out

    def chunked(a, n=P):
        return rows(a.reshape(-1, n, a.shape[1]).transpose(1, 0, 2).reshape(n, -1))

    def col(a, n=P):
        return rows(np.ascontiguousarray(a.reshape(-1, n).T))

    f32 = np.float32
    x = i["x"].reshape(N, D)
    ctxT = i["ctx_768"].reshape(NK, DC).T
    rem = np.zeros((DC, B, HG, HP), f32)
    for b in range(B):
        rem[:, b, :, :MR] = ctxT[:, None, b * M + P:(b + 1) * M]
    r = np.arange(P)[:, None]
    e = np.arange(8)
    dup = lambda w: np.concatenate([w.T, w.T], axis=1)
    kv = i["L2_xattn_Wkv"].reshape(H, 2, 8, DC)
    bkv = i["L2_xattn_bkv"].reshape(H, 2, 8)
    w1_3 = i["L3_ffn_W1"].transpose(2, 0, 1)
    s1_3 = i["L3_ffn_Ws1"].T
    w_2_1 = i["L1_ffn_w2"].reshape(8, 4, P, D).transpose(2, 0, 1, 3).reshape(P, -1)
    d_2 = i["L2_ffn_Wd"].transpose(0, 2, 1).reshape(16, 2, P, D).transpose(2, 0, 1, 3).reshape(P, -1)
    parts = {
        "const": dict(
            ident=np.eye(P), ones=np.ones((P, P)), head_rows=(r // 8 == np.arange(16)),
            rem_rows=(r // HP == np.arange(HG)) & (r % HP < MR),
            earlier=np.broadcast_to((e[None, :] < e[:, None]).reshape(1, 64), (P, 64)),
            slot_no=r % CAP2 + 1, neg_half=np.full((P, 8), -0.5),
            expert_base=np.broadcast_to(np.tile(e * CAP - 1.0, 8), (P, 64)), dummy_row=NSLOT + r + P * e),
        "ctx": dict(ctxT=rows(ctxT), ctx_rem=rows(rem.reshape(DC, -1))),
        "L0x": dict(Wk=rows(i["L0_xattn_Wk"]), Wv=rows(i["L0_xattn_Wv"]), Wq=i["L0_xattn_Wq"], W1=i["L0_xattn_W1"],
                    W2=chunked(i["L0_xattn_W2"]), bq=col(i["L0_xattn_bq"]), bk=col(i["L0_xattn_bk"]), b1=col(i["L0_xattn_b1"])),
        "L0f": dict(Wr=i["L0_ffn_router_w"], gate=i["L0_ffn_gate_w"].transpose(1, 0, 2).reshape(D, -1),
                    up=i["L0_ffn_up_w"].transpose(1, 0, 2).reshape(D, -1), sgate=i["L0_ffn_s_gate_w"], sup=i["L0_ffn_s_up_w"],
                    down=chunked(i["L0_ffn_down_w"].reshape(512, D)), sdown=chunked(i["L0_ffn_s_down_w"])),
        "L1x": dict(d2v=rows(i["L1_xattn_W_d2v"].T), img=i["L1_xattn_W_img"].T, att0=dup(i["L1_xattn_W_att0"]),
                    att1=dup(i["L1_xattn_W_att1"]), txt=i["L1_xattn_W_txt"].T, f1=chunked(i["L1_xattn_W_f1"].T),
                    f2=chunked(i["L1_xattn_W_f2"].T), b_d2v=col(i["L1_xattn_b_d2v"]), b_img=col(i["L1_xattn_b_img"]),
                    b_att0=col(np.tile(i["L1_xattn_b_att0"], 2)), b_att1=col(np.tile(i["L1_xattn_b_att1"], 2)),
                    b_txt=col(i["L1_xattn_b_txt"]), b_f1=col(i["L1_xattn_b_f1"])),
        "L1f": dict(Wr=i["L1_ffn_router_w"].T, w1=i["L1_ffn_w1"].transpose(1, 0, 2).reshape(D, -1), w2=w_2_1,
                    b1=i["L1_ffn_b1"].reshape(8, 4, P).transpose(2, 0, 1).reshape(P, -1)),
        "L2x": dict(Wk=rows(kv[:, 0].reshape(P, DC).T), Wv=rows(kv[:, 1].reshape(P, DC).T), Wq=i["L2_xattn_Wq"].T,
                    Wo=i["L2_xattn_Wo"].T, bq=col(i["L2_xattn_bq"]), bk=col(bkv[:, 0].reshape(P))),
        "L2f": dict(Wr=i["L2_ffn_gate_w"].T, sg=i["L2_ffn_Ws_g"].T, su=i["L2_ffn_Ws_u"].T, sd=chunked(i["L2_ffn_Ws_d"].T),
                    g=i["L2_ffn_Wg"].transpose(2, 0, 1).reshape(D, -1), u=i["L2_ffn_Wu"].transpose(2, 0, 1).reshape(D, -1),
                    d=d_2),
        "L3x": dict(Wk=rows(i["L3_xattn_Wk"]), Wv=rows(i["L3_xattn_Wv"]), Wq=i["L3_xattn_Wq"], Wo=chunked(i["L3_xattn_Wo"])),
        "L3f": dict(Wr=i["L3_ffn_gate_w"].T,
                    gate=np.concatenate([w1_3[:, :, 96:].reshape(D, -1), s1_3[:, 192:]], axis=1),
                    up=np.concatenate([w1_3[:, :, :96].reshape(D, -1), s1_3[:, :192]], axis=1),
                    down=np.concatenate([rows(i["L3_ffn_W2"].transpose(2, 0, 1).reshape(96, -1)),
                                         chunked(i["L3_ffn_Ws2"].T, 96)], axis=1)),
        "rows": dict(g=np.stack([i["g_xattn"], i["g_ffn"]], axis=1).reshape(1, 8), rb=i["L0_ffn_router_bias"].reshape(1, 1),
                     L0_bv=i["L0_xattn_bv"], L0_b2=i["L0_xattn_b2"], L1_bf2=i["L1_xattn_b_f2"], L1_b2=i["L1_ffn_b2"],
                     L2_bv=bkv[:, 1], L2_bo=i["L2_xattn_bo"], L3_bo=i["L3_xattn_bo"]),
    }
    m = np.arange(P)
    c = np.arange(4)
    mm = np.zeros((P, 16, P))
    for h in range(16):
        mm[h, h] = mm[16 + h, h] = 1
    s0, s3 = np.zeros((P, 4, P)), np.zeros((P, 8, 96))
    slot, score = np.zeros((P, B, 8, P)), np.zeros((P, B, 8, P))
    for part in range(3):
        for q in range(8):
            s0[part * 8 + q, q // 2, (q % 2) * 64:(q % 2) * 64 + 64] = 1
            s3[part * 8 + q, q] = 1
        for b in range(B):
            for q in range(16):
                cs = slice((q % 2) * 64, (q % 2) * 64 + 64)
                score[part * 32 + b * 16 + q, b, q // 2, cs] = 1
                slot[96 + b * 16 + q, b, q // 2, cs] = 1
    parts["sel"] = dict(ident=np.eye(P), ones=np.ones((P, P)), upto=(r <= m), minus_max=mm, L0f=s0, L3f=s3, slot=slot,
                        score=score, slot_iota=np.broadcast_to(np.tile(np.arange(CAP2) + 1, 16), (P, 1024)))
    packed = {}
    for group, items in PACK.items():
        n = 1 if group == "rows" else P
        dt = bf16 if group == "sel" else f32
        cols = [np.asarray(parts[group][name], dt).reshape(n, width) for name, width in items]
        packed[group] = np.ascontiguousarray(np.concatenate(cols, axis=1))
    return x, packed


def kernel(**inputs):
    import numpy as np
    import concourse.bacc as bacc
    from concourse.bass_utils import run_bass_kernel_spmd

    i = {name: np.asarray(a) for name, a in inputs.items()}
    x, packed = layout(np, i, mybir.dt.np(BF16))
    nc = bacc.Bacc("TRN2", target_bir_lowering=False, num_devices=1)
    arrays = {"x_in": np.ascontiguousarray(x)}
    dram = {}
    x_ap = nc.dram_tensor("x_in", x.shape, F32, kind="ExternalInput").ap()
    for group, a in packed.items():
        arrays[f"in_{group}"] = a
        dram[group] = nc.dram_tensor(f"in_{group}", a.shape, mybir.dt.from_np(a.dtype), kind="ExternalInput").ap()
    out = nc.dram_tensor("x_out", (N, D), F32, kind="ExternalOutput").ap()
    build(nc, dram, x_ap, out)
    r = run_bass_kernel_spmd(nc, [arrays], core_ids=[0])
    return r.results[0]["x_out"].reshape(B, S, D)
```

```python
from contextlib import ExitStack

import concourse.bass as bass
from concourse import mybir

ALU = mybir.AluOpType
ACT = mybir.ActivationFunctionType
AX = mybir.AxisListType
F32 = mybir.dt.float32
BF16 = mybir.dt.bfloat16
U32 = mybir.dt.uint32

P = 128
B, S, D = 2, 512, 128
N = B * S
NT = N // P
TB = S // P
M, DC = 154, 96
MR = M - P
NK = B * M
H = 16
HP = 32
HG = P // HP
NG = H // HG
EPS = 1e-5
E8 = 8
CAP = 192
NSLOT = E8 * CAP
CT = CAP // 2
E16, CAP2 = 16, 64
MAGIC = 12582912.0
NRING = 6


PACK = {
    "const": [("ident", 128), ("ones", 128), ("rem_rows", 4), ("earlier", 64),
              ("slot_no", 1), ("neg_half", 8), ("expert_base", 64), ("dummy_row", 8)],
    "ctx": [("ctxT", NK), ("ctx_rem", B * P)],
    "L0x": [("Wk", 128), ("Wv", 128), ("Wq", 128), ("W1", 256), ("W2", 256), ("bq", 1), ("bk", 1), ("b1", 2)],
    "L0f": [("Wr", 8), ("gate", 512), ("up", 512), ("sgate", 256), ("sup", 256), ("down", 512), ("sdown", 256)],
    "L1x": [("d2v", 128), ("img", 128), ("att0", 128), ("att1", 128), ("txt", 128), ("f1", 1024), ("f2", 512),
            ("b_d2v", 1), ("b_img", 1), ("b_att0", 1), ("b_att1", 1), ("b_txt", 1), ("b_f1", 4)],
    "L1f": [("Wr", 8), ("w1", 8 * 512), ("w2", 8 * 512), ("b1", 32)],
    "L2x": [("Wk", 128), ("Wv", 128), ("Wq", 128), ("Wo", 128), ("bq", 1), ("bk", 1)],
    "L2f": [("Wr", 16), ("sg", 256), ("su", 256), ("sd", 256), ("g", 4096), ("u", 4096), ("d", 4096)],
    "L3x": [("Wk", 1024), ("Wv", 1024), ("WqT", H * 128), ("Wo", 1024)],
    "L3f": [("Wr", 8), ("gate", 960), ("up", 960), ("down", 1280)],
    "sel": [("ident", 128), ("ones", 128), ("upto", 128), ("minus_max", 16 * 128), ("L0f", 4 * 128), ("L3f", 8 * 96),
            ("slot", 16 * 128), ("score", 16 * 128), ("slot_iota", 1024)],
    "rows": [("g", 8), ("rb", 1), ("L0_bv", 128), ("L0_b2", 128), ("L1_bf2", 128), ("L1_b2", 1024),
             ("L2_bv", 128), ("L2_bo", 128), ("L3_bo", 128)],
}
WIDTH = {group: sum(n for _, n in items) for group, items in PACK.items()}


def columns(group, name):
    at = 0
    for part, n in PACK[group]:
        if part == name:
            return at, at + n
        at += n
    raise KeyError(name)


EARLY = ["L0x", "L0f", "L1x", "L1f", "L2x", "L2f"]
PLACE, ARENA = {}, 0
for _g in EARLY:
    PLACE[_g] = ARENA
    ARENA += WIDTH[_g]
PLACE["L3x"] = PLACE["L1f"]
PLACE["L3f"] = PLACE["L1f"] + WIDTH["L3x"]
assert WIDTH["L3x"] <= WIDTH["L1f"] and PLACE["L3f"] + WIDTH["L3f"] <= PLACE["L2f"]
ARENA_SIZE = 11500


class Banks:

    def __init__(self, labels):
        self.at = {label: (i % NRING, i // NRING) for i, label in enumerate(labels)}
        assert len(self.at) == len(labels)


def attention8_prep_jobs(L):
    return [(L, "k")] + [(L, kind, b) for b in range(B) for kind in ("v", "vr")]


def attention8_jobs(L):
    n = {"L0x": 0, "L2x": 4}[L]
    jobs = [job for b in range(B) for job in (("xnT", n, b), (L, "q", b))]
    for b in range(B):
        jobs += [(L, "s", t, p) for t in range(b * TB, (b + 1) * TB) for p in range(H // 2)] + [(L, "nmT", b)]
    steps = [(b, g) for b in range(B) for g in range(NG)]

    def scores_T(b, g):
        return [(L, "st", b, g, j) for j in range(HG)] + [(L, "sr", b, g)]

    jobs += scores_T(*steps[0])
    for n, step in enumerate(steps):
        jobs += scores_T(*steps[n + 1]) if n + 1 < len(steps) else []
        if n:
            jobs += [(L, "ot", *steps[n - 1])] + (l1x_prep_jobs(n - 1) if L == "L0x" else [])
        jobs += [(L, "pv", *step)]
    jobs += [(L, "ot", *steps[-1])] + [(L, "oT", b) for b in range(B)]
    return jobs + ([(L, "h", c, b) for b in range(B) for c in range(2)] if L == "L0x" else [])


def moe_jobs(L, n, chunks, routed):
    jobs = []
    first = [(c, b) for c in range(routed) for b in range(B)]
    for b in range(B):
        jobs += [("xnT", n, b)] + [(L, "logits")] * (b == B - 1)
        jobs += [(L, kind, c, b) for c in range(routed, chunks) for kind in ("g", "u")]
    jobs += [(L, "wT", b) for b in range(B)]
    for turn, (c, b) in enumerate(first, B * (chunks - routed)):
        jobs += l1x_prep_jobs(L1X_PREP_TURNS[turn]) if L == "L0f" and turn in L1X_PREP_TURNS else []
        jobs += [(L, "g", c, b), (L, "u", c, b), (L, "w", c, b)]
    return jobs


AMAX = ["ctx", "vis", "img", "x", "cat", "h"]


def amax_jobs(name):
    return [("L1x", "amT", name), ("L1x", "amB", name)]


def l1x_prep_jobs(step):
    name, turn = L1X_PREP[step]
    if turn == "amT":
        return [("L1x", "amT", name)]
    if turn == "amB":
        return [("L1x", "amB", name)]
    if name == "kv":
        return [("L1x", "kv", a) for a in range(2)]
    if name == "kvT":
        return [("L1x", "kvT", a, b) for a in range(2) for b in range(B)]
    return [("L1x", name)]


L1X_PREP = [("wsum", None), ("ctx", "amT"), ("ctx", "amB"), ("vis", None), ("vis", "amT"), ("vis", "amB"),
            ("img", None), ("img", "amT"), ("img", "amB"), ("kv", None), ("kvT", None)]
L1X_PREP_TURNS = {5: 7, 7: 8, 9: 9, 11: 10}
assert B * NG - 1 + len(L1X_PREP_TURNS) == len(L1X_PREP)


def l1x_jobs():
    jobs = amax_jobs("x") + [("L1x", "txt", b) for b in range(B)]
    for a in range(2):
        jobs += [("L1x", "s", a, t) for t in range(0, NT, 2)]
        for b in range(B):
            jobs += [("L1x", "pT", a, b, 0), ("L1x", "pT", a, b, 1), ("L1x", "o", a, b)]
    jobs += amax_jobs("cat") + [("L1x", "f1", c, b) for c in range(4) for b in range(B)]
    return jobs + amax_jobs("h")


def l1f_jobs():
    jobs = [("L1f", "logits"), ("L1f", "count")]
    jobs += attention8_prep_jobs("L2x")
    jobs += [("L1f", "xgT", j) for j in range(3)]
    for kind, e in l1f_jobs_order():
        jobs += [("L1f", "h", e, c) for c in range(2)] if kind == "h" else [("L1f", "eo", e)]
    return jobs


def l2f_jobs():
    jobs = [("L2f", "logits"), ("L2f", "pT")]
    jobs += [("L2f", x, c, b) for c in range(2) for b in range(B) for x in ("sg", "su")]
    jobs += [("L2f", "slots")] + [("L2f", "stT")]
    jobs += [("L2f", "xg", b, half) for b in range(B) for half in range(2)]
    for k in range(E16 // 2):
        jobs += [("L2f", "gu", 2 * k), ("L2f", "gu", 2 * k + 1)]
        jobs += [("L2f", "bs", k, b, x) for b in range(B) for x in (0, 1)]
        jobs += [("L2f", "eo", k - 1)] if k else []
    return jobs + [("L2f", "eo", E16 // 2 - 1)]


ALL = ["L0x", "L0f", "L1x", "L1f", "L2x", "L2f", "L3x", "L3f"]
SUBLAYERS = 8


def all_jobs():
    jobs = attention8_prep_jobs("L0x") + attention8_jobs("L0x")
    jobs += moe_jobs("L0f", 1, 6, 4)
    jobs += [("xnT", 2, b) for b in range(B)] + l1x_jobs()
    jobs += [("xnT", 3, b) for b in range(B)] + l1f_jobs()
    jobs += attention8_jobs("L2x")
    jobs += [("xnT", 5, b) for b in range(B)] + l2f_jobs()
    jobs += attention64_jobs("L3x")
    jobs += moe_jobs("L3f", 7, 10, 8)
    return jobs


class Core:

    def __init__(self, nc, ctx, dram, out):
        self.nc, self.dram, self.out = nc, dram, out
        self.banks = Banks(all_jobs())

        def sb(name, shape, dt=F32):
            return ctx.enter_context(nc.sbuf_tensor(name, shape, dt))

        def sem(name):
            return ctx.enter_context(nc.semaphore(name))

        self.bank_filled = [sem(f"bank_filled{i}") for i in range(NRING)]
        self.bank_drained = [sem(f"bank_drained{i}") for i in range(NRING)]
        self.loaded = {g: sem(f"loaded_{g}") for g in PACK}
        self.x_ready = sem("x_ready")
        self.values_done = sem("values_done")
        self.p64_ready = sem("p64_ready")
        self.x_loaded = sem("x_loaded")
        self.out_stored = sem("out_stored")
        self.vector_step = sem("vector_step")
        self.scalar_step = sem("scalar_step")
        self.pool_step = sem("pool_step")
        self.var_ready = sem("var_ready")
        self.rstd_ready = sem("rstd_ready")
        self.normed = sem("normed")
        self.acc_filled = sem("acc_filled")
        self.residual_done = sem("residual_done")
        self.bias_ready = sem("bias_ready")
        self.gates_ready = sem("gates_ready")
        self.zeroed = sem("zeroed")
        self.v_ready = sem("v_ready")
        self.kparts_ready = sem("kparts_ready")
        self.qparts_ready = sem("qparts_ready")
        self.k_stacked = [sem(f"k_stacked{i}") for i in range(2)]
        self.q_stacked = [[sem(f"q_stacked{i}_{b}") for b in range(B)] for i in range(2)]
        self.m_stacked = [[sem(f"m_stacked{i}_{b}") for b in range(B)] for i in range(2)]
        self.nm_ready = sem("nm_ready")
        self.o_ready = sem("o_ready")
        self.l_ready = sem("l_ready")
        self.exp_ready = sem("exp_ready")
        self.w_ready = sem("w_ready")
        self.h_ready = sem("h_ready")
        self.am_ready = sem("am_ready")
        self.q_ready = sem("q_ready")
        self.l1_bias = sem("l1_bias")
        self.p_exp = sem("p_exp")
        self.p_norm = sem("p_norm")
        self.f_ready = sem("f_ready")
        self.slots_ready = sem("slots_ready")
        self.scattered = sem("scattered")
        self.slots_loaded = sem("slots_loaded")
        self.eo_stored = sem("eo_stored")
        self.y_loaded = [sem(f"y_loaded{b}") for b in range(B)]
        self.dram_zeroed = sem("dram_zeroed")
        self.parts_ready = sem("parts_ready")
        self.gather_sel = sem("gather_sel")
        self.scatter_sel = sem("scatter_sel")
        self.act_copied = sem("act_copied")

        self.ps = [ctx.enter_context(nc.psum_tensor(f"ring{i}", [P, 512], F32)) for i in range(NRING)]
        self.acc = [ctx.enter_context(nc.psum_tensor(f"acc{i}", [P, 512], F32)) for i in range(2)]

        self.packed = {g: sb(f"w_{g}", [P, WIDTH[g]], BF16 if g == "sel" else F32)
                       for g in ("const", "ctx", "sel", "rows")}
        self.mem = sb("mem", [P, ARENA + ARENA_SIZE])
        for g, at in PLACE.items():
            self.packed[g] = self.mem[:, at:at + WIDTH[g]]
        self.x = sb("x", [P, NT, D])
        self.xb = sb("xb", [P, NT, D])
        self.xn = sb("xn", [P, NT, D])
        self.xnT = sb("xnT", [P, N])
        self.stats = sb("stats", [P, NT, 6])
        self.mv = sb("mv", [P, NT, 2])
        self.rstd = sb("rstd", [P, NT])
        self.gates = sb("gates", [P, 8])
        self.small = sb("small", [P, 1024])
        self.nm = sb("nm", [P, NT, H])
        self.mpad = sb("mpad", [P, NT, P], BF16)
        self.nmT = sb("nmT", [P, N], BF16)
        self.bqs = sb("bqs", [P, 1])
        self.flag = sb("flag", [P, 4])
        self.den = sb("den", [P, 32])
        self.rden = sb("rden", [P, 2, H])
        self.onehot = sb("onehot", [P, 64], BF16)
        self.gp = sb("gp", [P, NT])
        self.idx = sb("idx", [P, NT], U32)
        self.top8 = sb("top8", [P, 8])
        self.slots = nc.dram_tensor("slots", (ROWS1, D), F32).ap()
        self.eo_rows = nc.dram_tensor("eo_rows", (ROWS1, D), F32).ap()
        self.rt = sb("rt", [P, 5, 128])
        self.cmp = self.xb[:, :, :].rearrange("p t d -> p (t d)").rearrange("p (a b) -> p a b", a=2)
        self.m8 = sb("m8", [P, NT])
        self.s8 = sb("s8", [P, NT])
        self.r8 = sb("r8", [P, NT])
        self.am = sb("am", [P, 8])
        self.m1 = sb("m1", [P, 1])
        self.sc = sb("sc", [P, 12])
        self.ws = sb("ws", [P, 8])
        self.wabs = sb("wabs", [P, 8])
        self.thr = sb("thr", [P, 16])
        self.comb = sb("comb", [P, 8])
        self.avg = sb("avg", [P, 2])
        self.avgq = sb("avgq", [P, 2], BF16)
        self.hm = sb("hm", [P, 4])
        self.l1s = sb("l1s", [P, 3, NT])

    def cols(self, at, shape, dt=F32):
        n = 1
        for d in shape:
            n *= d
        words = n if dt != BF16 else n // 2
        v = self.mem[:, at:at + words]
        if dt != F32:
            v = v.bitcast(dt)
        if len(shape) == 2:
            v = v.rearrange("p (a b) -> p a b", a=shape[0])
        if len(shape) == 3:
            v = v.rearrange("p (a b c) -> p a b c", a=shape[0], b=shape[1])
        if len(shape) == 4:
            v = v.rearrange("p (a b c d) -> p a b c d", a=shape[0], b=shape[1], c=shape[2])
        return v

    def w(self, group, name):
        a, b = columns(group, name)
        return self.packed[group][:, a:b]

    def bank(self, label):
        return self.ps[self.banks.at[label][0]]

    def filled(self, eng, label):
        b, use = self.banks.at[label]
        eng.wait_ge(self.bank_filled[b], use + 1)
        return self.ps[b]

    def drained(self, eng, label):
        b, use = self.banks.at[label]
        eng.wait_ge(self.bank_drained[b], use + 1)

    def open(self, pe, label):
        b, use = self.banks.at[label]
        if use:
            pe.wait_ge(self.bank_drained[b], use)
        return self.ps[b]

    def fill(self, label, ins):
        ins.then_inc(self.bank_filled[self.banks.at[label][0]], 1)

    def drain(self, label, ins):
        b, use = self.banks.at[label]
        ins.then_inc(self.bank_drained[b], 1)
        return self.bank_drained[b], use + 1


class Chain:

    def __init__(self, core, eng, own):
        self.core, self.eng, self.own, self.n, self.counts = core, eng, own, 0, {}
        self.last = None

    def did(self, ins, sem=None):
        sem = self.own if sem is None else sem
        ins.then_inc(sem, 1)
        key = str(sem)
        self.counts[key] = self.counts.get(key, 0) + 1
        self.last = (sem, self.counts[key])

    def drain(self, label, ins):
        self.last = self.core.drain(label, ins)

    def settle(self):
        self.eng.wait_ge(*self.last)


def bc(ap, axis, shape):
    return ap.unsqueeze(axis).to_broadcast([P, *shape])


def norm_vector(k, v, n, b, bias=None):
    nc = k.nc
    ts = range(b * TB, (b + 1) * TB)
    for t in ts:
        v.did(nc.vector.bn_stats(k.stats[:, t, :], k.x[:, t, :]))
    v.settle()
    for t in ts:
        v.did(nc.vector.bn_aggr(k.mv[:, t, :], k.stats[:, t, :]), k.var_ready if t == ts[-1] else None)
    if bias is not None:
        if n == 0:
            v.eng.wait_ge(k.gates_ready, 1)
            v.eng.wait_ge(k.loaded["rows"], 16)
        cs = slice(b * TB, (b + 1) * TB)
        v.did(nc.vector.scalar_tensor_tensor(
            out=k.xb[:, cs, :], in0=bc(bias, 1, [TB, D]), scalar=k.gates[:, n:n + 1], in1=k.x[:, cs, :],
            op0=ALU.mult, op1=ALU.add))
    v.eng.wait_ge(k.rstd_ready, B * n + b + 1)
    for t in ts:
        v.did(nc.vector.tensor_scalar(k.xn[:, t, :], k.x[:, t, :], k.mv[:, t, 0:1], k.rstd[:, t:t + 1],
                                      ALU.subtract, ALU.mult), k.normed)


def norm_pool(k, g, n, b):
    nc = k.nc
    rstd = k.rstd[:, b * TB:(b + 1) * TB]
    g.eng.wait_ge(k.var_ready, B * n + b + 1)
    g.did(nc.gpsimd.tensor_scalar_add(rstd, k.mv[:, b * TB:(b + 1) * TB, 1], EPS))
    g.settle()
    g.did(nc.gpsimd.tensor_tensor(rstd, rstd, k.w("const", "neg_half")[:, 0:TB], ALU.pow), k.rstd_ready)


def norm_tensor(k, pe, n, b):
    ps = k.open(pe, ("xnT", n, b))
    for i in range(TB):
        t = b * TB + i
        pe.wait_ge(k.normed, n * NT + t + 1)
        last = k.nc.tensor.transpose(ps[:, i * P:(i + 1) * P], k.xn[:, t, :], k.w("const", "ident"))
    k.fill(("xnT", n, b), last)


def norm_scalar(k, a, n, b):
    ps = k.filled(a.eng, ("xnT", n, b))
    a.drain(("xnT", n, b), k.nc.scalar.activation(k.xnT[:, b * S:(b + 1) * S], ps[:, :], ACT.Copy))


def wait_xnT(k, eng, n, b):
    k.drained(eng, ("xnT", n, b))


def residual_vector(k, v, n, b, base, gate=None):
    v.eng.wait_ge(k.acc_filled, 2 * acc_use(n) + b + 1)
    cs = slice(b * TB, (b + 1) * TB)
    ins = k.nc.vector.scalar_tensor_tensor(
        out=k.x[:, cs, :], in0=k.acc[b][:, :].rearrange("p (t d) -> p t d", t=TB),
        scalar=k.gates[:, n:n + 1] if gate is None else gate, in1=base[:, cs, :], op0=ALU.mult, op1=ALU.add)
    v.did(ins, k.residual_done)
    v.settle()


ACC_USERS = [0, 1, 2, 4, 5, 6, 7]


def acc_use(n):
    return ACC_USERS.index(n)


def open_acc(k, pe, n):
    if acc_use(n):
        pe.wait_ge(k.residual_done, 2 * acc_use(n))


HW = 160
NPAIR = H // 2
NBLK = H * HW // P
BLK_JOB = 4
GROUPS3 = [(0, 3), (3, 6), (6, 9), (9, 12), (12, 14), (14, 16)]
VW_JOBS = [(5 * i + a, 5 * i + z) for i in range(NBLK // 5) for a, z in ((0, 3), (3, 5))]


def folded_blocks(j):
    out, row = [], 0
    while row < P:
        at = j * P + row
        pair, col = divmod(at, 2 * HW)
        n = min(P - row, 2 * HW - col)
        out.append((row, row + n, pair, col))
        row += n
    return out


def attention64_jobs(L):
    jobs = [(L, "k", c) for c in range(NPAIR)] + [(L, "g", h) for h in range(H)]
    jobs += [("xnT", 6, 0)] + [(L, "v", c) for c in range(NPAIR)]
    scores = lambda t: [(L, "s", t, g) for g in range(len(GROUPS3))]
    folded = lambda b: [(L, "vw", b, i) for i in range(len(VW_JOBS))]
    jobs += scores(0) + [("xnT", 6, 1)] + folded(0)
    for t in range(NT):
        jobs += scores(t + 1) if t + 1 < NT else []
        jobs += folded(1) if t == 0 else []
        jobs += [(L, "pT", t, i) for i in range(NBLK // BLK_JOB)]
    return jobs


class Attention64:

    def __init__(self, k):
        self.L, self.n, self.scale = "L3x", 6, 64.0 ** -0.5
        self.kT = k.cols(0, [NPAIR, NK])
        assert NPAIR * NK <= PLACE["L1f"]
        at = PLACE["L2f"]
        self.wk = k.cols(at, [B, H, M])
        at += B * H * M
        self.vw = k.cols(at, [B, NBLK, D])
        at += B * NBLK * D
        self.p = k.cols(at, [2, H, HW])
        at += 2 * H * HW
        self.pT = k.cols(at, [2, NBLK, P])
        self.vbd = k.cols(at, [NPAIR, B, 2, HW])
        assert at + 2 * NBLK * P <= ARENA + ARENA_SIZE


def attention64_pool(k, g, A):
    nc = k.nc
    g.eng.wait_ge(k.acc_filled, 2 * acc_use(5) + 2)
    g.settle()
    g.did(nc.gpsimd.memset(A.p[:, 0, :, M:HW], 0.0), k.zeroed)
    for half in range(2):
        g.did(nc.gpsimd.memset(A.vbd[:, half * 4:half * 4 + 4, :, :, :], 0.0))
    g.settle()
    g.did(nc.gpsimd.memset(A.p[:, 1, :, M:HW], 0.0), k.zeroed)


ZEROED3 = 4


def attention64_tensor(k, pe, A):
    nc, L = k.nc, A.L
    pe.wait_ge(k.loaded[L], 16)
    ctxT = k.w("ctx", "ctxT")
    pair = lambda name, c: k.w(L, name)[:, c * P:(c + 1) * P]

    def keys(kind, name):
        for c in range(NPAIR):
            ps = k.open(pe, (L, kind, c))
            k.fill((L, kind, c), nc.tensor.matmul(ps[:, 0:NK], pair(name, c), ctxT, start=True, stop=True))

    def fold_keys():
        for h in range(H):
            k.drained(pe, (L, "k", h // 2))
            ps = k.open(pe, (L, "g", h))
            k.fill((L, "g", h), nc.tensor.matmul(ps[:, 0:NK], k.w(L, "WqT")[:, h * P:(h + 1) * P], A.kT[:, h // 2, :],
                                                 start=True, stop=True))

    def fold_values(b):
        for i, (first, end) in enumerate(VW_JOBS):
            ps = k.open(pe, (L, "vw", b, i))
            for j in range(first, end):
                at = (j - first) * D
                for row, last_row, c, col in folded_blocks(j):
                    k.drained(pe, (L, "v", c))
                    last = nc.tensor.matmul(ps[row:last_row, at:at + D],
                                            A.vbd[:, c, b, :, :].rearrange("p h m -> p (h m)")[:, col:col + last_row - row],
                                            pair("Wo", c), start=True, stop=True)
            k.fill((L, "vw", b, i), last)

    def scores(t):
        b = t // TB
        wait_xnT(k, pe, A.n, b)
        for g, (h0, h1) in enumerate(GROUPS3):
            k.drained(pe, (L, "g", h1 - 1))
            k.drained(pe, (L, "g", h1 - 2))
            ps = k.open(pe, (L, "s", t, g))
            k.fill((L, "s", t, g), nc.tensor.matmul(ps[:, 0:(h1 - h0) * M], k.xnT[:, t * P:(t + 1) * P],
                                                    A.wk[:, b, h0:h1, :].rearrange("p h m -> p (h m)"), start=True, stop=True))

    def turn(t):
        p = A.p[:, t % 2, :, :].rearrange("p h m -> p (h m)")
        for i in range(NBLK // BLK_JOB):
            ps = k.open(pe, (L, "pT", t, i))
            last_head = ((i + 1) * BLK_JOB * P - 1) // HW
            groups = next(g for g, (h0, h1) in enumerate(GROUPS3) if last_head < h1) + 1
            pe.wait_ge(k.p64_ready, t * len(GROUPS3) + groups)
            for j in range(BLK_JOB):
                at = (i * BLK_JOB + j) * P
                last = nc.tensor.transpose(ps[:, j * P:(j + 1) * P], p[:, at:at + P], k.w("const", "ident"))
            k.fill((L, "pT", t, i), last)

    def values(t):
        b, i = divmod(t, TB)
        for j in range(NBLK):
            if j % BLK_JOB == 0:
                k.drained(pe, (L, "pT", t, j // BLK_JOB))
            last = nc.tensor.matmul(k.acc[b][:, i * D:(i + 1) * D], A.pT[:, t % 2, j, :], A.vw[:, b, j, :],
                                    start=(j == 0), stop=(j == NBLK - 1))
        last.then_inc(k.values_done if i < TB - 1 else k.acc_filled, 1)

    keys("k", "Wk")
    fold_keys()
    norm_tensor(k, pe, A.n, 0)
    keys("v", "Wv")
    scores(0)
    norm_tensor(k, pe, A.n, 1)
    fold_values(0)
    open_acc(k, pe, A.n)
    for t in range(NT):
        if t + 1 < NT:
            scores(t + 1)
        if t == 0:
            fold_values(1)
        turn(t)
        if t % TB == 0:
            for i in range(len(VW_JOBS)):
                k.drained(pe, (L, "vw", t // TB, i))
        values(t)


def values_done(k, eng, t):
    b, i = divmod(t, TB)
    if i < TB - 1:
        eng.wait_ge(k.values_done, b * (TB - 1) + i + 1)
    else:
        eng.wait_ge(k.acc_filled, 2 * acc_use(6) + b + 1)


def attention64_scalar(k, a, A):
    nc, L = k.nc, A.L

    def folded_keys():
        for h in range(H):
            ps = k.filled(a.eng, (L, "g", h))
            a.drain((L, "g", h), nc.scalar.activation(A.wk[:, :, h, :], ps[:, 0:NK].rearrange("p (b m) -> p b m", b=B),
                                                      ACT.Copy, scale=A.scale))

    def exponentials(t):
        if t >= 2:
            k.filled(a.eng, (L, "pT", t - 2, NBLK // BLK_JOB - 1))
        for g, (h0, h1) in enumerate(GROUPS3):
            a.eng.wait_ge(k.nm_ready, 2 * 2 + t * len(GROUPS3) + g + 1)
            ps = k.filled(a.eng, (L, "s", t, g))
            for h in range(h0, h1):
                ins = nc.scalar.activation(A.p[:, t % 2, h, 0:M], ps[:, (h - h0) * M:(h - h0 + 1) * M], ACT.Exp,
                                           bias=k.nm[:, t, h:h + 1], accum_out=A_sum(k)[:, t % 2, h:h + 1])
                a.did(ins) if h < h1 - 1 else a.drain((L, "s", t, g), ins)

    def turned(t):
        if t >= 2:
            values_done(k, a.eng, t - 2)
        for i in range(NBLK // BLK_JOB):
            ps = k.filled(a.eng, (L, "pT", t, i))
            a.drain((L, "pT", t, i), nc.scalar.activation(
                A.pT[:, t % 2, i * BLK_JOB:(i + 1) * BLK_JOB, :].rearrange("p j q -> p (j q)"), ps[:, :], ACT.Copy))

    for c in range(NPAIR):
        ps = k.filled(a.eng, (L, "k", c))
        a.drain((L, "k", c), nc.scalar.activation(A.kT[:, c, :], ps[:, 0:NK], ACT.Copy))
    folded_keys()
    norm_scalar(k, a, A.n, 0)
    a.eng.wait_ge(k.zeroed, ZEROED3 + 1)
    exponentials(0)
    norm_scalar(k, a, A.n, 1)
    for t in range(NT):
        if t + 1 < NT:
            exponentials(t + 1)
        turned(t)


def A_sum(k):
    return k.den[:, :].rearrange("p (a h) -> p a h", a=2)


def attention64_vector(k, v, A):
    nc, L = k.nc, A.L

    def maxima(t):
        for g, (h0, h1) in enumerate(GROUPS3):
            ps = k.filled(v.eng, (L, "s", t, g))
            v.did(nc.vector.tensor_reduce(k.nm[:, t, h0:h1], ps[:, 0:(h1 - h0) * M].rearrange("p (h m) -> p h m", m=M),
                                          axis=AX.X, op=ALU.max, negate=True), k.nm_ready)

    def probabilities(t):
        for g, (h0, h1) in enumerate(GROUPS3):
            k.drained(v.eng, (L, "s", t, g))
            r = k.rden[:, t % 2, h0:h1]
            v.did(nc.vector.reciprocal(r, A_sum(k)[:, t % 2, h0:h1]))
            v.settle()
            p = A.p[:, t % 2, h0:h1, 0:M]
            v.did(nc.vector.tensor_tensor(p, p, r.unsqueeze(2).to_broadcast([P, h1 - h0, M]), ALU.mult), k.p64_ready)

    def folded_values(b):
        for i, (first, end) in enumerate(VW_JOBS):
            ps = k.filled(v.eng, (L, "vw", b, i))
            v.drain((L, "vw", b, i), nc.vector.tensor_copy(A.vw[:, b, first:end, :].rearrange("p j d -> p (j d)"),
                                                           ps[:, 0:(end - first) * D]))

    v.eng.wait_ge(k.zeroed, ZEROED3 + 2)
    for c in range(NPAIR):
        ps = k.filled(v.eng, (L, "v", c))
        src = ps[:, 0:NK].rearrange("p (b m) -> p b m", b=B)
        v.did(nc.vector.tensor_copy(A.vbd[0:64, c, :, 0, 0:M], src[0:64]))
        v.drain((L, "v", c), nc.vector.tensor_copy(A.vbd[64:P, c, :, 1, 0:M], src[64:P]))
    maxima(0)
    probabilities(0)
    folded_values(0)
    for t in range(NT):
        if t + 1 < NT:
            maxima(t + 1)
        if t == 0:
            folded_values(1)
        if t + 1 < NT:
            probabilities(t + 1)


def done(k, v):
    v.settle()
    v.did(k.nc.vector.tensor_copy(k.flag[:, 2:3], k.flag[:, 0:1]), k.x_ready)


PAIRS = [(0, 0), (0, 1), (0, 2), (1, 0), (1, 1), (2, 0)]
SEC = 16
NROW = SEC * len(PAIRS)
NROWM = NROW + 4
HPAIR = H // 2


class Attention8:

    def __init__(self, k, L, n):
        self.L, self.n = L, n
        self.use = {"L0x": 0, "L2x": 1}[L]
        self.scale = 8.0 ** -0.5
        at = PLACE["L2f"] if L == "L0x" else PLACE["L0x"]
        self.ks = k.cols(at, [H, B, 160], BF16)
        at += B * H * 80
        self.qf = k.cols(at, [N])
        self.pv = k.cols(at, [2, S])
        at += N
        self.qp = k.cols(at, [3, N], BF16)
        at += 3 * N // 2
        self.h = k.cols(at, [2, N]) if L == "L0x" else None
        at = ARENA
        self.qs = k.cols(at, [HPAIR, N], BF16)
        at += HPAIR * N // 2
        self.pt = k.cols(at, [2, HG + 1, S])
        self.vr = k.cols(ARENA + ARENA_SIZE - 2048, [B, NG, P])
        self.vm = k.cols(ARENA + ARENA_SIZE - 1024, [B, H, 32])
        self.kT = k.small[:, 0:B * 160].rearrange("p (b m) -> p b m", b=B)
        self.kp = k.small[:, 320:800].bitcast(BF16).rearrange("p (a m) -> p a m", a=3)
        self.tmp = k.rt[:, :, :].rearrange("p a b -> p (a b)")
        self.o, self.oT = k.xn, k.xnT
        self.zeroed = {0: 1, 1: 4}[self.use]


def stack_keys_sync(k, sp, A):
    sp.wait_ge(k.kparts_ready, A.use + 1)
    sp.dma_start(A.ks[NROW:NROWM, :, :, :].rearrange("p h b m -> p (h b m)"), k.dram["maxrows"]).then_inc(k.k_stacked[A.use], 16)
    for s, (_, part) in enumerate(PAIRS):
        for odd in range(2):
            r = s * SEC + odd * 8
            sp.dma_start(A.ks[r:r + 8, odd::2, :, :].rearrange("d h b m -> d h (b m)"), A.kp[64 * odd:64 * (odd + 1), part, :])\
              .then_inc(k.k_stacked[A.use], 16)


NKEYDMA = 1 + 2 * len(PAIRS)


def stack_queries_sync(k, sp, A):
    for b in range(B):
        cs = slice(b * S, (b + 1) * S)
        sp.wait_ge(k.qparts_ready, B * A.use + b + 1)
        for s, (part, _) in enumerate(PAIRS):
            sp.dma_start(A.qs[s * SEC:(s + 1) * SEC, :, cs], A.qp[:, part, cs]).then_inc(k.q_stacked[A.use][b], 16)


def stack_maxima_sync(k, sp, A):
    for b in range(B):
        cs = slice(b * S, (b + 1) * S)
        k.drained(sp, (A.L, "nmT", b))
        sp.dma_start(A.qs[NROW:NROWM, :, cs], k.nmT[0:2 * H, cs]).then_inc(k.m_stacked[A.use][b], 16)


def attention8_prep_pool(k, g, A):
    nc = k.nc
    if A.use:
        g.eng.wait_ge(k.acc_filled, 2 * acc_use(2) + 2)
    g.did(nc.gpsimd.memset(A.vr[:, :, :], 0.0))
    if A.use == 0:
        g.did(nc.gpsimd.memset(k.mpad[:, :, :], 0.0))
    g.did(nc.gpsimd.memset(A.vm[:, :, :, :], 0.0))
    g.settle()
    g.did(nc.gpsimd.memset(A.vm[:, :, :, 8:9], 1.0), k.zeroed)


def attention8_prep_tensor(k, pe, A):
    nc, L = k.nc, A.L
    pe.wait_ge(k.loaded["ctx"], 16)
    pe.wait_ge(k.loaded[L], 16)
    ctxT = k.w("ctx", "ctxT")
    ps = k.open(pe, (L, "k"))
    k.fill((L, "k"), nc.tensor.matmul(ps[:, 0:NK], k.w(L, "Wk"), ctxT, start=True, stop=True))
    for b in range(B):
        for kind, keys in (("v", ctxT[:, b * M:b * M + P]), ("vr", k.w("ctx", "ctx_rem")[:, b * P:(b + 1) * P])):
            ps = k.open(pe, (L, kind, b))
            k.fill((L, kind, b), nc.tensor.matmul(ps[:, 0:P], keys, k.w(L, "Wv"), start=True, stop=True))


def attention8_keys_vector(k, v, A):
    nc, L = k.nc, A.L
    if A.use:
        v.did(nc.vector.memset(A.ks[:, :, :, :], 0.0))
    v.eng.wait_ge(k.loaded[L], 16)
    v.did(nc.vector.tensor_scalar(k.bqs[:, 0:1], k.w(L, "bq"), A.scale, None, ALU.mult), k.bias_ready)
    ps = k.filled(v.eng, (L, "k"))
    v.did(nc.vector.memset(A.kT[:, :, M:160], 0.0))
    v.drain((L, "k"), nc.vector.tensor_scalar(A.kT[:, :, 0:M], ps[:, 0:NK].rearrange("p (b m) -> p b m", b=B), k.w(L, "bk"), None, ALU.add))
    v.settle()
    three_parts(k, v, k.small[:, 0:320], [A.kp[:, i, :] for i in range(3)], [A.tmp[:, 0:320]], k.kparts_ready)


def attention8_values_vector(k, v, A):
    nc, L = k.nc, A.L
    v.eng.wait_ge(k.zeroed, A.zeroed)
    v.eng.wait_ge(k.loaded["rows"], 16)
    rem = k.w("const", "rem_rows")
    bv = k.w("rows", L[:2] + "_bv")
    for b in range(B):
        ps = k.filled(v.eng, (L, "v", b))
        v.drain((L, "v", b), nc.vector.tensor_tensor(A.vm[:, b, :, 0:8], ps[:, 0:P].rearrange("p (h d) -> p h d", h=H),
                                                     bv.rearrange("p (h d) -> p h d", h=H), ALU.add))
        ps = k.filled(v.eng, (L, "vr", b))
        full = A.tmp[:, 320 + b * P:320 + (b + 1) * P]
        v.drain((L, "vr", b), nc.vector.tensor_tensor(full, ps[:, 0:P], bv, ALU.add))
        v.settle()
        for j in range(HG):
            dst = A.vr[:, b, :, 32 * j:32 * (j + 1)]
            src = full.rearrange("p (g j d) -> p g j d", g=NG, j=HG)[:, :, j, :]
            v.did(nc.vector.tensor_scalar(dst[:, :, 0:8], src, rem[:, j:j + 1], None, ALU.mult))
            v.did(nc.vector.tensor_copy(dst[:, :, 8:9], bc(rem[:, j:j + 1], 1, [NG, 1])))
    v.settle()
    v.did(nc.vector.tensor_copy(k.flag[:, 0:1], rem[:, 0:1]), k.v_ready)


def attention8_tensor(k, pe, A):
    nc, L = k.nc, A.L
    for b in range(B):
        norm_tensor(k, pe, A.n, b)
        wait_xnT(k, pe, A.n, b)
        ps = k.open(pe, (L, "q", b))
        k.fill((L, "q", b), nc.tensor.matmul(ps[:, :], k.w(L, "Wq"), k.xnT[:, b * S:(b + 1) * S], start=True, stop=True))
    pe.wait_ge(k.k_stacked[A.use], 16 * NKEYDMA)

    def scores(t):
        b = t // TB
        pe.wait_ge(k.q_stacked[A.use][b], 16 * len(PAIRS))
        for p in range(HPAIR):
            ps = k.open(pe, (L, "s", t, p))
            k.fill((L, "s", t, p), nc.tensor.matmul(ps[:, 0:2 * M], A.qs[0:NROW, p, t * P:(t + 1) * P],
                                                    A.ks[0:NROW, 2 * p:2 * p + 2, b, 0:M], start=True, stop=True))

    def minus_max(b):
        ps = k.open(pe, (L, "nmT", b))
        if A.use == 0:
            pe.wait_ge(k.loaded["sel"], 16)
        pe.wait_ge(k.nm_ready, 2 * A.use + b + 1)
        view = ps[:, :].bitcast(BF16)
        for i in range(TB):
            last = nc.tensor.transpose(view[:, i * P:(i + 1) * P], k.mpad[:, b * TB + i, :], k.w("sel", "ident"))
        k.fill((L, "nmT", b), last)

    def scores_T(b, g):
        pe.wait_ge(k.m_stacked[A.use][b], 16)
        queries = slice(b * S, (b + 1) * S)
        for j in range(HG):
            h = HG * g + j
            ps = k.open(pe, (L, "st", b, g, j))
            k.fill((L, "st", b, g, j), nc.tensor.matmul(ps[:, :], A.ks[0:NROWM, h, b, 0:P], A.qs[0:NROWM, h // 2, queries],
                                                        start=True, stop=True))
        ps = k.open(pe, (L, "sr", b, g))
        for j in range(HG):
            h = HG * g + j
            last = nc.tensor.matmul(ps[HP * j:HP * (j + 1), :], A.ks[0:NROWM, h, b, P:160], A.qs[0:NROWM, h // 2, queries],
                                    start=True, stop=True)
        k.fill((L, "sr", b, g), last)

    def values(n):
        b, g = steps[n]
        for j in range(HG):
            k.drained(pe, (L, "st", b, g, j))
        k.drained(pe, (L, "sr", b, g))
        pt = A.pt[:, n % 2]
        ps = k.open(pe, (L, "pv", b, g))
        nc.tensor.matmul(ps[:, :], A.vr[:, b, g, :], pt[:, HG, :], start=True, stop=False, skip_group_check=True)
        for j in range(HG):
            last = nc.tensor.matmul(ps[HP * j:HP * (j + 1), :], A.vm[:, b, HG * g + j, :], pt[:, j, :], start=False, stop=True,
                                    skip_group_check=True)
        k.fill((L, "pv", b, g), last)

    def turn(n):
        b, g = steps[n]
        k.drained(pe, (L, "pv", b, g))
        ps = k.open(pe, (L, "ot", b, g))
        for i in range(TB):
            last = nc.tensor.transpose(ps[:, i * P:(i + 1) * P], A.pv[:, n % 2, i * P:(i + 1) * P], k.w("const", "ident"))
        k.fill((L, "ot", b, g), last)

    for t in range(TB):
        scores(t)
    minus_max(0)
    for t in range(TB, NT):
        scores(t)
    minus_max(1)
    pe.wait_ge(k.v_ready, A.use + 1)
    steps = [(b, g) for b in range(B) for g in range(NG)]
    scores_T(*steps[0])
    for n in range(len(steps)):
        if n + 1 < len(steps):
            scores_T(*steps[n + 1])
        if n:
            turn(n - 1)
            if L == "L0x":
                l1x_prep_tensor(k, pe, n - 1)
        values(n)
    turn(len(steps) - 1)
    for b in range(B):
        pe.wait_ge(k.o_ready, B * A.use + b + 1)
        ps = k.open(pe, (L, "oT", b))
        for i in range(TB):
            last = nc.tensor.transpose(ps[:, i * P:(i + 1) * P], A.o[:, b * TB + i, :], k.w("const", "ident"))
        k.fill((L, "oT", b), last)
    open_acc(k, pe, A.n)
    if L == "L0x":
        for b in range(B):
            k.drained(pe, (L, "oT", b))
            for c in range(2):
                ps = k.open(pe, (L, "h", c, b))
                k.fill((L, "h", c, b), nc.tensor.matmul(ps[:, :], k.w(L, "W1")[:, c * P:(c + 1) * P],
                                                        A.oT[:, b * S:(b + 1) * S], start=True, stop=True))
    for b in range(B):
        if L == "L0x":
            for c in range(2):
                k.drained(pe, (L, "h", c, b))
        else:
            k.drained(pe, (L, "oT", b))
        for i in range(TB):
            t = b * TB + i
            out = k.acc[b][:, i * D:(i + 1) * D]
            if L == "L0x":
                for c in range(2):
                    last = nc.tensor.matmul(out, A.h[:, c, t * P:(t + 1) * P], k.w(L, "W2")[:, c * D:(c + 1) * D],
                                            start=(c == 0), stop=(c == 1))
            else:
                last = nc.tensor.matmul(out, A.oT[:, t * P:(t + 1) * P], k.w(L, "Wo"), start=True, stop=True)
        last.then_inc(k.acc_filled, 1)


def attention8_scalar(k, a, A):
    nc, L = k.nc, A.L
    a.eng.wait_ge(k.bias_ready, {0: 1, 1: 3}[A.use])
    for b in range(B):
        norm_scalar(k, a, A.n, b)
        ps = k.filled(a.eng, (L, "q", b))
        cs = slice(b * S, (b + 1) * S)
        a.did(nc.scalar.activation(A.qp[:, 0, cs], ps[:, :], ACT.Identity, bias=k.bqs[:, 0:1], scale=A.scale))
        a.drain((L, "q", b), nc.scalar.activation(A.qf[:, cs], ps[:, :], ACT.Identity, bias=k.bqs[:, 0:1], scale=A.scale))
    for b in range(B):
        ps = k.filled(a.eng, (L, "nmT", b))
        a.drain((L, "nmT", b), nc.scalar.activation(k.nmT[:, b * S:(b + 1) * S], ps[:, :].bitcast(BF16)[:, 0:S], ACT.Copy))
    for b in range(B):
        for g in range(NG):
            step = b * NG + g
            if step >= 2:
                k.filled(a.eng, (L, "pv", *divmod(step - 2, NG)))
            for j in range(HG + 1):
                label = (L, "st", b, g, j) if j < HG else (L, "sr", b, g)
                ps = k.filled(a.eng, label)
                a.drain(label, nc.scalar.activation(A.pt[:, step % 2, j, :], ps[:, :], ACT.Exp))
    for b in range(B):
        ps = k.filled(a.eng, (L, "oT", b))
        a.drain((L, "oT", b), nc.scalar.activation(A.oT[:, b * S:(b + 1) * S], ps[:, :], ACT.Copy))
        if L == "L0x":
            for c in range(2):
                ps = k.filled(a.eng, (L, "h", c, b))
                a.drain((L, "h", c, b), nc.scalar.activation(A.h[:, c, b * S:(b + 1) * S], ps[:, :], ACT.Relu,
                                                             bias=k.w(L, "b1")[:, c:c + 1]))


def attention8_vector(k, v, A):
    nc, L = k.nc, A.L
    for b in range(B):
        cs = slice(b * S, (b + 1) * S)
        k.drained(v.eng, (L, "q", b))
        v.did(nc.vector.tensor_tensor(A.qf[:, cs], A.qf[:, cs], A.qp[:, 0, cs], ALU.subtract))
        v.settle()
        v.did(nc.vector.tensor_copy(A.qp[:, 1, cs], A.qf[:, cs]))
        v.settle()
        v.did(nc.vector.tensor_tensor(A.qp[:, 2, cs], A.qf[:, cs], A.qp[:, 1, cs], ALU.subtract), k.qparts_ready)
    for b in range(B):
        for t in range(b * TB, (b + 1) * TB):
            for p in range(HPAIR):
                ps = k.filled(v.eng, (L, "s", t, p))
                v.drain((L, "s", t, p), nc.vector.tensor_reduce(
                    k.nm[:, t, 2 * p:2 * p + 2], ps[:, 0:2 * M].rearrange("p (h m) -> p h m", h=2),
                    axis=AX.X, op=ALU.max, negate=True))
        v.settle()
        ts = slice(b * TB, (b + 1) * TB)
        by_parity = k.nm[:, ts, :].rearrange("p t (h odd) -> p t odd h", odd=2)
        high, low = (k.mpad[:, ts, i * H:(i + 1) * H].rearrange("p t (odd h) -> p t odd h", odd=2) for i in range(2))
        v.did(nc.vector.tensor_copy(high, by_parity))
        v.settle()
        v.did(nc.vector.tensor_tensor(low, by_parity, high, ALU.subtract), k.nm_ready)

    def normalise(n):
        b, g = divmod(n, NG)
        ps = k.filled(v.eng, (L, "ot", b, g))
        src = ps[:, :].rearrange("p (i j d) -> p i j d", i=TB, j=HG)
        r = k.den[:, 0:TB * HG].rearrange("p (i j) -> p i j", i=TB)
        v.settle()
        v.did(nc.vector.reciprocal(r, src[:, :, :, 8]))
        v.settle()
        dst = A.o[:, b * TB:(b + 1) * TB, g * 32:(g + 1) * 32].rearrange("p i (j d) -> p i j d", j=HG)
        v.drain((L, "ot", b, g), nc.vector.tensor_tensor(dst, src[:, :, :, 0:8], r.unsqueeze(3).to_broadcast([P, TB, HG, 8]), ALU.mult))
        if g == NG - 1:
            v.settle()
            v.did(nc.vector.tensor_copy(k.flag[:, 1:2], k.flag[:, 0:1]), k.o_ready)

    for n in range(B * NG):
        ps = k.filled(v.eng, (L, "pv", *divmod(n, NG)))
        if n >= 2:
            k.filled(v.eng, (L, "ot", *divmod(n - 2, NG)))
        v.drain((L, "pv", *divmod(n, NG)), nc.vector.tensor_copy(A.pv[:, n % 2, :], ps[:, :]))
        if n:
            normalise(n - 1)
        if L == "L0x" and n < B * NG - 1:
            l1x_prep_vector(k, v, n)
    normalise(B * NG - 1)
    if L == "L0x":
        l1x_prep_vector(k, v, B * NG - 1)


class Moe:

    def __init__(self, k, L, n, width, chunks, routed):
        self.L, self.n, self.width, self.chunks, self.routed = L, n, width, chunks, routed
        self.topk = 4 if L == "L0f" else 2
        self.use = 0 if L == "L0f" else 1
        self.h = k.cols(ARENA, [chunks, N])
        self.sg = k.small[:, 0:1024].rearrange("p (a b) -> p a b", a=2)

    def part(self, k, kind, c):
        w = D if kind == "down" else self.width
        if self.L == "L0f" and c >= self.routed:
            kind, c = {"gate": "sgate", "up": "sup", "down": "sdown"}[kind], c - self.routed
        return k.w(self.L, kind)[:, c * w:(c + 1) * w]


ROUTERS = ["L0f", "L1f", "L2f", "L3f"]


def logits_tensor(k, pe, L, n, experts=E8):
    ps = k.open(pe, (L, "logits"))
    pe.wait_ge(k.loaded[L], 16)
    for t in range(NT):
        wait_xnT(k, pe, n, t // TB)
        last = k.nc.tensor.matmul(ps[:, t * experts:(t + 1) * experts], k.xnT[:, t * P:(t + 1) * P], k.w(L, "Wr"),
                                  start=True, stop=True)
    k.fill((L, "logits"), last)


def softmax_scalar(k, a, L, experts=E8):
    a.eng.wait_ge(k.l_ready, ROUTERS.index(L) + 1)
    w = NT * experts
    a.did(k.nc.scalar.activation(k.rt[:, 0, 0:w], k.rt[:, 0, 0:w], ACT.Exp), k.exp_ready)


def softmax_vector(k, v, L, experts=E8):
    nc = k.nc
    w = NT * experts
    ps = k.filled(v.eng, (L, "logits"))
    three = lambda ap: ap.rearrange("p (t e) -> p t e", t=NT)
    src = three(ps[:, 0:w])
    ex = three(k.rt[:, 0, 0:w])
    v.did(nc.vector.tensor_reduce(k.m8[:, :], src, axis=AX.X, op=ALU.max, negate=True))
    v.settle()
    v.drain((L, "logits"), nc.vector.tensor_tensor(ex, src, bc(k.m8[:, :], 2, [NT, experts]), ALU.add))
    v.settle()
    v.did(nc.vector.tensor_copy(k.flag[:, 3:4], k.flag[:, 0:1]), k.l_ready)
    v.eng.wait_ge(k.exp_ready, ROUTERS.index(L) + 1)
    v.did(nc.vector.tensor_reduce(k.s8[:, :], ex, axis=AX.X, op=ALU.add))
    v.settle()
    v.did(nc.vector.reciprocal(k.r8[:, :], k.s8[:, :]))
    v.settle()
    v.did(nc.vector.tensor_tensor(three(k.rt[:, 1, 0:w]), ex, bc(k.r8[:, :], 2, [NT, experts]), ALU.mult))
    v.settle()


def rank_vector(k, v, scores):
    nc = k.nc
    s = scores.rearrange("p (t e) -> p t e", t=NT)
    four = lambda ap: ap.rearrange("p (t e f) -> p t e f", t=NT, e=E8)
    other = s.unsqueeze(2).to_broadcast([P, NT, E8, E8])
    own = s.unsqueeze(3).to_broadcast([P, NT, E8, E8])
    gt, eq = four(k.cmp[:, 0, :]), four(k.cmp[:, 1, :])
    v.did(nc.vector.tensor_tensor(gt, other, own, ALU.is_gt))
    v.did(nc.vector.tensor_tensor(eq, other, own, ALU.is_equal))
    v.settle()
    earlier = k.w("const", "earlier").unsqueeze(1).to_broadcast([P, NT, 64])
    flat = lambda ap: ap.rearrange("p (t e) -> p t e", t=NT)
    v.did(nc.vector.tensor_tensor(flat(k.cmp[:, 1, :]), flat(k.cmp[:, 1, :]), earlier, ALU.mult))
    v.settle()
    v.did(nc.vector.tensor_tensor(k.cmp[:, 0, :], k.cmp[:, 0, :], k.cmp[:, 1, :], ALU.add))
    v.settle()
    v.did(nc.vector.tensor_reduce(k.rt[:, 3, 0:64], k.cmp[:, 0, :].rearrange("p (c f) -> p c f", f=E8), axis=AX.X, op=ALU.add))
    v.settle()


def three_parts(k, v, src, dst, tmp, last_sem):
    nc = k.nc
    v.did(nc.vector.tensor_copy(dst[0], src))
    v.settle()
    v.did(nc.vector.tensor_tensor(tmp[0], src, dst[0], ALU.subtract))
    v.settle()
    v.did(nc.vector.tensor_copy(dst[1], tmp[0]))
    v.settle()
    v.did(nc.vector.tensor_tensor(dst[2], tmp[0], dst[1], ALU.subtract), last_sem)


def moe_vector(k, v, A):
    nc, L = k.nc, A.L
    order = moe_order(A)
    def hidden(c, b):
        r = slice(0, A.width)
        cs = slice(b * S, (b + 1) * S)
        turn = order.index((c, b))
        k.drained(v.eng, (L, "g", c, b))
        ps = k.filled(v.eng, (L, "u", c, b))
        v.drain((L, "u", c, b), nc.vector.tensor_tensor(A.h[r, c, cs], A.sg[r, turn % 2, :], ps[r, :], ALU.mult))
        if c < A.routed:
            v.settle()
            ps = k.filled(v.eng, (L, "w", c, b))
            v.drain((L, "w", c, b), nc.vector.tensor_tensor(A.h[r, c, cs], A.h[r, c, cs], ps[r, :], ALU.mult))

    shared = A.chunks - A.routed
    for turn in range(shared):
        hidden(*order[turn])
    softmax_vector(k, v, L)
    hidden(*order[shared])
    probs, w = k.rt[:, 1, 0:64], k.rt[:, 2, 0:64]
    scores = probs
    if L == "L0f":
        scores = k.rt[:, 4, 0:64]
        v.did(nc.vector.tensor_scalar(scores, probs, k.w("rows", "rb"), None, ALU.add))
        v.settle()
    rank_vector(k, v, scores)
    for turn in range(shared + 1, 2 * shared):
        hidden(*order[turn])
    v.settle()
    v.did(nc.vector.scalar_tensor_tensor(out=w, in0=k.rt[:, 3, 0:64], scalar=float(A.topk), in1=probs,
                                         op0=ALU.is_lt, op1=ALU.mult))
    v.settle()
    three = lambda ap: ap.rearrange("p (t e) -> p t e", t=NT)
    if L == "L0f":
        v.did(nc.vector.tensor_reduce(k.s8[:, :], three(w), axis=AX.X, op=ALU.add))
        v.settle()
        v.did(nc.vector.tensor_scalar(k.s8[:, :], k.s8[:, :], 1e-20, None, ALU.add))
        v.settle()
        v.did(nc.vector.reciprocal(k.r8[:, :], k.s8[:, :]))
        v.settle()
        v.did(nc.vector.tensor_tensor(three(w), three(w), bc(k.r8[:, :], 2, [NT, E8]), ALU.mult))
        v.settle()
    parts = [k.mpad[:, :, 8 * i:8 * (i + 1)] for i in range(3)]
    three_parts(k, v, three(w), parts, [three(k.rt[:, 3, 0:64])], k.w_ready)

    for turn in range(2 * shared, len(order)):
        hidden(*order[turn])
        if L == "L0f" and turn + 2 in L1X_PREP_TURNS and L1X_PREP_TURNS[turn + 2] >= B * NG:
            l1x_prep_vector(k, v, L1X_PREP_TURNS[turn + 2])


def moe_order(A):
    return [(c, b) for b in range(B) for c in range(A.routed, A.chunks)] + [(c, b) for c in range(A.routed) for b in range(B)]


def moe_scalar(k, a, A):
    nc, L = k.nc, A.L
    order = moe_order(A)
    per_batch = A.chunks - A.routed
    shared = 2 * (A.chunks - A.routed)
    for turn, (c, b) in enumerate(order):
        if L == "L0f" and turn == max(L1X_PREP_TURNS):
            l1x_prep_scalar(k, a)
        if turn in (0, per_batch):
            norm_scalar(k, a, A.n, turn // per_batch)
        if turn == per_batch:
            softmax_scalar(k, a, L)
        if turn == shared:
            for bb in range(B):
                ps = k.filled(a.eng, (L, "wT", bb))
                a.drain((L, "wT", bb), nc.scalar.activation(k.nmT[:, bb * S:(bb + 1) * S], ps[:, :].bitcast(BF16)[:, 0:S], ACT.Copy))
        if turn >= 2:
            k.drained(a.eng, (L, "u", *order[turn - 2]))
        ps = k.filled(a.eng, (L, "g", c, b))
        a.drain((L, "g", c, b), nc.scalar.activation(A.sg[0:A.width, turn % 2, :], ps[0:A.width, :], ACT.Silu))


def moe_tensor(k, pe, A):
    nc, L = k.nc, A.L
    order = moe_order(A)
    per_batch = A.chunks - A.routed
    shared = 2 * (A.chunks - A.routed)
    pe.wait_ge(k.loaded[L], 16)
    for turn, (c, b) in enumerate(order):
        if L == "L0f" and turn in L1X_PREP_TURNS:
            l1x_prep_tensor(k, pe, L1X_PREP_TURNS[turn])
        if turn in (0, per_batch):
            norm_tensor(k, pe, A.n, turn // per_batch)
            wait_xnT(k, pe, A.n, turn // per_batch)
        if turn == per_batch:
            logits_tensor(k, pe, L, A.n)
        if turn == shared:
            for bb in range(B):
                ps = k.open(pe, (L, "wT", bb))
                pe.wait_ge(k.w_ready, ROUTERS.index(L) + 1)
                for i in range(TB):
                    last = nc.tensor.transpose(ps[:, :].bitcast(BF16)[:, i * P:(i + 1) * P], k.mpad[:, bb * TB + i, :],
                                               k.w("sel", "ident"))
                k.fill((L, "wT", bb), last)
        cs = slice(b * S, (b + 1) * S)
        for kind, name in (("g", "gate"), ("u", "up")):
            ps = k.open(pe, (L, kind, c, b))
            k.fill((L, kind, c, b), nc.tensor.matmul(ps[0:A.width, :], A.part(k, name, c), k.xnT[:, cs], start=True, stop=True))
        if c < A.routed:
            ps = k.open(pe, (L, "w", c, b))
            k.drained(pe, (L, "wT", b))
            k.fill((L, "w", c, b), nc.tensor.matmul(ps[0:A.width, :], k.w("sel", L)[:, c * A.width:(c + 1) * A.width],
                                                    k.nmT[:, cs], start=True, stop=True))
    open_acc(k, pe, A.n)
    for b in range(B):
        for c in range(A.chunks):
            k.drained(pe, (L, "w" if c < A.routed else "u", c, b))
        for i in range(TB):
            t = b * TB + i
            for c in range(A.chunks):
                last = nc.tensor.matmul(k.acc[b][:, i * D:(i + 1) * D], A.h[0:A.width, c, t * P:(t + 1) * P],
                                        A.part(k, "down", c)[0:A.width], start=(c == 0), stop=(c == A.chunks - 1))
        last.then_inc(k.acc_filled, 1)


WEIGHTS1 = [("d2v", 1, 128 * 96), ("img", 1, 128 * 128), ("att0", 1, 128 * 128), ("att1", 1, 128 * 128),
            ("txt", 1, 128 * 128), ("f1", 8, 512 * 256), ("f2", 4, 128 * 512)]


class L1x:

    def __init__(self, k):
        at = PLACE["L2f"] + 7168
        self.wq = k.cols(at, [17 * P], BF16)
        at += 17 * P // 2
        self.kT = k.cols(at, [2, B, 256])
        at += 1024
        self.kv = k.cols(at, [2, B, 2, P])
        at += 1024
        self.prep = k.cols(at, [2, 512])
        at += 1024
        self.ctxq = k.cols(at, [NK], BF16)
        self.hq = k.cols(PLACE["L0x"], [4, N], BF16)
        at = ARENA
        self.tmp = k.cols(at, [2, N])
        at += 2 * N
        self.xq = k.cols(at, [N], BF16)
        at += N // 2
        self.fused = k.cols(at, [N])
        at += N
        self.p = k.cols(at, [NT, 256])
        self.pT = k.cols(at + 2048, [B, 2, S])
        self.h = k.cols(at, [4, N])
        self.f8 = k.l1s

    def weight(self, name):
        at = 0
        for n, blocks, _ in WEIGHTS1:
            if n == name:
                return self.wq[:, at:at + blocks * P]
            at += blocks * P


def amax_vector(k, v, name, src):
    amax_rows(k, v, src)
    amax_row(k, v, name)
    amax_scale(k, v, name)


def amax_rows(k, v, src):
    nc = k.nc
    if src is not None:
        v.did(nc.vector.tensor_reduce(k.am[:, 0:1], src, axis=AX.X, op=ALU.max, apply_absolute_value=True))
    v.settle()
    v.did(nc.vector.tensor_copy(k.am[:, 4:5], k.am[:, 0:1]), k.am_ready)


def amax_row(k, v, name):
    ps = k.filled(v.eng, ("L1x", "amT", name))
    v.drain(("L1x", "amT", name), k.nc.vector.tensor_reduce(k.m1[0:1, 0:1], ps[0:1, 0:P], axis=AX.X, op=ALU.max))


def amax_scale(k, v, name):
    nc, i = k.nc, AMAX.index(name)
    ps = k.filled(v.eng, ("L1x", "amB", name))
    v.drain(("L1x", "amB", name), nc.vector.tensor_scalar(k.sc[:, 2 * i:2 * i + 1], ps[:, 0:1], 1e-8, 1.0 / 127.0, ALU.max, ALU.mult))
    v.settle()
    v.did(nc.vector.reciprocal(k.sc[:, 2 * i + 1:2 * i + 2], k.sc[:, 2 * i:2 * i + 1]))
    v.settle()


def amax_turn(k, pe, name):
    ps = k.open(pe, ("L1x", "amT", name))
    pe.wait_ge(k.am_ready, AMAX.index(name) + 1)
    k.fill(("L1x", "amT", name), k.nc.tensor.transpose(ps[0:1, 0:P], k.am[:, 4:5], k.w("const", "ident")))


def amax_spread(k, pe, name):
    ps = k.open(pe, ("L1x", "amB", name))
    k.drained(pe, ("L1x", "amT", name))
    k.fill(("L1x", "amB", name), k.nc.tensor.matmul(ps[:, 0:1], k.w("const", "ones")[0:1, :], k.m1[0:1, 0:1], start=True, stop=True))


def amax_tensor(k, pe, name):
    amax_turn(k, pe, name)
    amax_spread(k, pe, name)


def quantise_vector(k, v, name, src, dst, tmp, sem=None):
    nc, i = k.nc, AMAX.index(name)
    v.did(nc.vector.tensor_scalar(tmp, src, k.sc[:, 2 * i + 1:2 * i + 2], MAGIC, ALU.mult, ALU.add))
    v.settle()
    v.did(nc.vector.tensor_scalar(dst, tmp, MAGIC, 127.0, ALU.subtract, ALU.min), sem)


def scale_vector(k, v, weight, name):
    w = [n for n, _, _ in WEIGHTS1].index(weight)
    i = AMAX.index(name)
    v.did(k.nc.vector.tensor_tensor(k.comb[:, w:w + 1], k.ws[:, w:w + 1], k.sc[:, 2 * i:2 * i + 1], ALU.mult))
    v.settle()
    return k.comb[:, w:w + 1]


def l1x_keys_pool(k, g):
    g.did(k.nc.gpsimd.memset(L1x(k).kT[:, :, :, M:256], 0.0), k.zeroed)


def l1x_pool(k, g):
    g.eng.wait_ge(k.x_ready, 2)
    g.did(k.nc.gpsimd.memset(L1x(k).p[:, :, M:256], 0.0), k.zeroed)


def ternary_vector(k, v, names):
    nc, T = k.nc, L1x(k)
    for turn, name in enumerate(names):
        i, blocks = next((i, blocks) for i, (n, blocks, _) in enumerate(WEIGHTS1) if n == name)
        below = T.prep[:, turn % 2, 0:blocks * P // 2].bitcast(BF16)
        v.settle()
        v.did(nc.vector.tensor_scalar(below, k.w("L1x", name), k.thr[:, 8 + i:9 + i], None, ALU.is_lt))
        v.settle()
        v.did(nc.vector.scalar_tensor_tensor(out=T.weight(name), in0=k.w("L1x", name), scalar=k.thr[:, i:i + 1],
                                             in1=below, op0=ALU.is_gt, op1=ALU.subtract))
    v.settle()


def l1x_prep_vector(k, v, step):
    nc, T = k.nc, L1x(k)
    name, turn = L1X_PREP[step]
    quantised, act = T.prep[:, 0, 0:NK], T.prep[:, 1, 0:NK]
    v.settle()
    if name == "wsum":
        v.eng.wait_ge(k.loaded["L1x"], 16)
        for i, (weight, _, _) in enumerate(WEIGHTS1):
            v.did(nc.vector.tensor_reduce(k.wabs[:, i:i + 1], k.w("L1x", weight), axis=AX.X, op=ALU.add, apply_absolute_value=True),
                  k.q_ready if i == 6 else None)
    elif (name, turn) == ("ctx", "amT"):
        ps = k.filled(v.eng, ("L1x", "wsum"))
        for a, b, count in ((0, 1, 128 * 96), (1, 5, 128 * 128), (5, 6, 512 * 256), (6, 7, 128 * 512)):
            ins = nc.vector.tensor_scalar(k.ws[:, a:b], ps[:, a:b], 1.0 / count, 1e-5, ALU.mult, ALU.max)
            v.did(ins) if b < 7 else v.drain(("L1x", "wsum"), ins)
        v.settle()
        v.did(nc.vector.tensor_scalar(k.thr[:, 0:7], k.ws[:, 0:7], 0.5, None, ALU.mult))
        v.did(nc.vector.tensor_scalar(k.thr[:, 8:15], k.ws[:, 0:7], -0.5, None, ALU.mult))
        amax_rows(k, v, k.w("ctx", "ctxT"))
        ternary_vector(k, v, ("d2v", "img"))
    elif turn == "amT":
        weight, source = {"vis": ("d2v", "ctx"), "img": ("img", "vis")}[name]
        s = scale_vector(k, v, weight, source)
        ps = k.filled(v.eng, ("L1x", name))
        v.drain(("L1x", name), nc.vector.tensor_scalar(act, ps[:, 0:NK], s, k.w("L1x", "b_" + weight), ALU.mult, ALU.add))
        v.settle()
        amax_rows(k, v, act)
        if name == "img":
            v.did(nc.vector.tensor_reduce(k.avg[:, 0:2], act.rearrange("p (b m) -> p b m", b=B), axis=AX.X, op=ALU.add))
            v.settle()
            v.did(nc.vector.tensor_scalar(k.avg[:, 0:2], k.avg[:, 0:2], 1.0 / M, None, ALU.mult))
    elif turn == "amB":
        amax_row(k, v, name)
    elif name == "kvT":
        v.eng.wait_ge(k.zeroed, 2)
        for r in range(2):
            s = scale_vector(k, v, f"att{r}", "img")
            ps = k.filled(v.eng, ("L1x", "kv", r))
            v.drain(("L1x", "kv", r), nc.vector.tensor_scalar(
                T.kT[:, r, :, 0:M], ps[:, 0:NK].rearrange("p (b m) -> p b m", b=B), s, k.w("L1x", f"b_att{r}"), ALU.mult, ALU.add))
        ternary_vector(k, v, ("f2",))
    else:
        source = {"vis": "ctx", "img": "vis", "kv": "img"}[name]
        amax_scale(k, v, source)
        quantise_vector(k, v, source, k.w("ctx", "ctxT") if source == "ctx" else act, T.ctxq, quantised, k.q_ready)
        ternary_vector(k, v, {"vis": ("att0", "att1"), "img": ("txt",), "kv": ("f1",)}[name])


def l1x_prep_tensor(k, pe, step):
    nc, T = k.nc, L1x(k)
    name, turn = L1X_PREP[step]
    if turn == "amT":
        amax_turn(k, pe, name)
    elif turn == "amB":
        amax_spread(k, pe, name)
    elif name == "wsum":
        ps = k.open(pe, ("L1x", "wsum"))
        pe.wait_ge(k.q_ready, 1)
        k.fill(("L1x", "wsum"), nc.tensor.matmul(ps[:, 0:7], k.w("const", "ones"), k.wabs[:, 0:7], start=True, stop=True))
    elif name == "kv":
        for r in range(2):
            ps = k.open(pe, ("L1x", "kv", r))
            pe.wait_ge(k.q_ready, 4)
            k.fill(("L1x", "kv", r), nc.tensor.matmul(ps[:, 0:NK], T.weight(f"att{r}"), T.ctxq, start=True, stop=True))
    elif name == "kvT":
        for r in range(2):
            for b in range(B):
                k.drained(pe, ("L1x", "kv", r))
                ps = k.open(pe, ("L1x", "kvT", r, b))
                for half in range(2):
                    last = nc.tensor.transpose(ps[:, half * P:(half + 1) * P], T.kT[:, r, b, half * P:(half + 1) * P],
                                               k.w("const", "ident"))
                k.fill(("L1x", "kvT", r, b), last)
    else:
        ps = k.open(pe, ("L1x", name))
        pe.wait_ge(k.q_ready, {"vis": 2, "img": 3}[name])
        k.fill(("L1x", name), nc.tensor.matmul(ps[:, 0:NK], T.weight({"vis": "d2v", "img": "img"}[name]), T.ctxq,
                                               start=True, stop=True))


INV_SQRT = float(D) ** -0.5


def l1x_vector(k, v):
    nc, T = k.nc, L1x(k)
    for b in range(B):
        wait_xnT(k, v.eng, 2, b)
    v.eng.wait_ge(k.zeroed, 3)
    amax_vector(k, v, "x", k.xnT[:, :])
    quantise_vector(k, v, "x", k.xnT[:, :], T.xq, T.tmp[:, 0, :], k.q_ready)
    s = scale_vector(k, v, "txt", "x")
    for b in range(B):
        ps = k.filled(v.eng, ("L1x", "txt", b))
        v.drain(("L1x", "txt", b), nc.vector.tensor_scalar(T.fused[:, b * S:(b + 1) * S], ps[:, :], s, k.w("L1x", "b_txt"), ALU.mult, ALU.add))
    for r in range(2):
        for t in range(0, NT, 2):
            ps = k.filled(v.eng, ("L1x", "s", r, t))
            v.did(nc.vector.tensor_reduce(k.am[:, 2:4], ps[:, 0:2 * M].rearrange("p (i m) -> p i m", i=2), axis=AX.X, op=ALU.max))
            v.settle()
            v.did(nc.vector.tensor_scalar(k.l1s[:, 0, t:t + 2], k.am[:, 2:4], -INV_SQRT, None, ALU.mult), k.l1_bias)
            v.settle()
        for t in range(0, NT, 2):
            k.drained(v.eng, ("L1x", "s", r, t))
            v.did(nc.vector.reciprocal(k.l1s[:, 2, t:t + 2], k.l1s[:, 1, t:t + 2]))
            v.settle()
            for i in range(t, t + 2):
                v.did(nc.vector.tensor_scalar(T.p[:, i, 0:M], T.p[:, i, 0:M], k.l1s[:, 2, i:i + 1], 0.1, ALU.mult, ALU.mult), k.p_norm)
        for b in range(B):
            ps = k.filled(v.eng, ("L1x", "o", r, b))
            cs = slice(b * S, (b + 1) * S)
            v.drain(("L1x", "o", r, b), nc.vector.tensor_tensor(T.fused[:, cs], T.fused[:, cs], ps[:, :], ALU.add))
        v.settle()
    v.did(nc.vector.tensor_reduce(k.am[:, 2:3], T.fused, axis=AX.X, op=ALU.max, apply_absolute_value=True))
    v.did(nc.vector.tensor_reduce(k.am[:, 3:4], k.avg[:, 0:2], axis=AX.X, op=ALU.max, apply_absolute_value=True))
    v.settle()
    v.did(nc.vector.tensor_reduce(k.am[:, 0:1], k.am[:, 2:4], axis=AX.X, op=ALU.max))
    amax_vector(k, v, "cat", None)
    quantise_vector(k, v, "cat", k.avg[:, 0:2], k.avgq[:, 0:2], k.am[:, 2:4])
    v.settle()
    quantise_vector(k, v, "cat", T.fused, T.xq, T.tmp[:, 0, :], k.q_ready)
    scale_vector(k, v, "f1", "cat")
    v.did(nc.vector.tensor_copy(k.flag[:, 3:4], k.flag[:, 0:1]), k.bias_ready)
    for c in range(4):
        for b in range(B):
            k.drained(v.eng, ("L1x", "f1", c, b))
        v.did(nc.vector.tensor_reduce(k.hm[:, c:c + 1], T.h[:, c, :], axis=AX.X, op=ALU.max))
    v.settle()
    amax_vector(k, v, "h", k.hm[:, 0:4])
    for c in range(4):
        if c >= 2:
            v.settle()
        quantise_vector(k, v, "h", T.h[:, c, :], T.hq[:, c, :], T.tmp[:, c % 2, :], k.q_ready)
    s = scale_vector(k, v, "f2", "h")
    v.did(nc.vector.tensor_tensor(k.comb[:, 7:8], s, k.gates[:, 2:3], ALU.mult))
    v.settle()


def l1x_scalar(k, a):
    nc, T = k.nc, L1x(k)
    for r in range(2):
        for t in range(0, NT, 2):
            ps = k.filled(a.eng, ("L1x", "s", r, t))
            a.eng.wait_ge(k.l1_bias, (r * NT + t) // 2 + 1)
            if r:
                k.filled(a.eng, ("L1x", "pT", 0, t // TB, 1))
            for i in range(2):
                ins = nc.scalar.activation(T.p[:, t + i, 0:M], ps[:, i * M:(i + 1) * M], ACT.Exp, bias=k.l1s[:, 0, t + i:t + i + 1],
                                           scale=INV_SQRT, accum_out=k.l1s[:, 1, t + i:t + i + 1])
                a.did(ins) if i == 0 else a.drain(("L1x", "s", r, t), ins)
        for b in range(B):
            if r:
                k.filled(a.eng, ("L1x", "o", 0, b))
            for half in range(2):
                label = ("L1x", "pT", r, b, half)
                ps = k.filled(a.eng, label)
                a.drain(label, nc.scalar.activation(T.pT[:, b, half, :], ps[:, :], ACT.Copy))
    a.eng.wait_ge(k.bias_ready, 2)
    for c in range(4):
        for b in range(B):
            ps = k.filled(a.eng, ("L1x", "f1", c, b))
            a.drain(("L1x", "f1", c, b), nc.scalar.activation(T.h[:, c, b * S:(b + 1) * S], ps[:, :], ACT.Relu,
                                                              bias=k.w("L1x", "b_f1")[:, c:c + 1], scale=k.comb[:, 5:6]))


def l1x_prep_scalar(k, a):
    T = L1x(k)
    for r in range(2):
        for b in range(B):
            ps = k.filled(a.eng, ("L1x", "kvT", r, b))
            a.drain(("L1x", "kvT", r, b), k.nc.scalar.activation(
                T.kv[:, r, b, :, :], ps[:, 0:256].rearrange("p (i d) -> p i d", i=2), ACT.Copy))


def l1x_tensor(k, pe):
    nc, T = k.nc, L1x(k)
    amax_tensor(k, pe, "x")
    pe.wait_ge(k.q_ready, 5)
    for b in range(B):
        ps = k.open(pe, ("L1x", "txt", b))
        k.fill(("L1x", "txt", b), nc.tensor.matmul(ps[:, :], T.weight("txt"), T.xq[:, b * S:(b + 1) * S], start=True, stop=True))
    for r in range(2):
        for t in range(0, NT, 2):
            b = t // TB
            k.drained(pe, ("L1x", "txt", b) if r == 0 else ("L1x", "o", 0, b))
            ps = k.open(pe, ("L1x", "s", r, t))
            for i in range(2):
                last = nc.tensor.matmul(ps[:, i * M:(i + 1) * M], T.fused[:, (t + i) * P:(t + i + 1) * P], T.kT[:, r, b, 0:M], start=True, stop=True)
            k.fill(("L1x", "s", r, t), last)
        for b in range(B):
            for half in range(2):
                ps = k.open(pe, ("L1x", "pT", r, b, half))
                for i in range(TB):
                    t = b * TB + i
                    pe.wait_ge(k.p_norm, r * NT + t + 1)
                    last = nc.tensor.transpose(ps[:, i * P:(i + 1) * P], T.p[:, t, half * P:(half + 1) * P], k.w("const", "ident"))
                k.fill(("L1x", "pT", r, b, half), last)
            ps = k.open(pe, ("L1x", "o", r, b))
            k.drained(pe, ("L1x", "kvT", r, b))
            for half in range(2):
                k.drained(pe, ("L1x", "pT", r, b, half))
                last = nc.tensor.matmul(ps[:, :], T.kv[:, r, b, half, :], T.pT[:, b, half, :], start=(half == 0), stop=(half == 1))
            k.fill(("L1x", "o", r, b), last)
    amax_tensor(k, pe, "cat")
    pe.wait_ge(k.q_ready, 6)
    for c in range(4):
        for b in range(B):
            ps = k.open(pe, ("L1x", "f1", c, b))
            w = T.weight("f1")
            nc.tensor.matmul(ps[:, :], w[:, c * P:(c + 1) * P], T.xq[:, b * S:(b + 1) * S], start=True, stop=False)
            k.fill(("L1x", "f1", c, b), nc.tensor.matmul(ps[:, :], w[:, 512 + c * P:512 + (c + 1) * P],
                                                         k.avgq[:, b:b + 1].to_broadcast([P, S]), start=False, stop=True))
    amax_tensor(k, pe, "h")
    pe.wait_ge(k.q_ready, 10)
    open_acc(k, pe, 2)
    for b in range(B):
        for i in range(TB):
            t = b * TB + i
            for c in range(4):
                last = nc.tensor.matmul(k.acc[b][:, i * D:(i + 1) * D], T.hq[:, c, t * P:(t + 1) * P],
                                        T.weight("f2")[:, c * D:(c + 1) * D], start=(c == 0), stop=(c == 3))
        last.then_inc(k.acc_filled, 1)


ROWS1 = NSLOT + N


class L1f:

    def __init__(self, k):
        at = ARENA
        self.xg = k.cols(at, [12, D])
        at += 12 * D
        self.xgT = k.cols(at, [NSLOT])
        at += NSLOT
        self.h = k.cols(at, [2, 4, CAP])
        at += 2 * 4 * CAP
        self.eo = k.cols(at, [E8, 2, D])
        at += E8 * 2 * D
        self.y = k.cols(at, [NT, D])
        self.zeros = k.cols(PLACE["L2f"] + 12000, [1024])


def l1f_jobs_order():
    for e in range(E8):
        if e == 0:
            yield "h", 0
        if e + 1 < E8:
            yield "h", e + 1
        yield "eo", e


def l1f_vector(k, v, A2):
    nc, T = k.nc, L1f(k)
    softmax_vector(k, v, "L1f")
    probs = k.rt[:, 1, 0:64]
    rank_vector(k, v, probs)
    one = k.rt[:, 2, 0:64]
    three = lambda ap: ap.rearrange("p (t e) -> p t e", t=NT)
    v.did(nc.vector.tensor_scalar(one, k.rt[:, 3, 0:64], 1.0, None, ALU.is_lt))
    v.settle()
    v.did(nc.vector.tensor_copy(k.onehot[:, :], one), k.w_ready)
    v.did(nc.vector.tensor_tensor(k.rt[:, 3, 0:64], one, probs, ALU.mult))
    v.did(nc.vector.tensor_tensor(k.rt[:, 4, 0:64], one, k.w("const", "expert_base"), ALU.mult))
    v.settle()
    v.did(nc.vector.tensor_reduce(k.m8[:, :], three(k.rt[:, 3, 0:64]), axis=AX.X, op=ALU.add))
    v.did(nc.vector.tensor_reduce(k.s8[:, :], three(k.rt[:, 4, 0:64]), axis=AX.X, op=ALU.add))
    v.settle()
    v.did(nc.vector.tensor_scalar(k.gp[:, :], k.m8[:, :], k.gates[:, 3:4], None, ALU.mult))
    ps = k.filled(v.eng, ("L1f", "count"))
    v.drain(("L1f", "count"), nc.vector.tensor_tensor(k.rt[:, 0, 0:64], ps[:, 0:64], one, ALU.mult))
    v.settle()
    v.did(nc.vector.tensor_reduce(k.r8[:, :], three(k.rt[:, 0, 0:64]), axis=AX.X, op=ALU.add))
    v.settle()
    dummy = k.w("const", "dummy_row")
    v.did(nc.vector.tensor_tensor(k.s8[:, :], k.s8[:, :], k.r8[:, :], ALU.add))
    v.settle()
    v.did(nc.vector.tensor_tensor(k.s8[:, :], k.s8[:, :], dummy, ALU.subtract))
    v.settle()
    v.did(nc.vector.scalar_tensor_tensor(out=k.s8[:, :], in0=k.r8[:, :], scalar=float(CAP), in1=k.s8[:, :], op0=ALU.is_le, op1=ALU.mult))
    v.settle()
    v.did(nc.vector.tensor_tensor(k.idx[:, :], k.s8[:, :], dummy, ALU.add), k.slots_ready)
    v.settle()
    attention8_keys_vector(k, v, A2)
    attention8_values_vector(k, v, A2)
    b2 = k.w("rows", "L1_b2")
    for e in range(E8):
        ps = k.filled(v.eng, ("L1f", "eo", e))
        v.drain(("L1f", "eo", e), nc.vector.tensor_tensor(
            T.eo[0:CT, e, :, :], ps[0:CT, 0:2 * D].rearrange("p (j d) -> p j d", j=2),
            b2[0:CT, e * D:(e + 1) * D].unsqueeze(1).to_broadcast([CT, 2, D]), ALU.add))


def l1f_residual_vector(k, v, b):
    T = L1f(k)
    v.eng.wait_ge(k.y_loaded[b], 16 * TB)
    for t in range(b * TB, (b + 1) * TB):
        v.did(k.nc.vector.scalar_tensor_tensor(out=k.x[:, t, :], in0=T.y[:, t, :], scalar=k.gp[:, t:t + 1], in1=k.x[:, t, :],
                                               op0=ALU.mult, op1=ALU.add))
    v.settle()


def l1f_scalar(k, a):
    nc, T = k.nc, L1f(k)
    softmax_scalar(k, a, "L1f")
    for j in range(3):
        ps = k.filled(a.eng, ("L1f", "xgT", j))
        a.drain(("L1f", "xgT", j), nc.scalar.activation(T.xgT[:, j * 512:(j + 1) * 512], ps[:, :], ACT.Copy))
    b1 = k.w("L1f", "b1")
    for e in range(E8):
        if e >= 2:
            k.filled(a.eng, ("L1f", "eo", e - 2))
        for c in range(2):
            ps = k.filled(a.eng, ("L1f", "h", e, c))
            for i in range(2):
                f = 2 * c + i
                ins = nc.scalar.activation(T.h[:, e % 2, f, :], ps[:, i * CAP:(i + 1) * CAP], ACT.Gelu, bias=b1[:, 4 * e + f:4 * e + f + 1])
                a.did(ins) if i == 0 else a.drain(("L1f", "h", e, c), ins)


def l1f_tensor(k, pe, A2):
    nc, T = k.nc, L1f(k)
    logits_tensor(k, pe, "L1f", 3)
    ps = k.open(pe, ("L1f", "count"))
    pe.wait_ge(k.w_ready, 2)
    nc.tensor.matmul(ps[:, 0:64], k.w("sel", "upto"), k.onehot[:, :], start=True, stop=False, skip_group_check=True)
    for t in range(NT - 1):
        rest = NT - 1 - t
        last = nc.tensor.matmul(ps[:, (t + 1) * E8:64].rearrange("p (t e) -> p t e", t=rest), k.w("sel", "ones"),
                                bc(k.onehot[:, t * E8:(t + 1) * E8], 1, [rest, E8]), start=False, stop=(t == NT - 2),
                                skip_group_check=True)
    k.fill(("L1f", "count"), last)
    attention8_prep_tensor(k, pe, A2)
    pe.wait_ge(k.slots_loaded, 16)
    for j in range(3):
        ps = k.open(pe, ("L1f", "xgT", j))
        for i in range(4):
            last = nc.tensor.transpose(ps[:, i * P:(i + 1) * P], T.xg[:, 4 * j + i, :], k.w("const", "ident"))
        k.fill(("L1f", "xgT", j), last)
    for j in range(3):
        k.drained(pe, ("L1f", "xgT", j))
    w1, w2 = k.w("L1f", "w1"), k.w("L1f", "w2")
    for kind, e in l1f_jobs_order():
        if kind == "h":
            for c in range(2):
                ps = k.open(pe, ("L1f", "h", e, c))
                for i in range(2):
                    f = 2 * c + i
                    last = nc.tensor.matmul(ps[:, i * CAP:(i + 1) * CAP], w1[:, e * 512 + f * P:e * 512 + (f + 1) * P],
                                            T.xgT[:, e * CAP:(e + 1) * CAP], start=True, stop=True)
                k.fill(("L1f", "h", e, c), last)
        else:
            ps = k.open(pe, ("L1f", "eo", e))
            for c in range(2):
                k.drained(pe, ("L1f", "h", e, c))
            for j in range(2):
                for f in range(4):
                    last = nc.tensor.matmul(ps[0:CT, j * D:(j + 1) * D], T.h[:, e % 2, f, j * CT:(j + 1) * CT],
                                            w2[:, (4 * e + f) * D:(4 * e + f + 1) * D], start=(f == 0), stop=(f == 3))
            k.fill(("L1f", "eo", e), last)


def l1f_zero_pool(k, g):
    g.did(k.nc.gpsimd.memset(L1f(k).zeros, 0.0), k.parts_ready)


def l1f_zero_sync(k, sp):
    T = L1f(k)
    sp.wait_ge(k.parts_ready, 1)
    flat = lambda ap, a, b: ap[a:b, :].rearrange("(p r) d -> p (r d)", p=P)
    sp.dma_start(flat(k.slots, 0, 1024), T.zeros).then_inc(k.dram_zeroed, 16)
    sp.dma_start(flat(k.slots, 1024, NSLOT), T.zeros[:, 0:512]).then_inc(k.dram_zeroed, 16)
    sp.dma_start(flat(k.eo_rows, NSLOT, ROWS1), T.zeros).then_inc(k.dram_zeroed, 16)


def l1f_pool(k, g):
    nc, T = k.nc, L1f(k)
    g.eng.wait_ge(k.dram_zeroed, 48)
    g.eng.wait_ge(k.slots_ready, 1)
    g.eng.wait_ge(k.normed, NT * 4)
    for t in range(NT):
        nc.gpsimd.indirect_dma_start(out=k.slots[:, :], out_offset=bass.IndirectOffsetOnAxis(ap=k.idx[:, t:t + 1], axis=0),
                                     in_=k.xn[:, t, :], in_offset=None).then_inc(k.scattered, 16)
    g.eng.wait_ge(k.eo_stored, 16 * 4)
    for t in range(NT):
        nc.gpsimd.indirect_dma_start(out=T.y[:, t, :], out_offset=None, in_=k.eo_rows[:, :],
                                     in_offset=bass.IndirectOffsetOnAxis(ap=k.idx[:, t:t + 1], axis=0)).then_inc(k.y_loaded[t // TB], 16)


def l1f_sync(k, sp):
    T = L1f(k)
    for e in range(0, E8, 2):
        for i in range(2):
            k.drained(sp, ("L1f", "eo", e + i))
        sp.dma_start(k.eo_rows[e * CAP:(e + 2) * CAP, :].rearrange("(e j p) d -> p e j d", e=2, p=CT),
                     T.eo[0:CT, e:e + 2, :, :]).then_inc(k.eo_stored, 16)


class L2f:
    def __init__(self, k):
        at = PLACE["L0x"]
        self.xgT = k.cols(at, [E16, B, CAP2])
        self.hs = k.cols(at + 2048, [2, N])
        self.scb = k.cols(at + 4096, [2, S])
        at = ARENA
        self.selw = k.cols(at, [E16 // 2, B, S])
        self.eo = k.cols(at + 8192, [E16 // 2, B, D])
        self.h = k.cols(at + 10240, [4, 2, P])
        self.sel = k.cols(at, [NT, 1024], BF16)
        self.xp = k.cols(at + 4096, [3, NT * D], BF16)
        self.tmp = k.cols(at + 4096 + 1536, [NT * D])
        self.work = k.cols(at + 4096 + 2560, [S])[0:32]
        self.mask = k.cols(at + 4096 + 3072, [S])[0:32]
        self.cum = k.cols(at + 4096 + 3584, [S])[0:32]
        self.sg = k.small[:, 0:1024].rearrange("p (a b) -> p a b", a=2)
        self.ge = k.cmp[:, :, 0:256]
        self.stT = k.nmT[:, 0:S]


def l2f_pool(k, g):
    nc, T = k.nc, L2f(k)
    g.eng.wait_ge(k.normed, NT * 6)
    src = k.xn[:, :, :].rearrange("p t d -> p (t d)")
    g.did(nc.gpsimd.tensor_copy(T.xp[:, 0, :], src))
    g.settle()
    g.did(nc.gpsimd.tensor_tensor(T.tmp, src, T.xp[:, 0, :], ALU.subtract))
    g.settle()
    g.did(nc.gpsimd.tensor_copy(T.xp[:, 1, :], T.tmp))
    g.settle()
    g.did(nc.gpsimd.tensor_tensor(T.xp[:, 2, :], T.tmp, T.xp[:, 1, :], ALU.subtract), k.parts_ready)


SHARED2 = [(c, b) for c in range(2) for b in range(B)]


def l2f_vector(k, v):
    nc, T = k.nc, L2f(k)
    def shared(turn):
        c, b = SHARED2[turn]
        k.drained(v.eng, ("L2f", "sg", c, b))
        ps = k.filled(v.eng, ("L2f", "su", c, b))
        v.drain(("L2f", "su", c, b), nc.vector.tensor_tensor(T.hs[:, c, b * S:(b + 1) * S], T.sg[:, turn % 2, :], ps[:, :], ALU.mult))

    softmax_vector(k, v, "L2f", E16)
    p2 = k.rt[:, 2, :].rearrange("p (i c) -> p i c", i=TB)
    v.did(nc.vector.tensor_copy(p2.rearrange("p i (b e) -> p b i e", b=B), k.rt[:, 1, :].rearrange("p (b i e) -> p b i e", b=B, i=TB)), k.w_ready)
    v.settle()
    ps = k.filled(v.eng, ("L2f", "pT"))
    v.drain(("L2f", "pT"), nc.vector.tensor_copy(T.work, ps[0:32, :]))
    v.settle()
    for turn in range(CAP2 // 8):
        if turn % 2 and turn // 2 < len(SHARED2):
            shared(turn // 2)
        v.did(nc.vector.max(k.top8[0:32, :], T.work))
        v.settle()
        v.did(nc.vector.match_replace(out=T.work, in_to_replace=k.top8[0:32, :], in_values=T.work, imm_value=-1.0))
        v.settle()
    v.did(nc.vector.tensor_scalar(T.mask, T.work, 0.0, None, ALU.is_lt))
    v.settle()
    v.did(nc.vector.tensor_tensor_scan(T.cum, T.mask, T.mask, 0.0, ALU.add, ALU.max))
    v.settle()
    v.did(nc.vector.tensor_tensor(T.work, T.cum, T.mask, ALU.mult), k.slots_ready)
    parts = [k.mpad[:, 0:TB, 32 * i:32 * (i + 1)] for i in range(3)]
    three_parts(k, v, p2, parts, [k.rt[:, 3, :].rearrange("p (i c) -> p i c", i=TB)], None)
    ps = k.filled(v.eng, ("L2f", "slots"))
    v.drain(("L2f", "slots"), nc.vector.tensor_copy(k.mpad[:, 0:TB, 96:128], ps[:, 0:TB * 32].rearrange("p (i c) -> p i c", i=TB)))
    v.settle()
    iota = k.w("sel", "slot_iota").rearrange("p (e c) -> p e c", e=E16)
    for b in range(B):
        for i in range(TB):
            v.did(nc.vector.tensor_tensor(T.sel[:, b * TB + i, :].rearrange("p (e c) -> p e c", e=E16),
                                          bc(k.mpad[:, i, 96 + b * E16:96 + (b + 1) * E16], 2, [E16, CAP2]), iota, ALU.is_equal),
                  k.gather_sel)
    for b in range(B):
        for half in range(2):
            k.filled(v.eng, ("L2f", "xg", b, half))
    for kk in range(E16 // 2):
        for e in (2 * kk, 2 * kk + 1):
            ps = k.filled(v.eng, ("L2f", "gu", e))
            v.eng.wait_ge(k.act_copied, e + 1)
            if e >= 4:
                k.filled(v.eng, ("L2f", "eo", (e - 4) // 2))
            v.drain(("L2f", "gu", e), nc.vector.tensor_tensor(T.h[:, e % 4, :, :].rearrange("p f c -> p (f c)"), T.ge[:, e % 2, :],
                                                              ps[:, 256:512], ALU.mult))
        for b in range(B):
            ps = k.filled(v.eng, ("L2f", "bs", kk, b, 0))
            k.drained(v.eng, ("L2f", "bs", kk, b, 1))
            v.drain(("L2f", "bs", kk, b, 0), nc.vector.scalar_tensor_tensor(
                out=T.selw[:, kk, b, :], in0=ps[:, :], scalar=k.w("const", "slot_no"), in1=T.scb[:, b, :], op0=ALU.is_equal, op1=ALU.mult))


def l2f_scalar(k, a):
    nc, T = k.nc, L2f(k)
    softmax_scalar(k, a, "L2f", E16)
    for turn, (c, b) in enumerate(SHARED2):
        if turn >= 2:
            k.drained(a.eng, ("L2f", "su", *SHARED2[turn - 2]))
        ps = k.filled(a.eng, ("L2f", "sg", c, b))
        a.drain(("L2f", "sg", c, b), nc.scalar.activation(T.sg[:, turn % 2, :], ps[:, :], ACT.Gelu))
    ps = k.filled(a.eng, ("L2f", "stT"))
    a.drain(("L2f", "stT"), nc.scalar.activation(T.stT, ps[:, :].bitcast(BF16)[:, 0:S], ACT.Copy))
    for b in range(B):
        for half in range(2):
            ps = k.filled(a.eng, ("L2f", "xg", b, half))
            a.drain(("L2f", "xg", b, half), nc.scalar.activation(
                T.xgT[:, half * 8:(half + 1) * 8, b, :], ps[:, :].rearrange("p (e c) -> p e c", e=8), ACT.Copy))
    for kk in range(E16 // 2):
        for e in (2 * kk, 2 * kk + 1):
            ps = k.filled(a.eng, ("L2f", "gu", e))
            if e >= 2:
                k.drained(a.eng, ("L2f", "gu", e - 2))
            a.did(nc.scalar.activation(T.ge[:, e % 2, :], ps[:, 0:256], ACT.Gelu), k.act_copied)
        for b in range(B):
            if kk:
                k.drained(a.eng, ("L2f", "bs", kk - 1, b, 0))
            ps = k.filled(a.eng, ("L2f", "bs", kk, b, 1))
            a.drain(("L2f", "bs", kk, b, 1), nc.scalar.activation(T.scb[:, b, :], ps[:, :], ACT.Copy))
        if kk:
            eo_scalar(k, a, T, kk - 1)
    eo_scalar(k, a, T, E16 // 2 - 1)


def eo_scalar(k, a, T, kk):
    ps = k.filled(a.eng, ("L2f", "eo", kk))
    a.drain(("L2f", "eo", kk), k.nc.scalar.activation(T.eo[:, kk, :, :], ps[:, 0:2 * D].rearrange("p (b d) -> p b d", b=B), ACT.Copy))


def l2f_tensor(k, pe):
    nc, T = k.nc, L2f(k)
    logits_tensor(k, pe, "L2f", 5, E16)
    ps = k.open(pe, ("L2f", "pT"))
    pe.wait_ge(k.w_ready, 3)
    for i in range(TB):
        last = nc.tensor.transpose(ps[0:32, i * P:(i + 1) * P], k.rt[:, 2, 32 * i:32 * (i + 1)], k.w("const", "ident"))
    k.fill(("L2f", "pT"), last)
    for c, b in SHARED2:
        for kind in ("sg", "su"):
            ps = k.open(pe, ("L2f", kind, c, b))
            k.fill(("L2f", kind, c, b), nc.tensor.matmul(ps[:, :], k.w("L2f", kind)[:, c * P:(c + 1) * P], k.xnT[:, b * S:(b + 1) * S],
                                                         start=True, stop=True))
    ps = k.open(pe, ("L2f", "slots"))
    pe.wait_ge(k.slots_ready, 2)
    for i in range(TB):
        last = nc.tensor.transpose(ps[:, 32 * i:32 * (i + 1)], T.work[:, i * P:(i + 1) * P], k.w("const", "ident")[0:32, 0:32])
    k.fill(("L2f", "slots"), last)
    ps = k.open(pe, ("L2f", "stT"))
    k.drained(pe, ("L2f", "slots"))
    for i in range(TB):
        last = nc.tensor.transpose(ps[:, :].bitcast(BF16)[:, i * P:(i + 1) * P], k.mpad[:, i, :], k.w("sel", "ident"))
    k.fill(("L2f", "stT"), last)
    pe.wait_ge(k.parts_ready, 2)
    for b in range(B):
        for half in range(2):
            ps = k.open(pe, ("L2f", "xg", b, half))
            for i in range(TB):
                t = b * TB + i
                pe.wait_ge(k.gather_sel, t + 1)
                for part in range(3):
                    last = nc.tensor.matmul(ps[:, :], T.xp[:, part, t * D:(t + 1) * D], T.sel[:, t, half * 512:(half + 1) * 512],
                                            start=(i == 0 and part == 0), stop=(i == TB - 1 and part == 2))
            k.fill(("L2f", "xg", b, half), last)
    k.drained(pe, ("L2f", "stT"))

    def down(kk):
        ps = k.open(pe, ("L2f", "eo", kk))
        for e2 in range(2):
            e = 2 * kk + e2
            k.drained(pe, ("L2f", "gu", e))
            for b in range(B):
                for f in range(2):
                    last = nc.tensor.matmul(ps[64 * e2:64 * (e2 + 1), b * D:(b + 1) * D], T.h[:, e % 4, f, b * CAP2:(b + 1) * CAP2],
                                            k.w("L2f", "d")[:, (2 * e + f) * D:(2 * e + f + 1) * D], start=(f == 0), stop=(f == 1))
        k.fill(("L2f", "eo", kk), last)

    for kk in range(E16 // 2):
        for e in (2 * kk, 2 * kk + 1):
            ps = k.open(pe, ("L2f", "gu", e))
            for b in range(B):
                k.drained(pe, ("L2f", "xg", b, e // 8))
            for j, name in enumerate(("g", "g", "u", "u")):
                at = e * 256 + (j % 2) * P
                last = nc.tensor.matmul(ps[:, j * P:(j + 1) * P], k.w("L2f", name)[:, at:at + P],
                                        T.xgT[:, e, :, :].rearrange("p b c -> p (b c)"), start=True, stop=True)
            k.fill(("L2f", "gu", e), last)
        for b in range(B):
            for x, name in enumerate(("slot", "score")):
                ps = k.open(pe, ("L2f", "bs", kk, b, x))
                at = (b * 8 + kk) * P
                k.fill(("L2f", "bs", kk, b, x), nc.tensor.matmul(ps[:, :], k.w("sel", name)[:, at:at + P], T.stT, start=True, stop=True))
        if kk:
            down(kk - 1)
    down(E16 // 2 - 1)
    open_acc(k, pe, 5)
    for b in range(B):
        for kk in range(E16 // 2):
            k.drained(pe, ("L2f", "bs", kk, b, 0))
            k.drained(pe, ("L2f", "eo", kk))
        for c in range(2):
            k.drained(pe, ("L2f", "su", c, b))
        for i in range(TB):
            t = b * TB + i
            out = k.acc[b][:, i * D:(i + 1) * D]
            for c in range(2):
                nc.tensor.matmul(out, T.hs[:, c, t * P:(t + 1) * P], k.w("L2f", "sd")[:, c * D:(c + 1) * D], start=(c == 0), stop=False)
            for kk in range(E16 // 2):
                last = nc.tensor.matmul(out, T.selw[:, kk, b, i * P:(i + 1) * P], T.eo[:, kk, b, :], start=False, stop=(kk == 7))
        last.then_inc(k.acc_filled, 1)


def build(nc, dram, x_in, out):
    with ExitStack() as ctx:
        k = Core(nc, ctx, dram, out)
        block = ctx.enter_context(nc.Block())
        A0, A2 = Attention8(k, "L0x", 0), Attention8(k, "L2x", 4)
        A3 = Attention64(k)
        T1 = L1f(k)
        M0 = Moe(k, "L0f", 1, P, 6, 4)
        M3 = Moe(k, "L3f", 7, 96, 10, 8)

        @block.sync
        def _(sp):
            def load(*groups):
                for g in groups:
                    dst = k.packed[g][:, :] if g in ("const", "ctx", "sel", "rows") else k.packed[g]
                    src = dram[g].to_broadcast([P, WIDTH[g]]) if g == "rows" else dram[g]
                    sp.dma_start(dst, src).then_inc(k.loaded[g], 16)

            sp.dma_start(k.x[:, :, :], x_in.rearrange("(t p) d -> p t d", p=P)).then_inc(k.x_loaded, 16)
            load("const", "ctx", "L0x", "rows")
            stack_keys_sync(k, sp, A0)
            stack_queries_sync(k, sp, A0)
            load("sel", "L0f", "L1x")
            stack_maxima_sync(k, sp, A0)
            load("L1f")
            l1f_zero_sync(k, sp)
            load("L2x")
            sp.wait_ge(k.scattered, 16 * NT)
            sp.dma_start(T1.xg, k.slots[0:NSLOT, :].rearrange("(j p) d -> p j d", p=P)).then_inc(k.slots_loaded, 16)
            stack_keys_sync(k, sp, A2)
            l1f_sync(k, sp)
            stack_queries_sync(k, sp, A2)
            stack_maxima_sync(k, sp, A2)
            load("L2f")
            load("L3x")
            sp.wait_ge(k.x_ready, 5)
            load("L3f")
            sp.wait_ge(k.x_ready, SUBLAYERS)
            sp.dma_start(out.rearrange("(t p) d -> p t d", p=P), k.x[:, :, :]).then_inc(k.out_stored, 16)
            sp.wait_ge(k.out_stored, 16)

        @block.gpsimd
        def _(eng):
            g = Chain(k, eng, k.pool_step)
            l1f_zero_pool(k, g)
            eng.wait_ge(k.loaded["const"], 16)
            for b in range(B):
                norm_pool(k, g, 0, b)
            g.settle()
            attention8_prep_pool(k, g, A0)
            l1x_keys_pool(k, g)
            for b in range(B):
                norm_pool(k, g, 1, b)
            for b in range(B):
                norm_pool(k, g, 2, b)
            l1x_pool(k, g)
            for b in range(B):
                norm_pool(k, g, 3, b)
            attention8_prep_pool(k, g, A2)
            l1f_pool(k, g)
            for b in range(B):
                norm_pool(k, g, 4, b)
            for b in range(B):
                norm_pool(k, g, 5, b)
            l2f_pool(k, g)
            for b in range(B):
                norm_pool(k, g, 6, b)
            attention64_pool(k, g, A3)
            for b in range(B):
                norm_pool(k, g, 7, b)

        @block.scalar
        def _(eng):
            a = Chain(k, eng, k.scalar_step)
            eng.wait_ge(k.loaded["rows"], 16)
            a.did(nc.scalar.activation(k.gates[:, :], k.w("rows", "g"), ACT.Tanh), k.gates_ready)
            attention8_scalar(k, a, A0)
            moe_scalar(k, a, M0)
            for b in range(B):
                norm_scalar(k, a, 2, b)
            l1x_scalar(k, a)
            for b in range(B):
                norm_scalar(k, a, 3, b)
            l1f_scalar(k, a)
            attention8_scalar(k, a, A2)
            for b in range(B):
                norm_scalar(k, a, 5, b)
            l2f_scalar(k, a)
            attention64_scalar(k, a, A3)
            moe_scalar(k, a, M3)

        @block.vector
        def _(eng):
            v = Chain(k, eng, k.vector_step)

            def between(n, residual, bias=None):
                for b in range(B):
                    residual(b)
                    if b == B - 1:
                        done(k, v)
                    if n + 1 < SUBLAYERS:
                        norm_vector(k, v, n + 1, b, bias)

            v.did(nc.vector.memset(A0.ks[:, :, :, :], 0.0))
            eng.wait_ge(k.x_loaded, 16)
            eng.wait_ge(k.loaded["const"], 16)
            norm_vector(k, v, 0, 0, k.w("rows", "L0_b2"))
            attention8_keys_vector(k, v, A0)
            norm_vector(k, v, 0, 1, k.w("rows", "L0_b2"))
            attention8_values_vector(k, v, A0)
            attention8_vector(k, v, A0)
            between(0, lambda b: residual_vector(k, v, 0, b, k.xb))
            moe_vector(k, v, M0)
            between(1, lambda b: residual_vector(k, v, 1, b, k.x), k.w("rows", "L1_bf2"))
            l1x_vector(k, v)
            between(2, lambda b: residual_vector(k, v, 2, b, k.xb, k.comb[:, 7:8]))
            l1f_vector(k, v, A2)
            between(3, lambda b: l1f_residual_vector(k, v, b), k.w("rows", "L2_bo"))
            attention8_vector(k, v, A2)
            between(4, lambda b: residual_vector(k, v, 4, b, k.xb))
            l2f_vector(k, v)
            between(5, lambda b: residual_vector(k, v, 5, b, k.x), k.w("rows", "L3_bo"))
            attention64_vector(k, v, A3)
            between(6, lambda b: residual_vector(k, v, 6, b, k.xb))
            moe_vector(k, v, M3)
            between(7, lambda b: residual_vector(k, v, 7, b, k.x))

        @block.tensor
        def _(pe):
            pe.wait_ge(k.loaded["const"], 16)
            attention8_prep_tensor(k, pe, A0)
            attention8_tensor(k, pe, A0)
            moe_tensor(k, pe, M0)
            for b in range(B):
                norm_tensor(k, pe, 2, b)
            l1x_tensor(k, pe)
            for b in range(B):
                norm_tensor(k, pe, 3, b)
            l1f_tensor(k, pe, A2)
            attention8_tensor(k, pe, A2)
            for b in range(B):
                norm_tensor(k, pe, 5, b)
            l2f_tensor(k, pe)
            attention64_tensor(k, pe, A3)
            moe_tensor(k, pe, M3)


def layout(np, i, bf16):
    def rows(a):
        out = np.zeros((P, a.shape[1]), a.dtype)
        out[:a.shape[0]] = a
        return out

    def chunked(a, n=P):
        return rows(a.reshape(-1, n, a.shape[1]).transpose(1, 0, 2).reshape(n, -1))

    def col(a, n=P):
        return rows(np.ascontiguousarray(a.reshape(-1, n).T))

    f32 = np.float32
    x = i["x"].reshape(N, D)
    ctxT = i["ctx_768"].reshape(NK, DC).T
    rem = np.zeros((DC, B, HG, HP), f32)
    for b in range(B):
        rem[:, b, :, :MR] = ctxT[:, None, b * M + P:(b + 1) * M]
    r = np.arange(P)[:, None]
    e = np.arange(8)
    dup = lambda w: np.concatenate([w.T, w.T], axis=1)
    kv = i["L2_xattn_Wkv"].reshape(H, 2, 8, DC)
    bkv = i["L2_xattn_bkv"].reshape(H, 2, 8)
    w1_3 = i["L3_ffn_W1"].transpose(2, 0, 1)
    s1_3 = i["L3_ffn_Ws1"].T
    w_2_1 = i["L1_ffn_w2"].reshape(8, 4, P, D).transpose(2, 0, 1, 3).reshape(P, -1)
    d_2 = i["L2_ffn_Wd"].transpose(0, 2, 1).reshape(16, 2, P, D).transpose(2, 0, 1, 3).reshape(P, -1)
    wq_3 = np.zeros((8, 2, 2, 64, D), f32)
    for odd in range(2):
        wq_3[:, odd, odd] = i["L3_xattn_Wq"].T.reshape(8, 2, 64, D)[:, odd]
    wq_3 = wq_3.reshape(16, P, D).transpose(1, 0, 2).reshape(P, -1)
    stacked = np.arange(P).reshape(8, 2, 8).transpose(1, 2, 0).reshape(P)
    parts = {
        "const": dict(
            ident=np.eye(P), ones=np.ones((P, P)),
            rem_rows=(r // HP == np.arange(HG)) & (r % HP < MR),
            earlier=np.broadcast_to((e[None, :] < e[:, None]).reshape(1, 64), (P, 64)),
            slot_no=r % CAP2 + 1, neg_half=np.full((P, 8), -0.5),
            expert_base=np.broadcast_to(np.tile(e * CAP - 1.0, 8), (P, 64)), dummy_row=NSLOT + r + P * e),
        "ctx": dict(ctxT=rows(ctxT), ctx_rem=rows(rem.reshape(DC, -1))),
        "L0x": dict(Wk=rows(i["L0_xattn_Wk"][:, stacked]), Wv=rows(i["L0_xattn_Wv"]), Wq=i["L0_xattn_Wq"][:, stacked], W1=i["L0_xattn_W1"],
                    W2=chunked(i["L0_xattn_W2"]), bq=col(i["L0_xattn_bq"][stacked]), bk=col(i["L0_xattn_bk"][stacked]), b1=col(i["L0_xattn_b1"])),
        "L0f": dict(Wr=i["L0_ffn_router_w"], gate=i["L0_ffn_gate_w"].transpose(1, 0, 2).reshape(D, -1),
                    up=i["L0_ffn_up_w"].transpose(1, 0, 2).reshape(D, -1), sgate=i["L0_ffn_s_gate_w"], sup=i["L0_ffn_s_up_w"],
                    down=chunked(i["L0_ffn_down_w"].reshape(512, D)), sdown=chunked(i["L0_ffn_s_down_w"])),
        "L1x": dict(d2v=rows(i["L1_xattn_W_d2v"].T), img=i["L1_xattn_W_img"].T, att0=dup(i["L1_xattn_W_att0"]),
                    att1=dup(i["L1_xattn_W_att1"]), txt=i["L1_xattn_W_txt"].T, f1=chunked(i["L1_xattn_W_f1"].T),
                    f2=chunked(i["L1_xattn_W_f2"].T), b_d2v=col(i["L1_xattn_b_d2v"]), b_img=col(i["L1_xattn_b_img"]),
                    b_att0=col(np.tile(i["L1_xattn_b_att0"], 2)), b_att1=col(np.tile(i["L1_xattn_b_att1"], 2)),
                    b_txt=col(i["L1_xattn_b_txt"]), b_f1=col(i["L1_xattn_b_f1"])),
        "L1f": dict(Wr=i["L1_ffn_router_w"].T, w1=i["L1_ffn_w1"].transpose(1, 0, 2).reshape(D, -1), w2=w_2_1,
                    b1=i["L1_ffn_b1"].reshape(8, 4, P).transpose(2, 0, 1).reshape(P, -1)),
        "L2x": dict(Wk=rows(kv[:, 0].reshape(P, DC)[stacked].T), Wv=rows(kv[:, 1].reshape(P, DC).T), Wq=i["L2_xattn_Wq"][stacked].T,
                    Wo=i["L2_xattn_Wo"].T, bq=col(i["L2_xattn_bq"][stacked]), bk=col(bkv[:, 0].reshape(P)[stacked])),
        "L2f": dict(Wr=i["L2_ffn_gate_w"].T, sg=i["L2_ffn_Ws_g"].T, su=i["L2_ffn_Ws_u"].T, sd=chunked(i["L2_ffn_Ws_d"].T),
                    g=i["L2_ffn_Wg"].transpose(2, 0, 1).reshape(D, -1), u=i["L2_ffn_Wu"].transpose(2, 0, 1).reshape(D, -1),
                    d=d_2),
        "L3x": dict(Wk=rows(i["L3_xattn_Wk"]), Wv=rows(i["L3_xattn_Wv"]), WqT=wq_3, Wo=chunked(i["L3_xattn_Wo"])),
        "L3f": dict(Wr=i["L3_ffn_gate_w"].T,
                    gate=np.concatenate([w1_3[:, :, 96:].reshape(D, -1), s1_3[:, 192:]], axis=1),
                    up=np.concatenate([w1_3[:, :, :96].reshape(D, -1), s1_3[:, :192]], axis=1),
                    down=np.concatenate([rows(i["L3_ffn_W2"].transpose(2, 0, 1).reshape(96, -1)),
                                         chunked(i["L3_ffn_Ws2"].T, 96)], axis=1)),
        "rows": dict(g=np.stack([i["g_xattn"], i["g_ffn"]], axis=1).reshape(1, 8), rb=i["L0_ffn_router_bias"].reshape(1, 1),
                     L0_bv=i["L0_xattn_bv"], L0_b2=i["L0_xattn_b2"], L1_bf2=i["L1_xattn_b_f2"], L1_b2=i["L1_ffn_b2"],
                     L2_bv=bkv[:, 1], L2_bo=i["L2_xattn_bo"], L3_bo=i["L3_xattn_bo"]),
    }
    m = np.arange(P)
    c = np.arange(4)
    mm = np.zeros((P, 16, P))
    for h in range(16):
        mm[h, h] = mm[16 + h, h] = 1
    s0, s3 = np.zeros((P, 4, P)), np.zeros((P, 8, 96))
    slot, score = np.zeros((P, B, 8, P)), np.zeros((P, B, 8, P))
    for part in range(3):
        for q in range(8):
            s0[part * 8 + q, q // 2, (q % 2) * 64:(q % 2) * 64 + 64] = 1
            s3[part * 8 + q, q] = 1
        for b in range(B):
            for q in range(16):
                cs = slice((q % 2) * 64, (q % 2) * 64 + 64)
                score[part * 32 + b * 16 + q, b, q // 2, cs] = 1
                slot[96 + b * 16 + q, b, q // 2, cs] = 1
    parts["sel"] = dict(ident=np.eye(P), ones=np.ones((P, P)), upto=(r <= m), minus_max=mm, L0f=s0, L3f=s3, slot=slot,
                        score=score, slot_iota=np.broadcast_to(np.tile(np.arange(CAP2) + 1, 16), (P, 1024)))
    ones = np.zeros((4, H, B, 160), np.float32)
    for row in range(4):
        ones[row, row % 2::2, :, :M] = 1
    packed = {"maxrows": ones.reshape(4, -1).astype(bf16)}
    for group, items in PACK.items():
        n = 1 if group == "rows" else P
        dt = bf16 if group == "sel" else f32
        cols = [np.asarray(parts[group][name], dt).reshape(n, width) for name, width in items]
        packed[group] = np.ascontiguousarray(np.concatenate(cols, axis=1))
    return x, packed


def kernel(**inputs):
    import numpy as np
    import concourse.bacc as bacc
    from concourse.bass_utils import run_bass_kernel_spmd

    i = {name: np.asarray(a) for name, a in inputs.items()}
    x, packed = layout(np, i, mybir.dt.np(BF16))
    nc = bacc.Bacc("TRN2", target_bir_lowering=False, num_devices=1)
    arrays = {"x_in": np.ascontiguousarray(x)}
    dram = {}
    x_ap = nc.dram_tensor("x_in", x.shape, F32, kind="ExternalInput").ap()
    for group, a in packed.items():
        arrays[f"in_{group}"] = a
        dram[group] = nc.dram_tensor(f"in_{group}", a.shape, mybir.dt.from_np(a.dtype), kind="ExternalInput").ap()
    out = nc.dram_tensor("x_out", (N, D), F32, kind="ExternalOutput").ap()
    build(nc, dram, x_ap, out)
    r = run_bass_kernel_spmd(nc, [arrays], core_ids=[0])
    return r.results[0]["x_out"].reshape(B, S, D)
```

```python
from contextlib import ExitStack

import concourse.bass as bass
from concourse import mybir

ALU = mybir.AluOpType
ACT = mybir.ActivationFunctionType
AX = mybir.AxisListType
F32 = mybir.dt.float32
BF16 = mybir.dt.bfloat16
U32 = mybir.dt.uint32

P = 128
B, S, D = 2, 512, 128
N = B * S
NT = N // P
TB = S // P
M, DC = 154, 96
MR = M - P
NK = B * M
H = 16
HP = 32
HG = P // HP
NG = H // HG
EPS = 1e-5
E8 = 8
CAP = 192
NSLOT = E8 * CAP
CT = CAP // 2
E16, CAP2 = 16, 64
MAGIC = 12582912.0
NRING = 6


PACK = {
    "const": [("ident", 128), ("ones", 128), ("rem_rows", 4), ("earlier", 64),
              ("slot_no", 1), ("neg_half", 8), ("expert_base", 64), ("dummy_row", 8)],
    "ctx": [("ctxT", NK), ("ctx_rem", B * P)],
    "L0x": [("Wk", 128), ("Wv", 128), ("Wq", 128), ("W1", 256), ("W2", 256), ("bq", 1), ("bk", 1), ("b1", 2)],
    "L0f": [("Wr", 8), ("gate", 512), ("up", 512), ("sgate", 256), ("sup", 256), ("down", 512), ("sdown", 256)],
    "L1x": [("d2v", 128), ("img", 128), ("att0", 128), ("att1", 128), ("txt", 128), ("f1", 1024), ("f2", 512),
            ("b_d2v", 1), ("b_img", 1), ("b_att0", 1), ("b_att1", 1), ("b_txt", 1), ("b_f1", 4)],
    "L1f": [("Wr", 8), ("w1", 8 * 512), ("w2", 8 * 512), ("b1", 32)],
    "L2x": [("Wk", 128), ("Wv", 128), ("Wq", 128), ("Wo", 128), ("bq", 1), ("bk", 1)],
    "L2f": [("Wr", 16), ("sg", 256), ("su", 256), ("sd", 256), ("g", 4096), ("u", 4096), ("d", 4096)],
    "L3x": [("Wk", 1024), ("Wv", 1024), ("WqT", H * 128), ("Wo", 1024)],
    "L3f": [("Wr", 8), ("gate", 1024), ("up", 1024), ("down", 1024)],
    "sel": [("ident", 128), ("ones", 128), ("upto", 128), ("minus_max", 16 * 128), ("L0f", 4 * 128), ("L3f", 6 * 128),
            ("slot", 16 * 128), ("score", 16 * 128), ("slot_iota", 1024)],
    "rows": [("g", 8), ("rb", 1), ("L0_bv", 128), ("L0_b2", 128), ("L1_bf2", 128), ("L1_b2", 1024),
             ("L2_bv", 128), ("L2_bo", 128), ("L3_bo", 128)],
}
WIDTH = {group: sum(n for _, n in items) for group, items in PACK.items()}


def columns(group, name):
    at = 0
    for part, n in PACK[group]:
        if part == name:
            return at, at + n
        at += n
    raise KeyError(name)


EARLY = ["L0x", "L0f", "L1x", "L1f", "L2x", "L2f"]
PLACE, ARENA = {}, 0
for _g in EARLY:
    PLACE[_g] = ARENA
    ARENA += WIDTH[_g]
PLACE["L3x"] = PLACE["L2f"]
PLACE["L3f"] = 0
assert WIDTH["L3f"] <= PLACE["L1f"]
ARENA_SIZE = 11500


class Banks:

    def __init__(self, labels):
        self.at = {label: (i % NRING, i // NRING) for i, label in enumerate(labels)}
        assert len(self.at) == len(labels)


def attention8_prep_jobs(L):
    return [(L, "k")] + [(L, kind, b) for b in range(B) for kind in ("v", "vr")]


LATE = [(t, p) for t in range(TB, NT) for p in range(H // 2)]
BEFORE_TURN, AFTER_TURN = LATE[0:5], LATE[5:11]
LATE_STEP, LATE_GROUPS = 11, 2


def late_scores(b, g, j=None):
    rest = LATE[11:]
    late = rest[g * LATE_STEP:(g + 1) * LATE_STEP] if b == 0 else []
    return late if j is None else late[3 * j:3 * (j + 1)]


QUERY_TILE = {"L0x": 0, "L2x": 0}
TAIL_STEP = 5
assert 11 + LATE_GROUPS * LATE_STEP >= len(LATE) and 3 * HG >= LATE_STEP


def attention8_jobs(L):
    n = {"L0x": 0, "L2x": 4}[L]
    jobs = [("xnT", n, 0), (L, "q", 0), ("xnT", n, 1)]
    for t in range(TB):
        jobs += ([(L, "q", 1)] if t == QUERY_TILE[L] else []) + [(L, "s", t, p) for p in range(H // 2)]
    jobs += [(L, "s", t, p) for t, p in BEFORE_TURN] + [(L, "nmT", 0)] + [(L, "s", t, p) for t, p in AFTER_TURN]
    steps = [(b, g) for b in range(B) for g in range(NG)]

    def scores_T(b, g):
        return [job for j in range(HG) for job in [(L, "st", b, g, j)] + [(L, "s", t, p) for t, p in late_scores(b, g, j)]] + [(L, "sr", b, g)]

    jobs += scores_T(*steps[0])
    for n, step in enumerate(steps):
        jobs += scores_T(*steps[n + 1]) if n + 1 < len(steps) else []
        if n:
            jobs += [(L, "ot", *steps[n - 1])] + (l1x_prep_jobs(n - 1) if L == "L0x" else [])
        jobs += [(L, "oT", 0)] if n == TAIL_STEP else []
        jobs += [(L, "h", c, 0) for c in range(2)] if n == TAIL_STEP + 1 and L == "L0x" else []
        jobs += [(L, "pv", *step)]
        jobs += [(L, "nmT", 1)] if n == 1 else []
    jobs += [(L, "ot", *steps[-1]), (L, "oT", 1)]
    return jobs + ([(L, "h", c, 1) for c in range(2)] if L == "L0x" else [])


def moe_jobs(L, n, chunks, routed):
    jobs = []
    first = [(c, b) for c in range(routed) for b in range(B)]
    for b in range(B):
        jobs += [("xnT", n, b)] + [(L, "logits")] * (b == B - 1)
        jobs += [(L, kind, c, b) for c in range(routed, chunks) for kind in ("g", "u")]
    jobs += [(L, "wT", b) for b in range(B)]
    for turn, (c, b) in enumerate(first, B * (chunks - routed)):
        jobs += l1x_prep_jobs(L1X_PREP_TURNS[turn]) if L == "L0f" and turn in L1X_PREP_TURNS else []
        jobs += [(L, "g", c, b), (L, "u", c, b), (L, "w", c, b)]
    return jobs


AMAX = ["ctx", "vis", "img", "x", "cat", "h"]


def amax_jobs(name):
    return [("L1x", "amT", name), ("L1x", "amB", name)]


def l1x_prep_jobs(step):
    name, turn = L1X_PREP[step]
    if turn == "amT":
        return [("L1x", "amT", name)]
    if turn == "amB":
        return [("L1x", "amB", name)]
    if name == "kv":
        return [("L1x", "kv", a) for a in range(2)]
    if name == "kvT":
        return [("L1x", "kvT", a, b) for a in range(2) for b in range(B)]
    return [("L1x", name)]


L1X_PREP = [("wsum", None), ("ctx", "amT"), ("ctx", "amB"), ("vis", None), ("vis", "amT"), ("vis", "amB"),
            ("img", None), ("img", "amT"), ("img", "amB"), ("kv", None), ("kvT", None)]
L1X_PREP_TURNS = {5: 7, 7: 8, 9: 9, 11: 10}
assert B * NG - 1 + len(L1X_PREP_TURNS) == len(L1X_PREP)


def l1x_jobs():
    jobs = amax_jobs("x") + [("L1x", "txt", b) for b in range(B)]
    for a in range(2):
        jobs += [("L1x", "s", a, t) for t in range(0, NT, 2)]
        jobs += [("L1x", "pT", a, b, half) for b in range(B) for half in range(2)] + [("L1x", "o", a, b) for b in range(B)]
    jobs += amax_jobs("cat") + [("L1x", "f1", c, b) for c in range(4) for b in range(B)]
    return jobs + amax_jobs("h")


def l1f_jobs():
    jobs = [("L1f", "logits")] + fold64_jobs("k") + [("L1f", "count")] + fold64_jobs("v")
    jobs += attention8_prep_jobs("L2x")
    jobs += fold64_jobs(1)
    jobs += [("L1f", "xgT", j) for j in range(3)]
    for kind, e in l1f_jobs_order():
        jobs += [("L1f", "h", e, c) for c in range(2)] if kind == "h" else [("L1f", "eo", e)]
    return jobs + fold64_jobs("g") + fold64_jobs(0)


def l2f_jobs():
    jobs = [("L2f", "logits"), ("L2f", "pT")]
    jobs += [("L2f", x, c, b) for c in range(2) for b in range(B) for x in ("sg", "su")]
    jobs += [("L2f", "slots")] + [("L2f", "stT")]
    jobs += [("L2f", "xg", b, half) for b in range(B) for half in range(2)]
    for k in range(E16 // 2):
        jobs += [("L2f", "gu", 2 * k), ("L2f", "gu", 2 * k + 1)]
        jobs += [("L2f", "bs", k, b, x) for b in range(B) for x in (0, 1)]
        jobs += [("L2f", "eo", k - 1)] if k else []
    return jobs + [("L2f", "eo", E16 // 2 - 1)]


SUBLAYERS = 8


def all_jobs():
    jobs = attention8_prep_jobs("L0x") + attention8_jobs("L0x")
    jobs += moe_jobs("L0f", 1, 6, 4)
    jobs += [("xnT", 2, b) for b in range(B)] + l1x_jobs()
    jobs += [("xnT", 3, b) for b in range(B)] + l1f_jobs()
    jobs += attention8_jobs("L2x")
    jobs += [("xnT", 5, b) for b in range(B)] + l2f_jobs()
    jobs += attention64_jobs("L3x")
    jobs += moe_jobs("L3f", 7, 8, 6)
    return jobs


class Core:

    def __init__(self, nc, ctx, dram, out):
        self.nc, self.dram, self.out = nc, dram, out
        self.banks = Banks(all_jobs())

        def sb(name, shape, dt=F32):
            return ctx.enter_context(nc.sbuf_tensor(name, shape, dt))

        def sem(name):
            return ctx.enter_context(nc.semaphore(name))

        self.bank_filled = [sem(f"bank_filled{i}") for i in range(NRING)]
        self.bank_drained = [sem(f"bank_drained{i}") for i in range(NRING)]
        self.loaded = {g: sem(f"loaded_{g}") for g in PACK}
        self.x_ready = sem("x_ready")
        self.values_done = sem("values_done")
        self.p64_ready = sem("p64_ready")
        self.x_loaded = sem("x_loaded")
        self.out_stored = sem("out_stored")
        self.vector_step = sem("vector_step")
        self.scalar_step = sem("scalar_step")
        self.pool_step = sem("pool_step")
        self.var_ready = sem("var_ready")
        self.rstd_ready = sem("rstd_ready")
        self.normed = sem("normed")
        self.acc_filled = sem("acc_filled")
        self.residual_done = sem("residual_done")
        self.bias_ready = sem("bias_ready")
        self.gates_ready = sem("gates_ready")
        self.zeroed = sem("zeroed")
        self.v_ready = sem("v_ready")
        self.kparts_ready = sem("kparts_ready")
        self.q0_ready = sem("q0_ready")
        self.qparts_ready = sem("qparts_ready")
        self.k_stacked = [sem(f"k_stacked{i}") for i in range(2)]
        self.q_stacked = [[sem(f"q_stacked{i}_{b}") for b in range(B)] for i in range(2)]
        self.m_stacked = [[sem(f"m_stacked{i}_{b}") for b in range(B)] for i in range(2)]
        self.nm_ready = sem("nm_ready")
        self.o_ready = sem("o_ready")
        self.l_ready = sem("l_ready")
        self.exp_ready = sem("exp_ready")
        self.w_ready = sem("w_ready")
        self.h_ready = sem("h_ready")
        self.am_ready = sem("am_ready")
        self.q_ready = sem("q_ready")
        self.l1_bias = sem("l1_bias")
        self.p_exp = sem("p_exp")
        self.p_norm = sem("p_norm")
        self.f_ready = sem("f_ready")
        self.slots_ready = sem("slots_ready")
        self.scattered = sem("scattered")
        self.slots_loaded = sem("slots_loaded")
        self.eo_stored = sem("eo_stored")
        self.y_loaded = [sem(f"y_loaded{b}") for b in range(B)]
        self.dram_zeroed = sem("dram_zeroed")
        self.vw_stored = sem("vw_stored")
        self.vw_loaded = sem("vw_loaded")
        self.parts_ready = sem("parts_ready")
        self.gather_sel = sem("gather_sel")
        self.scatter_sel = sem("scatter_sel")
        self.act_copied = sem("act_copied")

        self.ps = [ctx.enter_context(nc.psum_tensor(f"ring{i}", [P, 512], F32)) for i in range(NRING)]
        self.acc = [ctx.enter_context(nc.psum_tensor(f"acc{i}", [P, 512], F32)) for i in range(2)]

        self.packed = {g: sb(f"w_{g}", [P, WIDTH[g]], BF16 if g == "sel" else F32)
                       for g in ("const", "ctx", "sel", "rows")}
        self.mem = sb("mem", [P, ARENA + ARENA_SIZE])
        for g, at in PLACE.items():
            self.packed[g] = self.mem[:, at:at + WIDTH[g]]
        self.x = sb("x", [P, NT, D])
        self.xb = sb("xb", [P, NT, D])
        self.xn = sb("xn", [P, NT, D])
        self.xnT = sb("xnT", [P, N])
        self.stats = sb("stats", [P, NT, 6])
        self.mv = sb("mv", [P, NT, 2])
        self.rstd = sb("rstd", [P, NT])
        self.gates = sb("gates", [P, 8])
        self.small = sb("small", [P, 1024])
        self.nm = sb("nm", [P, NT, H])
        self.mpad = sb("mpad", [P, NT, P], BF16)
        self.nmT = sb("nmT", [P, N], BF16)
        self.bqs = sb("bqs", [P, 1])
        self.flag = sb("flag", [P, 4])
        self.den = sb("den", [P, 32])
        self.rden = sb("rden", [P, 2, H])
        self.onehot = sb("onehot", [P, 64], BF16)
        self.gp = sb("gp", [P, NT])
        self.idx = sb("idx", [P, NT], U32)
        self.top8 = sb("top8", [P, 8])
        self.slots = nc.dram_tensor("slots", (ROWS1, D), F32).ap()
        self.vw_rows = nc.dram_tensor("vw_rows", (P, NBLK * D), F32).ap()
        self.eo_rows = nc.dram_tensor("eo_rows", (ROWS1, D), F32).ap()
        self.rt = sb("rt", [P, 5, 128])
        self.cmp = self.xb[:, :, :].rearrange("p t d -> p (t d)").rearrange("p (a b) -> p a b", a=2)
        self.m8 = sb("m8", [P, NT])
        self.s8 = sb("s8", [P, NT])
        self.r8 = sb("r8", [P, NT])
        self.am = sb("am", [P, 8])
        self.m1 = sb("m1", [P, 1])
        self.sc = sb("sc", [P, 12])
        self.ws = sb("ws", [P, 8])
        self.wabs = sb("wabs", [P, 8])
        self.thr = sb("thr", [P, 16])
        self.comb = sb("comb", [P, 8])
        self.avg = sb("avg", [P, 2])
        self.avgq = sb("avgq", [P, 2], BF16)
        self.hm = sb("hm", [P, 8])
        self.l1s = sb("l1s", [P, 3, NT])
        self.preloads = 0
        self.preloaded = sb("preloaded", [P, 16])

    def cols(self, at, shape, dt=F32):
        n = 1
        for d in shape:
            n *= d
        words = n if dt != BF16 else n // 2
        v = self.mem[:, at:at + words]
        if dt != F32:
            v = v.bitcast(dt)
        if len(shape) == 2:
            v = v.rearrange("p (a b) -> p a b", a=shape[0])
        if len(shape) == 3:
            v = v.rearrange("p (a b c) -> p a b c", a=shape[0], b=shape[1])
        if len(shape) == 4:
            v = v.rearrange("p (a b c d) -> p a b c d", a=shape[0], b=shape[1], c=shape[2])
        return v

    def w(self, group, name):
        a, b = columns(group, name)
        return self.packed[group][:, a:b]

    def bank(self, label):
        return self.ps[self.banks.at[label][0]]

    def filled(self, eng, label):
        b, use = self.banks.at[label]
        eng.wait_ge(self.bank_filled[b], use + 1)
        return self.ps[b]

    def drained(self, eng, label):
        b, use = self.banks.at[label]
        eng.wait_ge(self.bank_drained[b], use + 1)

    def open(self, pe, label):
        b, use = self.banks.at[label]
        if use:
            pe.wait_ge(self.bank_drained[b], use)
        return self.ps[b]

    def fill(self, label, ins):
        ins.then_inc(self.bank_filled[self.banks.at[label][0]], 1)

    def drain(self, label, ins):
        b, use = self.banks.at[label]
        ins.then_inc(self.bank_drained[b], 1)
        return self.bank_drained[b], use + 1


def preload(k, a, func):
    n = k.preloads
    k.preloads += 1
    a.did(k.nc.scalar.activation(k.preloaded[:, n:n + 1], k.gates[:, 0:1], func))


class Chain:

    def __init__(self, core, eng, own):
        self.core, self.eng, self.own, self.n, self.counts = core, eng, own, 0, {}
        self.last = None

    def did(self, ins, sem=None):
        sem = self.own if sem is None else sem
        ins.then_inc(sem, 1)
        key = str(sem)
        self.counts[key] = self.counts.get(key, 0) + 1
        self.last = (sem, self.counts[key])

    def drain(self, label, ins):
        self.last = self.core.drain(label, ins)

    def settle(self):
        self.eng.wait_ge(*self.last)


def bc(ap, axis, shape):
    return ap.unsqueeze(axis).to_broadcast([P, *shape])


def norm_vector(k, v, n, b, bias=None):
    nc = k.nc
    ts = range(b * TB, (b + 1) * TB)
    for t in ts:
        v.did(nc.vector.bn_stats(k.stats[:, t, :], k.x[:, t, :]))
    v.settle()
    for t in ts:
        v.did(nc.vector.bn_aggr(k.mv[:, t, :], k.stats[:, t, :]), k.var_ready if t == ts[-1] else None)
    if bias is not None:
        output_bias_vector(k, v, n, b, bias)
    v.eng.wait_ge(k.rstd_ready, B * n + b + 1)
    for t in ts:
        v.did(nc.vector.tensor_scalar(k.xn[:, t, :], k.x[:, t, :], k.mv[:, t, 0:1], k.rstd[:, t:t + 1],
                                      ALU.subtract, ALU.mult), k.normed)


def output_bias_vector(k, v, n, b, bias):
    cs = slice(b * TB, (b + 1) * TB)
    v.did(k.nc.vector.scalar_tensor_tensor(out=k.xb[:, cs, :], in0=bc(bias, 1, [TB, D]), scalar=k.gates[:, n:n + 1],
                                           in1=k.x[:, cs, :], op0=ALU.mult, op1=ALU.add))


def norm_pool(k, g, n, b):
    nc = k.nc
    rstd = k.rstd[:, b * TB:(b + 1) * TB]
    g.eng.wait_ge(k.var_ready, B * n + b + 1)
    g.did(nc.gpsimd.tensor_scalar_add(rstd, k.mv[:, b * TB:(b + 1) * TB, 1], EPS))
    g.settle()
    g.did(nc.gpsimd.tensor_tensor(rstd, rstd, k.w("const", "neg_half")[:, 0:TB], ALU.pow), k.rstd_ready)


def norm_tensor(k, pe, n, b):
    ps = k.open(pe, ("xnT", n, b))
    for i in range(TB):
        t = b * TB + i
        pe.wait_ge(k.normed, n * NT + t + 1)
        last = k.nc.tensor.transpose(ps[:, i * P:(i + 1) * P], k.xn[:, t, :], k.w("const", "ident"))
    k.fill(("xnT", n, b), last)


def norm_scalar(k, a, n, b):
    ps = k.filled(a.eng, ("xnT", n, b))
    a.drain(("xnT", n, b), k.nc.scalar.activation(k.xnT[:, b * S:(b + 1) * S], ps[:, :], ACT.Copy))


def wait_xnT(k, eng, n, b):
    k.drained(eng, ("xnT", n, b))


def residual_vector(k, v, n, b, base, gate=None):
    v.eng.wait_ge(k.acc_filled, 2 * acc_use(n) + b + 1)
    cs = slice(b * TB, (b + 1) * TB)
    ins = k.nc.vector.scalar_tensor_tensor(
        out=k.x[:, cs, :], in0=k.acc[b][:, :].rearrange("p (t d) -> p t d", t=TB),
        scalar=k.gates[:, n:n + 1] if gate is None else gate, in1=base[:, cs, :], op0=ALU.mult, op1=ALU.add)
    v.did(ins, k.residual_done)
    v.settle()


ACC_USERS = [0, 1, 2, 4, 5, 6, 7]


def acc_use(n):
    return ACC_USERS.index(n)


def open_acc(k, pe, n):
    if acc_use(n):
        pe.wait_ge(k.residual_done, 2 * acc_use(n))


HW = 160
NPAIR = H // 2
NBLK = H * HW // P
BLK_JOB = 4
GROUPS3 = [(0, 3), (3, 6), (6, 9), (9, 12), (12, 14), (14, 16)]
TILE_ORDER = [("s", 0), ("s", 1), ("s", 2), ("pT", 0), ("s", 3), ("pT", 1), ("s", 4), ("pT", 2), ("s", 5), ("pT", 3), ("pT", 4)]
VW_JOBS = [(5 * i + a, 5 * i + z) for i in range(NBLK // 5) for a, z in ((0, 3), (3, 5))]


def folded_blocks(j):
    out, row = [], 0
    while row < P:
        at = j * P + row
        pair, col = divmod(at, 2 * HW)
        n = min(P - row, 2 * HW - col)
        out.append((row, row + n, pair, col))
        row += n
    return out


def fold64_jobs(kind):
    L = "L3x"
    if kind in ("k", "v"):
        return [(L, kind, c) for c in range(NPAIR)]
    if kind == "g":
        return [(L, "g", h) for h in range(H)]
    return [(L, "vw", kind, i) for i in range(len(VW_JOBS))]


def attention64_jobs(L):
    scores = lambda t: [(L, "s", t, g) for g in range(len(GROUPS3))]
    jobs = [("xnT", 6, 0)] + scores(0) + [("xnT", 6, 1)]
    for t in range(NT):
        jobs += [(L, kind, t + (kind == "s"), i) for kind, i in TILE_ORDER if kind == "pT" or t + 1 < NT]
    return jobs


class Attention64:

    def __init__(self, k):
        self.L, self.n, self.scale = "L3x", 6, 64.0 ** -0.5
        at = PLACE["L3x"] + WIDTH["L3x"]
        self.kT = k.cols(at, [NPAIR, NK])
        at += NPAIR * NK
        self.vbd = k.cols(at, [NPAIR, B, 2, HW])
        assert at + NPAIR * B * 2 * HW <= ARENA
        at = PLACE["L1f"]
        self.wk = k.cols(at, [B, H, M])
        at += B * H * M
        self.vw = [k.cols(at, [NBLK, D]), k.cols(PLACE["L2f"], [NBLK, D])]
        assert at + NBLK * D <= PLACE["L2x"]
        self.vw_made = k.cols(2560, [NBLK, D])
        assert 2560 + NBLK * D <= PLACE["L1f"]
        at = PLACE["L2f"] + NBLK * D
        self.p = k.cols(at, [2, H, HW])
        at += 2 * H * HW
        self.pT = k.cols(at, [2, NBLK, P])
        assert at + 2 * NBLK * P <= ARENA


def fold64_pool(k, g, A):
    g.eng.wait_ge(k.dram_zeroed, 48)
    for half in range(2):
        g.did(k.nc.gpsimd.memset(A.vbd[:, half * 4:half * 4 + 4, :, :, :], 0.0), k.zeroed if half else None)


def attention64_pool(k, g, A):
    g.eng.wait_ge(k.acc_filled, 2 * acc_use(5) + 2)
    g.settle()
    g.did(k.nc.gpsimd.memset(A.p[:, :, :, M:HW].rearrange("p a h m -> p (a h) m"), 0.0), k.zeroed)


def project64_tensor(k, pe, A, kind):
    nc, L = k.nc, A.L
    pe.wait_ge(k.loaded[L], 16)
    for c in range(NPAIR):
        ps = k.open(pe, (L, kind, c))
        k.fill((L, kind, c), nc.tensor.matmul(ps[:, 0:NK], k.w(L, "W" + kind)[:, c * P:(c + 1) * P], k.w("ctx", "ctxT"),
                                              start=True, stop=True))


def fold_keys_tensor(k, pe, A):
    nc, L = k.nc, A.L
    for h in range(H):
        k.drained(pe, (L, "k", h // 2))
        ps = k.open(pe, (L, "g", h))
        k.fill((L, "g", h), nc.tensor.matmul(ps[:, 0:NK], k.w(L, "WqT")[:, h * P:(h + 1) * P], A.kT[:, h // 2, :],
                                             start=True, stop=True))


def fold_values_tensor(k, pe, A, b):
    nc, L = k.nc, A.L
    for i, (first, end) in enumerate(VW_JOBS):
        ps = k.open(pe, (L, "vw", b, i))
        for j in range(first, end):
            at = (j - first) * D
            for row, last_row, c, col in folded_blocks(j):
                k.drained(pe, (L, "v", c))
                last = nc.tensor.matmul(ps[row:last_row, at:at + D],
                                        A.vbd[:, c, b, :, :].rearrange("p h m -> p (h m)")[:, col:col + last_row - row],
                                        k.w(L, "Wo")[:, c * P:(c + 1) * P], start=True, stop=True)
        k.fill((L, "vw", b, i), last)


def project64_scalar(k, a, A, kind):
    nc, L = k.nc, A.L
    if kind == "v":
        a.eng.wait_ge(k.zeroed, ZEROED3)
    for c in range(NPAIR):
        ps = k.filled(a.eng, (L, kind, c))
        if kind == "k":
            a.drain((L, kind, c), nc.scalar.activation(A.kT[:, c, :], ps[:, 0:NK], ACT.Copy))
        else:
            src = ps[:, 0:NK].rearrange("p (b m) -> p b m", b=B)
            a.did(nc.scalar.activation(A.vbd[0:64, c, :, 0, 0:M], src[0:64], ACT.Copy))
            a.drain((L, kind, c), nc.scalar.activation(A.vbd[64:P, c, :, 1, 0:M], src[64:P], ACT.Copy))


def fold_keys_scalar(k, a, A):
    nc, L = k.nc, A.L
    for h in range(H):
        ps = k.filled(a.eng, (L, "g", h))
        a.drain((L, "g", h), nc.scalar.activation(A.wk[:, :, h, :], ps[:, 0:NK].rearrange("p (b m) -> p b m", b=B),
                                                  ACT.Copy, scale=A.scale))


def fold_values_scalar(k, a, A):
    nc, L = k.nc, A.L
    for i, (first, end) in enumerate(VW_JOBS):
        ps = k.filled(a.eng, (L, "vw", 1, i))
        a.drain((L, "vw", 1, i), nc.scalar.activation(A.vw_made[:, first:end, :].rearrange("p j d -> p (j d)"),
                                                      ps[:, 0:(end - first) * D], ACT.Copy))


def fold_values_vector(k, v, A):
    nc, L = k.nc, A.L
    for i, (first, end) in enumerate(VW_JOBS):
        ps = k.filled(v.eng, (L, "vw", 0, i))
        v.drain((L, "vw", 0, i), nc.vector.tensor_copy(A.vw[0][:, first:end, :].rearrange("p j d -> p (j d)"),
                                                       ps[:, 0:(end - first) * D]))


def folded_store_sync(k, sp, A):
    for i in range(len(VW_JOBS)):
        k.drained(sp, (A.L, "vw", 1, i))
    sp.dma_start(k.vw_rows, A.vw_made.rearrange("p j d -> p (j d)")).then_inc(k.vw_stored, 16)


def folded_load_sync(k, sp, A):
    sp.wait_ge(k.vw_stored, 16)
    sp.dma_start(A.vw[1].rearrange("p j d -> p (j d)"), k.vw_rows).then_inc(k.vw_loaded, 16)


ZEROED3 = 4


def attention64_tensor(k, pe, A):
    nc, L = k.nc, A.L

    def scores(t, g):
        b = t // TB
        wait_xnT(k, pe, A.n, b)
        h0, h1 = GROUPS3[g]
        if t == 0:
            for h in range(h0, h1):
                k.drained(pe, (L, "g", h))
        ps = k.open(pe, (L, "s", t, g))
        k.fill((L, "s", t, g), nc.tensor.matmul(ps[:, 0:(h1 - h0) * M], k.xnT[:, t * P:(t + 1) * P],
                                                A.wk[:, b, h0:h1, :].rearrange("p h m -> p (h m)"), start=True, stop=True))

    def turn(t, i):
        p = A.p[:, t % 2, :, :].rearrange("p h m -> p (h m)")
        ps = k.open(pe, (L, "pT", t, i))
        last_head = ((i + 1) * BLK_JOB * P - 1) // HW
        groups = next(g for g, (h0, h1) in enumerate(GROUPS3) if last_head < h1) + 1
        pe.wait_ge(k.p64_ready, t * len(GROUPS3) + groups)
        for j in range(BLK_JOB):
            at = (i * BLK_JOB + j) * P
            last = nc.tensor.transpose(ps[:, j * P:(j + 1) * P], p[:, at:at + P], k.w("const", "ident"))
        k.fill((L, "pT", t, i), last)

    def values(t):
        b, i = divmod(t, TB)
        for j in range(NBLK):
            if j % BLK_JOB == 0:
                k.drained(pe, (L, "pT", t, j // BLK_JOB))
            last = nc.tensor.matmul(k.acc[b][:, i * D:(i + 1) * D], A.pT[:, t % 2, j, :], A.vw[b][:, j, :],
                                    start=(j == 0), stop=(j == NBLK - 1))
        last.then_inc(k.values_done if i < TB - 1 else k.acc_filled, 1)

    norm_tensor(k, pe, A.n, 0)
    for g in range(len(GROUPS3)):
        scores(0, g)
    norm_tensor(k, pe, A.n, 1)
    open_acc(k, pe, A.n)
    for i in range(len(VW_JOBS)):
        k.drained(pe, (L, "vw", 0, i))
    for t in range(NT):
        for kind, i in TILE_ORDER:
            if kind == "pT":
                turn(t, i)
            elif t + 1 < NT:
                scores(t + 1, i)
        if t == TB:
            pe.wait_ge(k.vw_loaded, 16)
        values(t)


def values_done(k, eng, t):
    b, i = divmod(t, TB)
    if i < TB - 1:
        eng.wait_ge(k.values_done, b * (TB - 1) + i + 1)
    else:
        eng.wait_ge(k.acc_filled, 2 * acc_use(6) + b + 1)


def attention64_scalar(k, a, A):
    nc, L = k.nc, A.L

    def exponentials(t):
        if t >= 2:
            k.filled(a.eng, (L, "pT", t - 2, NBLK // BLK_JOB - 1))
        for g, (h0, h1) in enumerate(GROUPS3):
            a.eng.wait_ge(k.nm_ready, 2 * 2 + t * len(GROUPS3) + g + 1)
            ps = k.filled(a.eng, (L, "s", t, g))
            for h in range(h0, h1):
                ins = nc.scalar.activation(A.p[:, t % 2, h, 0:M], ps[:, (h - h0) * M:(h - h0 + 1) * M], ACT.Exp,
                                           bias=k.nm[:, t, h:h + 1], accum_out=A_sum(k)[:, t % 2, h:h + 1])
                a.did(ins) if h < h1 - 1 else a.drain((L, "s", t, g), ins)

    norm_scalar(k, a, A.n, 0)
    exponentials(0)
    norm_scalar(k, a, A.n, 1)
    for t in range(1, NT):
        exponentials(t)


def A_sum(k):
    return k.den[:, :].rearrange("p (a h) -> p a h", a=2)


def attention64_vector(k, v, A):
    nc, L = k.nc, A.L

    def maxima(t, g):
        h0, h1 = GROUPS3[g]
        ps = k.filled(v.eng, (L, "s", t, g))
        v.did(nc.vector.tensor_reduce(k.nm[:, t, h0:h1], ps[:, 0:(h1 - h0) * M].rearrange("p (h m) -> p h m", m=M),
                                      axis=AX.X, op=ALU.max, negate=True), k.nm_ready)

    def probabilities(t):
        for g, (h0, h1) in enumerate(GROUPS3):
            k.drained(v.eng, (L, "s", t, g))
            r = k.rden[:, t % 2, h0:h1]
            v.did(nc.vector.reciprocal(r, A_sum(k)[:, t % 2, h0:h1]))
            v.settle()
            p = A.p[:, t % 2, h0:h1, 0:M]
            v.did(nc.vector.tensor_tensor(p, p, r.unsqueeze(2).to_broadcast([P, h1 - h0, M]), ALU.mult), k.p64_ready)

    def turned(t, i):
        if t >= 2:
            values_done(k, v.eng, t - 2)
        ps = k.filled(v.eng, (L, "pT", t, i))
        v.drain((L, "pT", t, i), nc.vector.tensor_copy(
            A.pT[:, t % 2, i * BLK_JOB:(i + 1) * BLK_JOB, :].rearrange("p j q -> p (j q)"), ps[:, :]))

    v.eng.wait_ge(k.zeroed, ZEROED3 + 2)
    for g in range(len(GROUPS3)):
        maxima(0, g)
    probabilities(0)
    for t in range(NT):
        for kind, i in TILE_ORDER:
            if kind == "pT":
                turned(t, i)
            elif t + 1 < NT:
                maxima(t + 1, i)
        if t + 1 < NT:
            probabilities(t + 1)


def done(k, v):
    v.settle()
    v.did(k.nc.vector.tensor_copy(k.flag[:, 2:3], k.flag[:, 0:1]), k.x_ready)


PAIRS = [(0, 0), (0, 1), (0, 2), (1, 0), (1, 1), (2, 0)]
SEC = 16
NROW = SEC * len(PAIRS)
NROWM = NROW + 4
HPAIR = H // 2


class Attention8:

    def __init__(self, k, L, n):
        self.L, self.n = L, n
        self.use = {"L0x": 0, "L2x": 1}[L]
        self.scale = 8.0 ** -0.5
        at = PLACE["L2f"] if L == "L0x" else PLACE["L0x"]
        self.ks = k.cols(at, [H, B, 160], BF16)
        at += B * H * 80
        self.qf = k.cols(at, [N])
        self.pv = k.cols(at, [2, S])
        at += N
        self.qp = k.cols(at, [3, N], BF16)
        at += 3 * N // 2
        self.h = k.cols(at, [2, N]) if L == "L0x" else None
        at = ARENA
        self.qs = k.cols(at, [HPAIR, N], BF16)
        at += HPAIR * N // 2
        self.pt = k.cols(at, [2, HG + 1, S])
        self.vr = k.cols(ARENA + ARENA_SIZE - 2048, [B, NG, P])
        self.vm = k.cols(ARENA + ARENA_SIZE - 1024, [B, H, 32])
        self.kT = k.small[:, 0:B * 160].rearrange("p (b m) -> p b m", b=B)
        self.kp = k.small[:, 320:800].bitcast(BF16).rearrange("p (a m) -> p a m", a=3)
        self.tmp = k.rt[:, :, :].rearrange("p a b -> p (a b)")
        self.o, self.oT = k.xn, k.xnT
        self.zeroed = {0: 1, 1: 5}[self.use]


def stack_keys_sync(k, sp, A):
    sp.wait_ge(k.kparts_ready, A.use + 1)
    sp.dma_start(A.ks[NROW:NROWM, :, :, :].rearrange("p h b m -> p (h b m)"), k.dram["maxrows"]).then_inc(k.k_stacked[A.use], 16)
    for s, (_, part) in enumerate(PAIRS):
        for odd in range(2):
            r = s * SEC + odd * 8
            sp.dma_start(A.ks[r:r + 8, odd::2, :, :].rearrange("d h b m -> d h (b m)"), A.kp[64 * odd:64 * (odd + 1), part, :])\
              .then_inc(k.k_stacked[A.use], 16)


NKEYDMA = 1 + 2 * len(PAIRS)


def stack_queries_sync(k, sp, A, b):
    cs = slice(b * S, (b + 1) * S)
    for s, (part, _) in enumerate(PAIRS):
        if part == 0:
            sp.wait_ge(k.q0_ready, B * A.use + b + 1)
        else:
            sp.wait_ge(k.qparts_ready, 2 * (B * A.use + b) + part)
        sp.dma_start(A.qs[s * SEC:(s + 1) * SEC, :, cs], A.qp[:, part, cs]).then_inc(k.q_stacked[A.use][b], 16)


def stack_maxima_sync(k, sp, A):
    for b in range(B):
        cs = slice(b * S, (b + 1) * S)
        k.drained(sp, (A.L, "nmT", b))
        sp.dma_start(A.qs[NROW:NROWM, :, cs], k.nmT[0:2 * H, cs]).then_inc(k.m_stacked[A.use][b], 16)


def attention8_prep_pool(k, g, A):
    nc = k.nc
    if A.use:
        g.eng.wait_ge(k.acc_filled, 2 * acc_use(2) + 2)
    g.did(nc.gpsimd.memset(A.vr[:, :, :], 0.0))
    g.did(nc.gpsimd.memset(A.vm[:, :, :, :], 0.0))
    g.settle()
    g.did(nc.gpsimd.memset(A.vm[:, :, :, 8:9], 1.0), k.zeroed)


def attention8_prep_tensor(k, pe, A):
    nc, L = k.nc, A.L
    pe.wait_ge(k.loaded["ctx"], 16)
    pe.wait_ge(k.loaded[L], 16)
    ctxT = k.w("ctx", "ctxT")
    ps = k.open(pe, (L, "k"))
    k.fill((L, "k"), nc.tensor.matmul(ps[:, 0:NK], k.w(L, "Wk"), ctxT, start=True, stop=True))
    for b in range(B):
        for kind, keys in (("v", ctxT[:, b * M:b * M + P]), ("vr", k.w("ctx", "ctx_rem")[:, b * P:(b + 1) * P])):
            ps = k.open(pe, (L, kind, b))
            k.fill((L, kind, b), nc.tensor.matmul(ps[:, 0:P], keys, k.w(L, "Wv"), start=True, stop=True))


def attention8_keys_vector(k, v, A):
    nc, L = k.nc, A.L
    if A.use:
        v.did(nc.vector.memset(A.ks[:, :, :, :], 0.0))
    v.eng.wait_ge(k.loaded[L], 16)
    v.did(nc.vector.tensor_scalar(k.bqs[:, 0:1], k.w(L, "bq"), A.scale, None, ALU.mult), k.bias_ready)
    ps = k.filled(v.eng, (L, "k"))
    v.did(nc.vector.memset(A.kT[:, :, M:160], 0.0))
    v.drain((L, "k"), nc.vector.tensor_scalar(A.kT[:, :, 0:M], ps[:, 0:NK].rearrange("p (b m) -> p b m", b=B), k.w(L, "bk"), None, ALU.add))
    v.settle()
    three_parts(k, v, k.small[:, 0:320], [A.kp[:, i, :] for i in range(3)], [A.tmp[:, 0:320]], k.kparts_ready)


def attention8_values_vector(k, v, A):
    nc, L = k.nc, A.L
    v.eng.wait_ge(k.zeroed, A.zeroed)
    v.eng.wait_ge(k.loaded["rows"], 16)
    rem = k.w("const", "rem_rows")
    bv = k.w("rows", L[:2] + "_bv")
    for b in range(B):
        ps = k.filled(v.eng, (L, "v", b))
        v.drain((L, "v", b), nc.vector.tensor_tensor(A.vm[:, b, :, 0:8], ps[:, 0:P].rearrange("p (h d) -> p h d", h=H),
                                                     bv.rearrange("p (h d) -> p h d", h=H), ALU.add))
        ps = k.filled(v.eng, (L, "vr", b))
        full = A.tmp[:, 320 + b * P:320 + (b + 1) * P]
        v.drain((L, "vr", b), nc.vector.tensor_tensor(full, ps[:, 0:P], bv, ALU.add))
        v.settle()
        for j in range(HG):
            dst = A.vr[:, b, :, 32 * j:32 * (j + 1)]
            src = full.rearrange("p (g j d) -> p g j d", g=NG, j=HG)[:, :, j, :]
            v.did(nc.vector.tensor_scalar(dst[:, :, 0:8], src, rem[:, j:j + 1], None, ALU.mult))
            v.did(nc.vector.tensor_copy(dst[:, :, 8:9], bc(rem[:, j:j + 1], 1, [NG, 1])))
    v.settle()
    v.did(nc.vector.tensor_copy(k.flag[:, 0:1], rem[:, 0:1]), k.v_ready)


def attention8_tensor(k, pe, A):
    nc, L = k.nc, A.L

    def queries(b):
        wait_xnT(k, pe, A.n, b)
        ps = k.open(pe, (L, "q", b))
        k.fill((L, "q", b), nc.tensor.matmul(ps[:, :], k.w(L, "Wq"), k.xnT[:, b * S:(b + 1) * S], start=True, stop=True))

    norm_tensor(k, pe, A.n, 0)
    queries(0)
    norm_tensor(k, pe, A.n, 1)
    pe.wait_ge(k.k_stacked[A.use], 16 * NKEYDMA)

    def scores(t, p):
        b = t // TB
        pe.wait_ge(k.q_stacked[A.use][b], 16 * len(PAIRS))
        ps = k.open(pe, (L, "s", t, p))
        k.fill((L, "s", t, p), nc.tensor.matmul(ps[:, 0:2 * M], A.qs[0:NROW, p, t * P:(t + 1) * P],
                                                A.ks[0:NROW, 2 * p:2 * p + 2, b, 0:M], start=True, stop=True))

    def minus_max(b):
        ps = k.open(pe, (L, "nmT", b))
        if A.use == 0:
            pe.wait_ge(k.loaded["sel"], 16)
        pe.wait_ge(k.nm_ready, 2 * A.use + b + 1)
        view = ps[:, :].bitcast(BF16)
        for i in range(TB):
            last = nc.tensor.transpose(view[:, i * P:(i + 1) * P], k.mpad[:, b * TB + i, :], k.w("sel", "ident"))
        k.fill((L, "nmT", b), last)

    def scores_T(b, g):
        pe.wait_ge(k.m_stacked[A.use][b], 16)
        queries = slice(b * S, (b + 1) * S)
        for j in range(HG):
            h = HG * g + j
            ps = k.open(pe, (L, "st", b, g, j))
            k.fill((L, "st", b, g, j), nc.tensor.matmul(ps[:, :], A.ks[0:NROWM, h, b, 0:P], A.qs[0:NROWM, h // 2, queries],
                                                        start=True, stop=True))
            for tile, p in late_scores(b, g, j):
                scores(tile, p)
        ps = k.open(pe, (L, "sr", b, g))
        for j in range(HG):
            h = HG * g + j
            last = nc.tensor.matmul(ps[HP * j:HP * (j + 1), :], A.ks[0:NROWM, h, b, P:160], A.qs[0:NROWM, h // 2, queries],
                                    start=True, stop=True)
        k.fill((L, "sr", b, g), last)

    def values(n):
        b, g = steps[n]
        for j in range(HG):
            k.drained(pe, (L, "st", b, g, j))
        k.drained(pe, (L, "sr", b, g))
        pt = A.pt[:, n % 2]
        ps = k.open(pe, (L, "pv", b, g))
        nc.tensor.matmul(ps[:, :], A.vr[:, b, g, :], pt[:, HG, :], start=True, stop=False, skip_group_check=True)
        for j in range(HG):
            last = nc.tensor.matmul(ps[HP * j:HP * (j + 1), :], A.vm[:, b, HG * g + j, :], pt[:, j, :], start=False, stop=True,
                                    skip_group_check=True)
        k.fill((L, "pv", b, g), last)

    def turn(n):
        b, g = steps[n]
        k.drained(pe, (L, "pv", b, g))
        ps = k.open(pe, (L, "ot", b, g))
        for i in range(TB):
            last = nc.tensor.transpose(ps[:, i * P:(i + 1) * P], A.pv[:, n % 2, i * P:(i + 1) * P], k.w("const", "ident"))
        k.fill((L, "ot", b, g), last)

    def turn_outputs(b):
        pe.wait_ge(k.o_ready, B * A.use + b + 1)
        ps = k.open(pe, (L, "oT", b))
        for i in range(TB):
            last = nc.tensor.transpose(ps[:, i * P:(i + 1) * P], A.o[:, b * TB + i, :], k.w("const", "ident"))
        k.fill((L, "oT", b), last)

    def hidden(b):
        k.drained(pe, (L, "oT", b))
        for c in range(2 if L == "L0x" else 0):
            ps = k.open(pe, (L, "h", c, b))
            k.fill((L, "h", c, b), nc.tensor.matmul(ps[:, :], k.w(L, "W1")[:, c * P:(c + 1) * P],
                                                    A.oT[:, b * S:(b + 1) * S], start=True, stop=True))

    def project(b):
        for c in range(2 if L == "L0x" else 0):
            k.drained(pe, (L, "h", c, b))
        for i in range(TB):
            t = b * TB + i
            out = k.acc[b][:, i * D:(i + 1) * D]
            if L == "L0x":
                for c in range(2):
                    last = nc.tensor.matmul(out, A.h[:, c, t * P:(t + 1) * P], k.w(L, "W2")[:, c * D:(c + 1) * D],
                                            start=(c == 0), stop=(c == 1))
            else:
                last = nc.tensor.matmul(out, A.oT[:, t * P:(t + 1) * P], k.w(L, "Wo"), start=True, stop=True)
        last.then_inc(k.acc_filled, 1)

    for t in range(TB):
        if t == QUERY_TILE[L]:
            queries(1)
        for p in range(HPAIR):
            scores(t, p)
    for t, p in BEFORE_TURN:
        scores(t, p)
    minus_max(0)
    for t, p in AFTER_TURN:
        scores(t, p)
    pe.wait_ge(k.v_ready, A.use + 1)
    steps = [(b, g) for b in range(B) for g in range(NG)]
    scores_T(*steps[0])
    for n in range(len(steps)):
        if n + 1 < len(steps):
            scores_T(*steps[n + 1])
        if n:
            turn(n - 1)
            if L == "L0x":
                l1x_prep_tensor(k, pe, n - 1)
        if n == TAIL_STEP:
            turn_outputs(0)
        if n == TAIL_STEP + 1:
            hidden(0)
        if n == TAIL_STEP + 2:
            open_acc(k, pe, A.n)
            project(0)
        values(n)
        if n == 1:
            minus_max(1)
    turn(len(steps) - 1)
    turn_outputs(1)
    hidden(1)
    project(1)


def attention8_scalar(k, a, A):
    nc, L = k.nc, A.L
    a.eng.wait_ge(k.bias_ready, {0: 1, 1: 3}[A.use])
    if A.use:
        a.eng.wait_ge(k.vw_stored, 16)
    for b in range(B):
        norm_scalar(k, a, A.n, b)
        ps = k.filled(a.eng, (L, "q", b))
        cs = slice(b * S, (b + 1) * S)
        a.did(nc.scalar.activation(A.qp[:, 0, cs], ps[:, :], ACT.Identity, bias=k.bqs[:, 0:1], scale=A.scale), k.q0_ready)
        a.drain((L, "q", b), nc.scalar.activation(A.qf[:, cs], ps[:, :], ACT.Identity, bias=k.bqs[:, 0:1], scale=A.scale))
    def minus_max(b):
        ps = k.filled(a.eng, (L, "nmT", b))
        a.drain((L, "nmT", b), nc.scalar.activation(k.nmT[:, b * S:(b + 1) * S], ps[:, :].bitcast(BF16)[:, 0:S], ACT.Copy))

    def outputs(b):
        ps = k.filled(a.eng, (L, "oT", b))
        a.drain((L, "oT", b), nc.scalar.activation(A.oT[:, b * S:(b + 1) * S], ps[:, :], ACT.Copy))

    def hidden(b):
        for c in range(2 if L == "L0x" else 0):
            ps = k.filled(a.eng, (L, "h", c, b))
            a.drain((L, "h", c, b), nc.scalar.activation(A.h[:, c, b * S:(b + 1) * S], ps[:, :], ACT.Relu,
                                                         bias=k.w(L, "b1")[:, c:c + 1]))

    minus_max(0)
    for b in range(B):
        for g in range(NG):
            step = b * NG + g
            if step == 3:
                minus_max(1)
            if step == TAIL_STEP + 2:
                outputs(0)
            if step >= 2:
                k.filled(a.eng, (L, "pv", *divmod(step - 2, NG)))
            for j in range(HG + 1):
                label = (L, "st", b, g, j) if j < HG else (L, "sr", b, g)
                ps = k.filled(a.eng, label)
                a.drain(label, nc.scalar.activation(A.pt[:, step % 2, j, :], ps[:, :], ACT.Exp))
    hidden(0)
    outputs(1)
    hidden(1)


def attention8_queries_vector(k, v, A, b):
    nc = k.nc
    cs = slice(b * S, (b + 1) * S)
    k.drained(v.eng, (A.L, "q", b))
    v.did(nc.vector.tensor_tensor(A.qf[:, cs], A.qf[:, cs], A.qp[:, 0, cs], ALU.subtract))
    v.settle()
    v.did(nc.vector.tensor_copy(A.qp[:, 1, cs], A.qf[:, cs]), k.qparts_ready)
    v.settle()
    v.did(nc.vector.tensor_tensor(A.qp[:, 2, cs], A.qf[:, cs], A.qp[:, 1, cs], ALU.subtract), k.qparts_ready)


def attention8_vector(k, v, A):
    nc, L = k.nc, A.L

    def maximum(t, p):
        ps = k.filled(v.eng, (L, "s", t, p))
        v.drain((L, "s", t, p), nc.vector.tensor_reduce(
            k.nm[:, t, 2 * p:2 * p + 2], ps[:, 0:2 * M].rearrange("p (h m) -> p h m", h=2), axis=AX.X, op=ALU.max, negate=True))

    def minus_max(b):
        v.settle()
        ts = slice(b * TB, (b + 1) * TB)
        by_parity = k.nm[:, ts, :].rearrange("p t (h odd) -> p t odd h", odd=2)
        high, low = (k.mpad[:, ts, i * H:(i + 1) * H].rearrange("p t (odd h) -> p t odd h", odd=2) for i in range(2))
        v.did(nc.vector.tensor_copy(high, by_parity))
        v.settle()
        v.did(nc.vector.tensor_tensor(low, by_parity, high, ALU.subtract), k.nm_ready)

    def normalise(n):
        b, g = divmod(n, NG)
        ps = k.filled(v.eng, (L, "ot", b, g))
        src = ps[:, :].rearrange("p (i j d) -> p i j d", i=TB, j=HG)
        r = k.den[:, 0:TB * HG].rearrange("p (i j) -> p i j", i=TB)
        v.settle()
        v.did(nc.vector.reciprocal(r, src[:, :, :, 8]))
        v.settle()
        dst = A.o[:, b * TB:(b + 1) * TB, g * 32:(g + 1) * 32].rearrange("p i (j d) -> p i j d", j=HG)
        v.drain((L, "ot", b, g), nc.vector.tensor_tensor(dst, src[:, :, :, 0:8], r.unsqueeze(3).to_broadcast([P, TB, HG, 8]), ALU.mult))
        if g == NG - 1:
            v.settle()
            v.did(nc.vector.tensor_copy(k.flag[:, 1:2], k.flag[:, 0:1]), k.o_ready)

    for t in range(TB):
        if t == QUERY_TILE[L]:
            attention8_queries_vector(k, v, A, 1)
        for p in range(HPAIR):
            maximum(t, p)
    minus_max(0)
    for t, p in BEFORE_TURN + AFTER_TURN + late_scores(0, 0):
        maximum(t, p)
    for n in range(B * NG):
        if n + 1 < LATE_GROUPS:
            for t, p in late_scores(0, n + 1):
                maximum(t, p)
        if n == 1:
            minus_max(1)
        if n:
            normalise(n - 1)
        ps = k.filled(v.eng, (L, "pv", *divmod(n, NG)))
        if n >= 2:
            k.filled(v.eng, (L, "ot", *divmod(n - 2, NG)))
        v.drain((L, "pv", *divmod(n, NG)), nc.vector.tensor_copy(A.pv[:, n % 2, :], ps[:, :]))
        if L == "L0x" and n < B * NG - 1:
            l1x_prep_vector(k, v, n)
    normalise(B * NG - 1)
    if L == "L0x":
        l1x_prep_vector(k, v, B * NG - 1)


class Moe:

    def __init__(self, k, L, n, chunks, routed):
        self.L, self.n, self.chunks, self.routed = L, n, chunks, routed
        self.topk = 4 if L == "L0f" else 2
        self.use = 0 if L == "L0f" else 1
        self.h = k.cols(ARENA, [chunks, N])
        self.sg = k.small[:, 0:1024].rearrange("p (a b) -> p a b", a=2)

    def part(self, k, kind, c):
        if self.L == "L0f" and c >= self.routed:
            kind, c = {"gate": "sgate", "up": "sup", "down": "sdown"}[kind], c - self.routed
        return k.w(self.L, kind)[:, c * P:(c + 1) * P]


ROUTERS = ["L0f", "L1f", "L2f", "L3f"]


def logits_tensor(k, pe, L, n, experts=E8):
    ps = k.open(pe, (L, "logits"))
    pe.wait_ge(k.loaded[L], 16)
    for t in range(NT):
        wait_xnT(k, pe, n, t // TB)
        last = k.nc.tensor.matmul(ps[:, t * experts:(t + 1) * experts], k.xnT[:, t * P:(t + 1) * P], k.w(L, "Wr"),
                                  start=True, stop=True)
    k.fill((L, "logits"), last)


def softmax_scalar(k, a, L, experts=E8):
    a.eng.wait_ge(k.l_ready, ROUTERS.index(L) + 1)
    w = NT * experts
    a.did(k.nc.scalar.activation(k.rt[:, 0, 0:w], k.rt[:, 0, 0:w], ACT.Exp), k.exp_ready)
    preload(k, a, {"L0f": ACT.Silu, "L1f": ACT.Copy, "L2f": ACT.Gelu, "L3f": ACT.Silu}[L])


def softmax_vector(k, v, L, experts=E8):
    nc = k.nc
    w = NT * experts
    ps = k.filled(v.eng, (L, "logits"))
    three = lambda ap: ap.rearrange("p (t e) -> p t e", t=NT)
    src = three(ps[:, 0:w])
    ex = three(k.rt[:, 0, 0:w])
    v.did(nc.vector.tensor_reduce(k.m8[:, :], src, axis=AX.X, op=ALU.max, negate=True))
    v.settle()
    v.drain((L, "logits"), nc.vector.tensor_tensor(ex, src, bc(k.m8[:, :], 2, [NT, experts]), ALU.add))
    v.settle()
    v.did(nc.vector.tensor_copy(k.flag[:, 3:4], k.flag[:, 0:1]), k.l_ready)
    v.eng.wait_ge(k.exp_ready, ROUTERS.index(L) + 1)
    v.did(nc.vector.tensor_reduce(k.s8[:, :], ex, axis=AX.X, op=ALU.add))
    v.settle()
    v.did(nc.vector.reciprocal(k.r8[:, :], k.s8[:, :]))
    v.settle()
    v.did(nc.vector.tensor_tensor(three(k.rt[:, 1, 0:w]), ex, bc(k.r8[:, :], 2, [NT, experts]), ALU.mult))
    v.settle()


def rank_vector(k, v, scores):
    nc = k.nc
    s = scores.rearrange("p (t e) -> p t e", t=NT)
    four = lambda ap: ap.rearrange("p (t e f) -> p t e f", t=NT, e=E8)
    other = s.unsqueeze(2).to_broadcast([P, NT, E8, E8])
    own = s.unsqueeze(3).to_broadcast([P, NT, E8, E8])
    gt, eq = four(k.cmp[:, 0, :]), four(k.cmp[:, 1, :])
    v.did(nc.vector.tensor_tensor(gt, other, own, ALU.is_gt))
    v.did(nc.vector.tensor_tensor(eq, other, own, ALU.is_equal))
    v.settle()
    earlier = k.w("const", "earlier").unsqueeze(1).to_broadcast([P, NT, 64])
    flat = lambda ap: ap.rearrange("p (t e) -> p t e", t=NT)
    v.did(nc.vector.tensor_tensor(flat(k.cmp[:, 1, :]), flat(k.cmp[:, 1, :]), earlier, ALU.mult))
    v.settle()
    v.did(nc.vector.tensor_tensor(k.cmp[:, 0, :], k.cmp[:, 0, :], k.cmp[:, 1, :], ALU.add))
    v.settle()
    v.did(nc.vector.tensor_reduce(k.rt[:, 3, 0:64], k.cmp[:, 0, :].rearrange("p (c f) -> p c f", f=E8), axis=AX.X, op=ALU.add))
    v.settle()


def three_parts(k, v, src, dst, tmp, last_sem):
    nc = k.nc
    v.did(nc.vector.tensor_copy(dst[0], src))
    v.settle()
    v.did(nc.vector.tensor_tensor(tmp[0], src, dst[0], ALU.subtract))
    v.settle()
    v.did(nc.vector.tensor_copy(dst[1], tmp[0]))
    v.settle()
    v.did(nc.vector.tensor_tensor(dst[2], tmp[0], dst[1], ALU.subtract), last_sem)


def moe_vector(k, v, A):
    nc, L = k.nc, A.L
    order = moe_order(A)
    def hidden(c, b):
        cs = slice(b * S, (b + 1) * S)
        turn = order.index((c, b))
        k.drained(v.eng, (L, "g", c, b))
        ps = k.filled(v.eng, (L, "u", c, b))
        v.drain((L, "u", c, b), nc.vector.tensor_tensor(A.h[:, c, cs], A.sg[:, turn % 2, :], ps[:, :], ALU.mult))
        if c < A.routed:
            v.settle()
            ps = k.filled(v.eng, (L, "w", c, b))
            v.drain((L, "w", c, b), nc.vector.tensor_tensor(A.h[:, c, cs], A.h[:, c, cs], ps[:, :], ALU.mult))

    shared = A.chunks - A.routed
    for turn in range(shared):
        hidden(*order[turn])
    softmax_vector(k, v, L)
    hidden(*order[shared])
    probs, w = k.rt[:, 1, 0:64], k.rt[:, 2, 0:64]
    scores = probs
    if L == "L0f":
        scores = k.rt[:, 4, 0:64]
        v.did(nc.vector.tensor_scalar(scores, probs, k.w("rows", "rb"), None, ALU.add))
        v.settle()
    rank_vector(k, v, scores)
    for turn in range(shared + 1, 2 * shared):
        hidden(*order[turn])
    v.settle()
    v.did(nc.vector.scalar_tensor_tensor(out=w, in0=k.rt[:, 3, 0:64], scalar=float(A.topk), in1=probs,
                                         op0=ALU.is_lt, op1=ALU.mult))
    v.settle()
    three = lambda ap: ap.rearrange("p (t e) -> p t e", t=NT)
    if L == "L0f":
        v.did(nc.vector.tensor_reduce(k.s8[:, :], three(w), axis=AX.X, op=ALU.add))
        v.settle()
        v.did(nc.vector.tensor_scalar(k.s8[:, :], k.s8[:, :], 1e-20, None, ALU.add))
        v.settle()
        v.did(nc.vector.reciprocal(k.r8[:, :], k.s8[:, :]))
        v.settle()
        v.did(nc.vector.tensor_tensor(three(w), three(w), bc(k.r8[:, :], 2, [NT, E8]), ALU.mult))
        v.settle()
    parts = [k.mpad[:, :, 8 * i:8 * (i + 1)] for i in range(3)]
    three_parts(k, v, three(w), parts, [three(k.rt[:, 3, 0:64])], k.w_ready)

    for turn in range(2 * shared, len(order)):
        hidden(*order[turn])
        if L == "L0f" and turn + 2 in L1X_PREP_TURNS and L1X_PREP_TURNS[turn + 2] >= B * NG:
            l1x_prep_vector(k, v, L1X_PREP_TURNS[turn + 2])


def moe_order(A):
    return [(c, b) for b in range(B) for c in range(A.routed, A.chunks)] + [(c, b) for c in range(A.routed) for b in range(B)]


def moe_scalar(k, a, A):
    nc, L = k.nc, A.L
    order = moe_order(A)
    per_batch = A.chunks - A.routed
    shared = 2 * (A.chunks - A.routed)
    preload(k, a, ACT.Silu)
    for turn, (c, b) in enumerate(order):
        if L == "L0f" and turn == max(L1X_PREP_TURNS):
            l1x_prep_scalar(k, a)
        if turn in (0, per_batch):
            norm_scalar(k, a, A.n, turn // per_batch)
        if turn == per_batch:
            softmax_scalar(k, a, L)
        if turn == shared:
            for bb in range(B):
                ps = k.filled(a.eng, (L, "wT", bb))
                a.drain((L, "wT", bb), nc.scalar.activation(k.nmT[:, bb * S:(bb + 1) * S], ps[:, :].bitcast(BF16)[:, 0:S], ACT.Copy))
        if turn >= 2:
            k.drained(a.eng, (L, "u", *order[turn - 2]))
        ps = k.filled(a.eng, (L, "g", c, b))
        a.drain((L, "g", c, b), nc.scalar.activation(A.sg[:, turn % 2, :], ps[:, :], ACT.Silu))


def moe_tensor(k, pe, A):
    nc, L = k.nc, A.L
    order = moe_order(A)
    per_batch = A.chunks - A.routed
    shared = 2 * (A.chunks - A.routed)

    def down(b, chunks, first, last_chunk):
        for c in chunks:
            k.drained(pe, (L, "w" if c < A.routed else "u", c, b))
        for i in range(TB):
            t = b * TB + i
            for c in chunks:
                last = nc.tensor.matmul(k.acc[b][:, i * D:(i + 1) * D], A.h[:, c, t * P:(t + 1) * P],
                                        A.part(k, "down", c), start=(c == first and i == 0),
                                        stop=(c == last_chunk and i == TB - 1), skip_group_check=True)
        return last

    pe.wait_ge(k.loaded[L], 16)
    for turn, (c, b) in enumerate(order):
        if L == "L0f" and turn in L1X_PREP_TURNS:
            l1x_prep_tensor(k, pe, L1X_PREP_TURNS[turn])
        if turn in (0, per_batch):
            norm_tensor(k, pe, A.n, turn // per_batch)
            wait_xnT(k, pe, A.n, turn // per_batch)
        if turn == per_batch:
            logits_tensor(k, pe, L, A.n)
        if turn == shared:
            open_acc(k, pe, A.n)
            for bb in range(B):
                down(bb, range(A.routed, A.chunks), A.routed, None)
            for bb in range(B):
                ps = k.open(pe, (L, "wT", bb))
                pe.wait_ge(k.w_ready, ROUTERS.index(L) + 1)
                for i in range(TB):
                    last = nc.tensor.transpose(ps[:, :].bitcast(BF16)[:, i * P:(i + 1) * P], k.mpad[:, bb * TB + i, :],
                                               k.w("sel", "ident"))
                k.fill((L, "wT", bb), last)
        cs = slice(b * S, (b + 1) * S)
        for kind, name in (("g", "gate"), ("u", "up")):
            ps = k.open(pe, (L, kind, c, b))
            k.fill((L, kind, c, b), nc.tensor.matmul(ps[:, :], A.part(k, name, c), k.xnT[:, cs], start=True, stop=True))
        if c < A.routed:
            ps = k.open(pe, (L, "w", c, b))
            k.drained(pe, (L, "wT", b))
            k.fill((L, "w", c, b), nc.tensor.matmul(ps[:, :], k.w("sel", L)[:, c * P:(c + 1) * P],
                                                    k.nmT[:, cs], start=True, stop=True))
    for b in range(B):
        down(b, range(A.routed), None, A.routed - 1).then_inc(k.acc_filled, 1)


WEIGHTS1 = [("d2v", 1, 128 * 96), ("img", 1, 128 * 128), ("att0", 1, 128 * 128), ("att1", 1, 128 * 128),
            ("txt", 1, 128 * 128), ("f1", 8, 512 * 256), ("f2", 4, 128 * 512)]


class L1x:

    def __init__(self, k):
        at = PLACE["L2f"] + 7168
        self.wq = k.cols(at, [17 * P], BF16)
        at += 17 * P // 2
        self.kT = k.cols(at, [2, B, 256])
        at += 1024
        self.kv = k.cols(at, [2, B, 2, P])
        at += 1024
        self.prep = k.cols(at, [2, 512])
        at += 1024
        self.ctxq = k.cols(at, [NK], BF16)
        self.hq = k.cols(PLACE["L0x"], [4, N], BF16)
        at = ARENA
        self.tmp = k.cols(at, [2, N])
        at += 2 * N
        self.xq = k.cols(at, [N], BF16)
        at += N // 2
        self.fused = k.cols(at, [N])
        at += N
        self.p = k.cols(at, [NT, 256])
        self.pT = k.cols(at + 2048, [B, 2, S])
        self.h = k.cols(at, [4, N])

    def weight(self, name):
        at = 0
        for n, blocks, _ in WEIGHTS1:
            if n == name:
                return self.wq[:, at:at + blocks * P]
            at += blocks * P


def amax_vector(k, v, name, src):
    amax_rows(k, v, src)
    amax_row(k, v, name)
    amax_scale(k, v, name)


def amax_rows(k, v, src):
    nc = k.nc
    if src is not None:
        v.did(nc.vector.tensor_reduce(k.am[:, 0:1], src, axis=AX.X, op=ALU.max, apply_absolute_value=True))
    v.settle()
    v.did(nc.vector.tensor_copy(k.am[:, 4:5], k.am[:, 0:1]), k.am_ready)


def amax_row(k, v, name):
    ps = k.filled(v.eng, ("L1x", "amT", name))
    v.drain(("L1x", "amT", name), k.nc.vector.tensor_reduce(k.m1[0:1, 0:1], ps[0:1, 0:P], axis=AX.X, op=ALU.max))


def amax_scale(k, v, name):
    nc, i = k.nc, AMAX.index(name)
    ps = k.filled(v.eng, ("L1x", "amB", name))
    v.drain(("L1x", "amB", name), nc.vector.tensor_scalar(k.sc[:, 2 * i:2 * i + 1], ps[:, 0:1], 1e-8, 1.0 / 127.0, ALU.max, ALU.mult))
    v.settle()
    v.did(nc.vector.reciprocal(k.sc[:, 2 * i + 1:2 * i + 2], k.sc[:, 2 * i:2 * i + 1]))
    v.settle()


def amax_turn(k, pe, name):
    ps = k.open(pe, ("L1x", "amT", name))
    pe.wait_ge(k.am_ready, AMAX.index(name) + 1)
    k.fill(("L1x", "amT", name), k.nc.tensor.transpose(ps[0:1, 0:P], k.am[:, 4:5], k.w("const", "ident")))


def amax_spread(k, pe, name):
    ps = k.open(pe, ("L1x", "amB", name))
    k.drained(pe, ("L1x", "amT", name))
    k.fill(("L1x", "amB", name), k.nc.tensor.matmul(ps[:, 0:1], k.w("const", "ones")[0:1, :], k.m1[0:1, 0:1], start=True, stop=True))


def amax_tensor(k, pe, name):
    amax_turn(k, pe, name)
    amax_spread(k, pe, name)


def quantise_vector(k, v, name, src, dst, tmp, sem=None):
    nc, i = k.nc, AMAX.index(name)
    v.did(nc.vector.tensor_scalar(tmp, src, k.sc[:, 2 * i + 1:2 * i + 2], MAGIC, ALU.mult, ALU.add))
    v.settle()
    v.did(nc.vector.tensor_scalar(dst, tmp, MAGIC, 127.0, ALU.subtract, ALU.min), sem)


def scale_vector(k, v, weight, name):
    w = [n for n, _, _ in WEIGHTS1].index(weight)
    i = AMAX.index(name)
    v.did(k.nc.vector.tensor_tensor(k.comb[:, w:w + 1], k.ws[:, w:w + 1], k.sc[:, 2 * i:2 * i + 1], ALU.mult))
    v.settle()
    return k.comb[:, w:w + 1]


def l1x_keys_pool(k, g):
    g.did(k.nc.gpsimd.memset(L1x(k).kT[:, :, :, M:256], 0.0), k.zeroed)


def l1x_pool(k, g):
    g.eng.wait_ge(k.x_ready, 2)
    g.did(k.nc.gpsimd.memset(L1x(k).p[:, :, M:256], 0.0), k.zeroed)


def ternary_vector(k, v, names):
    nc, T = k.nc, L1x(k)
    for turn, name in enumerate(names):
        i, blocks = next((i, blocks) for i, (n, blocks, _) in enumerate(WEIGHTS1) if n == name)
        below = T.prep[:, turn % 2, 0:blocks * P // 2].bitcast(BF16)
        v.settle()
        v.did(nc.vector.tensor_scalar(below, k.w("L1x", name), k.thr[:, 8 + i:9 + i], None, ALU.is_lt))
        v.settle()
        v.did(nc.vector.scalar_tensor_tensor(out=T.weight(name), in0=k.w("L1x", name), scalar=k.thr[:, i:i + 1],
                                             in1=below, op0=ALU.is_gt, op1=ALU.subtract))
    v.settle()


def l1x_prep_vector(k, v, step):
    nc, T = k.nc, L1x(k)
    name, turn = L1X_PREP[step]
    quantised, act = T.prep[:, 0, 0:NK], T.prep[:, 1, 0:NK]
    v.settle()
    if name == "wsum":
        v.eng.wait_ge(k.loaded["L1x"], 16)
        for i, (weight, _, _) in enumerate(WEIGHTS1):
            v.did(nc.vector.tensor_reduce(k.wabs[:, i:i + 1], k.w("L1x", weight), axis=AX.X, op=ALU.add, apply_absolute_value=True),
                  k.q_ready if i == 6 else None)
    elif (name, turn) == ("ctx", "amT"):
        ps = k.filled(v.eng, ("L1x", "wsum"))
        for a, b, count in ((0, 1, 128 * 96), (1, 5, 128 * 128), (5, 6, 512 * 256), (6, 7, 128 * 512)):
            ins = nc.vector.tensor_scalar(k.ws[:, a:b], ps[:, a:b], 1.0 / count, 1e-5, ALU.mult, ALU.max)
            v.did(ins) if b < 7 else v.drain(("L1x", "wsum"), ins)
        v.settle()
        v.did(nc.vector.tensor_scalar(k.thr[:, 0:7], k.ws[:, 0:7], 0.5, None, ALU.mult))
        v.did(nc.vector.tensor_scalar(k.thr[:, 8:15], k.ws[:, 0:7], -0.5, None, ALU.mult))
        amax_rows(k, v, k.w("ctx", "ctxT"))
        ternary_vector(k, v, ("d2v", "img"))
    elif turn == "amT":
        weight, source = {"vis": ("d2v", "ctx"), "img": ("img", "vis")}[name]
        s = scale_vector(k, v, weight, source)
        ps = k.filled(v.eng, ("L1x", name))
        v.drain(("L1x", name), nc.vector.tensor_scalar(act, ps[:, 0:NK], s, k.w("L1x", "b_" + weight), ALU.mult, ALU.add))
        v.settle()
        amax_rows(k, v, act)
        if name == "img":
            v.did(nc.vector.tensor_reduce(k.avg[:, 0:2], act.rearrange("p (b m) -> p b m", b=B), axis=AX.X, op=ALU.add))
            v.settle()
            v.did(nc.vector.tensor_scalar(k.avg[:, 0:2], k.avg[:, 0:2], 1.0 / M, None, ALU.mult))
    elif turn == "amB":
        amax_row(k, v, name)
    elif name == "kvT":
        v.eng.wait_ge(k.zeroed, 2)
        for r in range(2):
            s = scale_vector(k, v, f"att{r}", "img")
            ps = k.filled(v.eng, ("L1x", "kv", r))
            v.drain(("L1x", "kv", r), nc.vector.tensor_scalar(
                T.kT[:, r, :, 0:M], ps[:, 0:NK].rearrange("p (b m) -> p b m", b=B), s, k.w("L1x", f"b_att{r}"), ALU.mult, ALU.add))
        ternary_vector(k, v, ("f2",))
    else:
        source = {"vis": "ctx", "img": "vis", "kv": "img"}[name]
        amax_scale(k, v, source)
        quantise_vector(k, v, source, k.w("ctx", "ctxT") if source == "ctx" else act, T.ctxq, quantised, k.q_ready)
        ternary_vector(k, v, {"vis": ("att0", "att1"), "img": ("txt",), "kv": ("f1",)}[name])


def l1x_prep_tensor(k, pe, step):
    nc, T = k.nc, L1x(k)
    name, turn = L1X_PREP[step]
    if turn == "amT":
        amax_turn(k, pe, name)
    elif turn == "amB":
        amax_spread(k, pe, name)
    elif name == "wsum":
        ps = k.open(pe, ("L1x", "wsum"))
        pe.wait_ge(k.q_ready, 1)
        k.fill(("L1x", "wsum"), nc.tensor.matmul(ps[:, 0:7], k.w("const", "ones"), k.wabs[:, 0:7], start=True, stop=True))
    elif name == "kv":
        for r in range(2):
            ps = k.open(pe, ("L1x", "kv", r))
            pe.wait_ge(k.q_ready, 4)
            k.fill(("L1x", "kv", r), nc.tensor.matmul(ps[:, 0:NK], T.weight(f"att{r}"), T.ctxq, start=True, stop=True))
    elif name == "kvT":
        for r in range(2):
            for b in range(B):
                k.drained(pe, ("L1x", "kv", r))
                ps = k.open(pe, ("L1x", "kvT", r, b))
                for half in range(2):
                    last = nc.tensor.transpose(ps[:, half * P:(half + 1) * P], T.kT[:, r, b, half * P:(half + 1) * P],
                                               k.w("const", "ident"))
                k.fill(("L1x", "kvT", r, b), last)
    else:
        ps = k.open(pe, ("L1x", name))
        pe.wait_ge(k.q_ready, {"vis": 2, "img": 3}[name])
        k.fill(("L1x", name), nc.tensor.matmul(ps[:, 0:NK], T.weight({"vis": "d2v", "img": "img"}[name]), T.ctxq,
                                               start=True, stop=True))


INV_SQRT = float(D) ** -0.5


def l1x_vector(k, v):
    nc, T = k.nc, L1x(k)
    for b in range(B):
        wait_xnT(k, v.eng, 2, b)
        v.did(nc.vector.tensor_reduce(k.am[:, 2 + b:3 + b], k.xnT[:, b * S:(b + 1) * S], axis=AX.X, op=ALU.max,
                                      apply_absolute_value=True))
    v.eng.wait_ge(k.zeroed, 3)
    v.settle()
    v.did(nc.vector.tensor_reduce(k.am[:, 0:1], k.am[:, 2:4], axis=AX.X, op=ALU.max))
    amax_vector(k, v, "x", None)
    for b in range(B):
        cs = slice(b * S, (b + 1) * S)
        quantise_vector(k, v, "x", k.xnT[:, cs], T.xq[:, cs], T.tmp[:, 0, cs], k.q_ready)
    s = scale_vector(k, v, "txt", "x")
    for b in range(B):
        ps = k.filled(v.eng, ("L1x", "txt", b))
        v.drain(("L1x", "txt", b), nc.vector.tensor_scalar(T.fused[:, b * S:(b + 1) * S], ps[:, :], s, k.w("L1x", "b_txt"), ALU.mult, ALU.add))
    for r in range(2):
        for t in range(0, NT, 2):
            ps = k.filled(v.eng, ("L1x", "s", r, t))
            v.did(nc.vector.tensor_reduce(k.am[:, 2:4], ps[:, 0:2 * M].rearrange("p (i m) -> p i m", i=2), axis=AX.X, op=ALU.max))
            v.settle()
            v.did(nc.vector.tensor_scalar(k.l1s[:, 0, t:t + 2], k.am[:, 2:4], -INV_SQRT, None, ALU.mult), k.l1_bias)
            v.settle()
        for t in range(0, NT, 2):
            k.drained(v.eng, ("L1x", "s", r, t))
            v.did(nc.vector.reciprocal(k.l1s[:, 2, t:t + 2], k.l1s[:, 1, t:t + 2]))
            v.settle()
            for i in range(t, t + 2):
                v.did(nc.vector.tensor_scalar(T.p[:, i, 0:M], T.p[:, i, 0:M], k.l1s[:, 2, i:i + 1], 0.1, ALU.mult, ALU.mult), k.p_norm)
        for b in range(B):
            ps = k.filled(v.eng, ("L1x", "o", r, b))
            cs = slice(b * S, (b + 1) * S)
            v.drain(("L1x", "o", r, b), nc.vector.tensor_tensor(T.fused[:, cs], T.fused[:, cs], ps[:, :], ALU.add))
        v.settle()
    v.did(nc.vector.tensor_reduce(k.am[:, 2:3], T.fused, axis=AX.X, op=ALU.max, apply_absolute_value=True))
    v.did(nc.vector.tensor_reduce(k.am[:, 3:4], k.avg[:, 0:2], axis=AX.X, op=ALU.max, apply_absolute_value=True))
    v.settle()
    v.did(nc.vector.tensor_reduce(k.am[:, 0:1], k.am[:, 2:4], axis=AX.X, op=ALU.max))
    amax_vector(k, v, "cat", None)
    quantise_vector(k, v, "cat", k.avg[:, 0:2], k.avgq[:, 0:2], k.am[:, 2:4])
    v.settle()
    for b in range(B):
        cs = slice(b * S, (b + 1) * S)
        quantise_vector(k, v, "cat", T.fused[:, cs], T.xq[:, cs], T.tmp[:, 0, cs], k.q_ready)
    scale_vector(k, v, "f1", "cat")
    v.did(nc.vector.tensor_copy(k.flag[:, 3:4], k.flag[:, 0:1]), k.bias_ready)
    for c in range(4):
        for b in range(B):
            k.drained(v.eng, ("L1x", "f1", c, b))
            v.did(nc.vector.tensor_reduce(k.hm[:, 2 * c + b:2 * c + b + 1], T.h[:, c, b * S:(b + 1) * S], axis=AX.X,
                                          op=ALU.max))
    v.settle()
    amax_vector(k, v, "h", k.hm[:, 0:8])
    for b in range(B):
        for pair in range(2):
            cs = slice(b * S, (b + 1) * S)
            two = slice(2 * pair, 2 * pair + 2)
            quantise_vector(k, v, "h", T.h[:, two, cs], T.hq[:, two, cs], T.tmp[:, :, cs], k.q_ready)
            v.settle()
    s = scale_vector(k, v, "f2", "h")
    v.did(nc.vector.tensor_tensor(k.comb[:, 7:8], s, k.gates[:, 2:3], ALU.mult))
    v.settle()


def l1x_scalar(k, a):
    nc, T = k.nc, L1x(k)
    for r in range(2):
        for t in range(0, NT, 2):
            ps = k.filled(a.eng, ("L1x", "s", r, t))
            a.eng.wait_ge(k.l1_bias, (r * NT + t) // 2 + 1)
            if r:
                k.filled(a.eng, ("L1x", "pT", 0, t // TB, 1))
            for i in range(2):
                ins = nc.scalar.activation(T.p[:, t + i, 0:M], ps[:, i * M:(i + 1) * M], ACT.Exp, bias=k.l1s[:, 0, t + i:t + i + 1],
                                           scale=INV_SQRT, accum_out=k.l1s[:, 1, t + i:t + i + 1])
                a.did(ins) if i == 0 else a.drain(("L1x", "s", r, t), ins)
        for b in range(B):
            if r:
                k.filled(a.eng, ("L1x", "o", 0, b))
            for half in range(2):
                label = ("L1x", "pT", r, b, half)
                ps = k.filled(a.eng, label)
                a.drain(label, nc.scalar.activation(T.pT[:, b, half, :], ps[:, :], ACT.Copy))
    a.eng.wait_ge(k.bias_ready, 2)
    for c in range(4):
        for b in range(B):
            ps = k.filled(a.eng, ("L1x", "f1", c, b))
            a.drain(("L1x", "f1", c, b), nc.scalar.activation(T.h[:, c, b * S:(b + 1) * S], ps[:, :], ACT.Relu,
                                                              bias=k.w("L1x", "b_f1")[:, c:c + 1], scale=k.comb[:, 5:6]))


def l1x_prep_scalar(k, a):
    T = L1x(k)
    for r in range(2):
        for b in range(B):
            ps = k.filled(a.eng, ("L1x", "kvT", r, b))
            a.drain(("L1x", "kvT", r, b), k.nc.scalar.activation(
                T.kv[:, r, b, :, :], ps[:, 0:256].rearrange("p (i d) -> p i d", i=2), ACT.Copy))


def l1x_tensor(k, pe):
    nc, T = k.nc, L1x(k)
    amax_tensor(k, pe, "x")
    for b in range(B):
        pe.wait_ge(k.q_ready, 4 + b + 1)
        ps = k.open(pe, ("L1x", "txt", b))
        k.fill(("L1x", "txt", b), nc.tensor.matmul(ps[:, :], T.weight("txt"), T.xq[:, b * S:(b + 1) * S], start=True, stop=True))
    for r in range(2):
        for t in range(0, NT, 2):
            b = t // TB
            k.drained(pe, ("L1x", "txt", b) if r == 0 else ("L1x", "o", 0, b))
            ps = k.open(pe, ("L1x", "s", r, t))
            for i in range(2):
                last = nc.tensor.matmul(ps[:, i * M:(i + 1) * M], T.fused[:, (t + i) * P:(t + i + 1) * P], T.kT[:, r, b, 0:M], start=True, stop=True)
            k.fill(("L1x", "s", r, t), last)
        for b in range(B):
            for half in range(2):
                ps = k.open(pe, ("L1x", "pT", r, b, half))
                for i in range(TB):
                    t = b * TB + i
                    pe.wait_ge(k.p_norm, r * NT + t + 1)
                    last = nc.tensor.transpose(ps[:, i * P:(i + 1) * P], T.p[:, t, half * P:(half + 1) * P], k.w("const", "ident"))
                k.fill(("L1x", "pT", r, b, half), last)
        for b in range(B):
            ps = k.open(pe, ("L1x", "o", r, b))
            k.drained(pe, ("L1x", "kvT", r, b))
            for half in range(2):
                k.drained(pe, ("L1x", "pT", r, b, half))
                last = nc.tensor.matmul(ps[:, :], T.kv[:, r, b, half, :], T.pT[:, b, half, :], start=(half == 0), stop=(half == 1))
            k.fill(("L1x", "o", r, b), last)
    amax_tensor(k, pe, "cat")
    for c in range(4):
        for b in range(B):
            pe.wait_ge(k.q_ready, 6 + b + 1)
            ps = k.open(pe, ("L1x", "f1", c, b))
            w = T.weight("f1")
            nc.tensor.matmul(ps[:, :], w[:, c * P:(c + 1) * P], T.xq[:, b * S:(b + 1) * S], start=True, stop=False)
            k.fill(("L1x", "f1", c, b), nc.tensor.matmul(ps[:, :], w[:, 512 + c * P:512 + (c + 1) * P],
                                                         k.avgq[:, b:b + 1].to_broadcast([P, S]), start=False, stop=True))
    amax_tensor(k, pe, "h")
    open_acc(k, pe, 2)
    for b in range(B):
        pe.wait_ge(k.q_ready, 8 + 2 * (b + 1))
        for i in range(TB):
            t = b * TB + i
            for c in range(4):
                last = nc.tensor.matmul(k.acc[b][:, i * D:(i + 1) * D], T.hq[:, c, t * P:(t + 1) * P],
                                        T.weight("f2")[:, c * D:(c + 1) * D], start=(c == 0), stop=(c == 3))
        last.then_inc(k.acc_filled, 1)


ROWS1 = NSLOT + N


class L1f:

    def __init__(self, k):
        at = ARENA
        self.xg = k.cols(at, [12, D])
        at += 12 * D
        self.xgT = k.cols(at, [NSLOT])
        at += NSLOT
        self.h = k.cols(at, [2, 4, CAP])
        at += 2 * 4 * CAP
        self.eo = k.cols(at, [E8, 2, D])
        at += E8 * 2 * D
        self.y = k.cols(at, [NT, D])
        self.zeros = k.cols(PLACE["L2f"] + 12000, [1024])


def l1f_jobs_order():
    for e in range(E8):
        if e == 0:
            yield "h", 0
        if e + 1 < E8:
            yield "h", e + 1
        yield "eo", e


def l1f_vector(k, v, A2, A3):
    nc, T = k.nc, L1f(k)
    softmax_vector(k, v, "L1f")
    probs = k.rt[:, 1, 0:64]
    rank_vector(k, v, probs)
    one = k.rt[:, 2, 0:64]
    three = lambda ap: ap.rearrange("p (t e) -> p t e", t=NT)
    v.did(nc.vector.tensor_scalar(one, k.rt[:, 3, 0:64], 1.0, None, ALU.is_lt))
    v.settle()
    v.did(nc.vector.tensor_copy(k.onehot[:, :], one), k.w_ready)
    v.did(nc.vector.tensor_tensor(k.rt[:, 3, 0:64], one, probs, ALU.mult))
    v.did(nc.vector.tensor_tensor(k.rt[:, 4, 0:64], one, k.w("const", "expert_base"), ALU.mult))
    v.settle()
    v.did(nc.vector.tensor_reduce(k.m8[:, :], three(k.rt[:, 3, 0:64]), axis=AX.X, op=ALU.add))
    v.did(nc.vector.tensor_reduce(k.s8[:, :], three(k.rt[:, 4, 0:64]), axis=AX.X, op=ALU.add))
    v.settle()
    v.did(nc.vector.tensor_scalar(k.gp[:, :], k.m8[:, :], k.gates[:, 3:4], None, ALU.mult))
    ps = k.filled(v.eng, ("L1f", "count"))
    v.drain(("L1f", "count"), nc.vector.tensor_tensor(k.rt[:, 0, 0:64], ps[:, 0:64], one, ALU.mult))
    v.settle()
    v.did(nc.vector.tensor_reduce(k.r8[:, :], three(k.rt[:, 0, 0:64]), axis=AX.X, op=ALU.add))
    v.settle()
    dummy = k.w("const", "dummy_row")
    v.did(nc.vector.tensor_tensor(k.s8[:, :], k.s8[:, :], k.r8[:, :], ALU.add))
    v.settle()
    v.did(nc.vector.tensor_tensor(k.s8[:, :], k.s8[:, :], dummy, ALU.subtract))
    v.settle()
    v.did(nc.vector.scalar_tensor_tensor(out=k.s8[:, :], in0=k.r8[:, :], scalar=float(CAP), in1=k.s8[:, :], op0=ALU.is_le, op1=ALU.mult))
    v.settle()
    v.did(nc.vector.tensor_tensor(k.idx[:, :], k.s8[:, :], dummy, ALU.add), k.slots_ready)
    v.settle()
    attention8_keys_vector(k, v, A2)
    attention8_values_vector(k, v, A2)
    b2 = k.w("rows", "L1_b2")
    for e in range(E8):
        ps = k.filled(v.eng, ("L1f", "eo", e))
        v.drain(("L1f", "eo", e), nc.vector.tensor_tensor(
            T.eo[0:CT, e, :, :], ps[0:CT, 0:2 * D].rearrange("p (j d) -> p j d", j=2),
            b2[0:CT, e * D:(e + 1) * D].unsqueeze(1).to_broadcast([CT, 2, D]), ALU.add))
    fold_values_vector(k, v, A3)


def l1f_residual_vector(k, v, b):
    T = L1f(k)
    v.eng.wait_ge(k.y_loaded[b], 16 * TB)
    for t in range(b * TB, (b + 1) * TB):
        v.did(k.nc.vector.scalar_tensor_tensor(out=k.x[:, t, :], in0=T.y[:, t, :], scalar=k.gp[:, t:t + 1], in1=k.x[:, t, :],
                                               op0=ALU.mult, op1=ALU.add))
    v.settle()


def l1f_scalar(k, a, A3):
    nc, T = k.nc, L1f(k)
    softmax_scalar(k, a, "L1f")
    project64_scalar(k, a, A3, "k")
    project64_scalar(k, a, A3, "v")
    fold_values_scalar(k, a, A3)
    preload(k, a, ACT.Gelu)
    for j in range(3):
        ps = k.filled(a.eng, ("L1f", "xgT", j))
        a.drain(("L1f", "xgT", j), nc.scalar.activation(T.xgT[:, j * 512:(j + 1) * 512], ps[:, :], ACT.Copy))
    b1 = k.w("L1f", "b1")
    for e in range(E8):
        if e >= 2:
            k.filled(a.eng, ("L1f", "eo", e - 2))
        for c in range(2):
            ps = k.filled(a.eng, ("L1f", "h", e, c))
            for i in range(2):
                f = 2 * c + i
                ins = nc.scalar.activation(T.h[:, e % 2, f, :], ps[:, i * CAP:(i + 1) * CAP], ACT.Gelu, bias=b1[:, 4 * e + f:4 * e + f + 1])
                a.did(ins) if i == 0 else a.drain(("L1f", "h", e, c), ins)
    fold_keys_scalar(k, a, A3)


def l1f_tensor(k, pe, A2, A3):
    nc, T = k.nc, L1f(k)
    logits_tensor(k, pe, "L1f", 3)
    project64_tensor(k, pe, A3, "k")
    ps = k.open(pe, ("L1f", "count"))
    pe.wait_ge(k.w_ready, 2)
    nc.tensor.matmul(ps[:, 0:64], k.w("sel", "upto"), k.onehot[:, :], start=True, stop=False, skip_group_check=True)
    for t in range(NT - 1):
        rest = NT - 1 - t
        last = nc.tensor.matmul(ps[:, (t + 1) * E8:64].rearrange("p (t e) -> p t e", t=rest), k.w("sel", "ones"),
                                bc(k.onehot[:, t * E8:(t + 1) * E8], 1, [rest, E8]), start=False, stop=(t == NT - 2),
                                skip_group_check=True)
    k.fill(("L1f", "count"), last)
    project64_tensor(k, pe, A3, "v")
    attention8_prep_tensor(k, pe, A2)
    fold_values_tensor(k, pe, A3, 1)
    pe.wait_ge(k.slots_loaded, 16)
    for j in range(3):
        ps = k.open(pe, ("L1f", "xgT", j))
        for i in range(4):
            last = nc.tensor.transpose(ps[:, i * P:(i + 1) * P], T.xg[:, 4 * j + i, :], k.w("const", "ident"))
        k.fill(("L1f", "xgT", j), last)
    for j in range(3):
        k.drained(pe, ("L1f", "xgT", j))
    w1, w2 = k.w("L1f", "w1"), k.w("L1f", "w2")
    for kind, e in l1f_jobs_order():
        if kind == "h":
            for c in range(2):
                ps = k.open(pe, ("L1f", "h", e, c))
                for i in range(2):
                    f = 2 * c + i
                    last = nc.tensor.matmul(ps[:, i * CAP:(i + 1) * CAP], w1[:, e * 512 + f * P:e * 512 + (f + 1) * P],
                                            T.xgT[:, e * CAP:(e + 1) * CAP], start=True, stop=True)
                k.fill(("L1f", "h", e, c), last)
        else:
            ps = k.open(pe, ("L1f", "eo", e))
            for c in range(2):
                k.drained(pe, ("L1f", "h", e, c))
            for j in range(2):
                for f in range(4):
                    last = nc.tensor.matmul(ps[0:CT, j * D:(j + 1) * D], T.h[:, e % 2, f, j * CT:(j + 1) * CT],
                                            w2[:, (4 * e + f) * D:(4 * e + f + 1) * D], start=(f == 0), stop=(f == 3))
            k.fill(("L1f", "eo", e), last)
    fold_keys_tensor(k, pe, A3)
    fold_values_tensor(k, pe, A3, 0)


def l1f_zero_pool(k, g):
    g.did(k.nc.gpsimd.memset(L1f(k).zeros, 0.0), k.parts_ready)


def l1f_zero_sync(k, sp):
    T = L1f(k)
    sp.wait_ge(k.parts_ready, 1)
    flat = lambda ap, a, b: ap[a:b, :].rearrange("(p r) d -> p (r d)", p=P)
    sp.dma_start(flat(k.slots, 0, 1024), T.zeros).then_inc(k.dram_zeroed, 16)
    sp.dma_start(flat(k.slots, 1024, NSLOT), T.zeros[:, 0:512]).then_inc(k.dram_zeroed, 16)
    sp.dma_start(flat(k.eo_rows, NSLOT, ROWS1), T.zeros).then_inc(k.dram_zeroed, 16)


def l1f_pool(k, g):
    nc, T = k.nc, L1f(k)
    g.eng.wait_ge(k.dram_zeroed, 48)
    g.eng.wait_ge(k.slots_ready, 1)
    g.eng.wait_ge(k.normed, NT * 4)
    for t in range(NT):
        nc.gpsimd.indirect_dma_start(out=k.slots[:, :], out_offset=bass.IndirectOffsetOnAxis(ap=k.idx[:, t:t + 1], axis=0),
                                     in_=k.xn[:, t, :], in_offset=None).then_inc(k.scattered, 16)
    g.eng.wait_ge(k.eo_stored, 16 * 4)
    for t in range(NT):
        nc.gpsimd.indirect_dma_start(out=T.y[:, t, :], out_offset=None, in_=k.eo_rows[:, :],
                                     in_offset=bass.IndirectOffsetOnAxis(ap=k.idx[:, t:t + 1], axis=0)).then_inc(k.y_loaded[t // TB], 16)


def l1f_sync(k, sp):
    T = L1f(k)
    for e in range(0, E8, 2):
        for i in range(2):
            k.drained(sp, ("L1f", "eo", e + i))
        sp.dma_start(k.eo_rows[e * CAP:(e + 2) * CAP, :].rearrange("(e j p) d -> p e j d", e=2, p=CT),
                     T.eo[0:CT, e:e + 2, :, :]).then_inc(k.eo_stored, 16)


class L2f:
    def __init__(self, k):
        at = PLACE["L0x"]
        self.xgT = k.cols(at, [E16, B, CAP2])
        self.hs = k.cols(at + 2048, [2, N])
        self.scb = k.cols(at + 4096, [2, S])
        at = ARENA
        self.selw = k.cols(at, [E16 // 2, B, S])
        self.eo = k.cols(at + 8192, [E16 // 2, B, D])
        self.h = k.cols(at + 10240, [4, 2, P])
        self.sel = k.cols(at, [NT, 1024], BF16)
        self.xp = k.cols(at + 4096, [3, NT * D], BF16)
        self.tmp = k.cols(at + 4096 + 1536, [NT * D])
        self.work = k.cols(at + 4096 + 2560, [S])[0:32]
        self.mask = k.cols(at + 4096 + 3072, [S])[0:32]
        self.cum = k.cols(at + 4096 + 3584, [S])[0:32]
        self.sg = k.small[:, 0:1024].rearrange("p (a b) -> p a b", a=2)
        self.ge = k.cmp[:, :, 0:256]
        self.stT = k.nmT[:, 0:S]


def l2f_pool(k, g):
    nc, T = k.nc, L2f(k)
    g.eng.wait_ge(k.normed, NT * 6)
    src = k.xn[:, :, :].rearrange("p t d -> p (t d)")
    g.did(nc.gpsimd.tensor_copy(T.xp[:, 0, :], src))
    g.settle()
    g.did(nc.gpsimd.tensor_tensor(T.tmp, src, T.xp[:, 0, :], ALU.subtract))
    g.settle()
    g.did(nc.gpsimd.tensor_copy(T.xp[:, 1, :], T.tmp))
    g.settle()
    g.did(nc.gpsimd.tensor_tensor(T.xp[:, 2, :], T.tmp, T.xp[:, 1, :], ALU.subtract), k.parts_ready)


SHARED2 = [(c, b) for c in range(2) for b in range(B)]


def l2f_vector(k, v):
    nc, T = k.nc, L2f(k)
    def shared(turn):
        c, b = SHARED2[turn]
        k.drained(v.eng, ("L2f", "sg", c, b))
        ps = k.filled(v.eng, ("L2f", "su", c, b))
        v.drain(("L2f", "su", c, b), nc.vector.tensor_tensor(T.hs[:, c, b * S:(b + 1) * S], T.sg[:, turn % 2, :], ps[:, :], ALU.mult))

    softmax_vector(k, v, "L2f", E16)
    p2 = k.rt[:, 2, :].rearrange("p (i c) -> p i c", i=TB)
    v.did(nc.vector.tensor_copy(p2.rearrange("p i (b e) -> p b i e", b=B), k.rt[:, 1, :].rearrange("p (b i e) -> p b i e", b=B, i=TB)), k.w_ready)
    v.settle()
    ps = k.filled(v.eng, ("L2f", "pT"))
    v.drain(("L2f", "pT"), nc.vector.tensor_copy(T.work, ps[0:32, :]))
    v.settle()
    for turn in range(CAP2 // 8):
        if turn % 2 and turn // 2 < len(SHARED2):
            shared(turn // 2)
        v.did(nc.vector.max(k.top8[0:32, :], T.work))
        v.settle()
        v.did(nc.vector.match_replace(out=T.work, in_to_replace=k.top8[0:32, :], in_values=T.work, imm_value=-1.0))
        v.settle()
    v.did(nc.vector.tensor_scalar(T.mask, T.work, 0.0, None, ALU.is_lt))
    v.settle()
    v.did(nc.vector.tensor_tensor_scan(T.cum, T.mask, T.mask, 0.0, ALU.add, ALU.max))
    v.settle()
    v.did(nc.vector.tensor_tensor(T.work, T.cum, T.mask, ALU.mult), k.slots_ready)
    parts = [k.mpad[:, 0:TB, 32 * i:32 * (i + 1)] for i in range(3)]
    three_parts(k, v, p2, parts, [k.rt[:, 3, :].rearrange("p (i c) -> p i c", i=TB)], None)
    ps = k.filled(v.eng, ("L2f", "slots"))
    v.drain(("L2f", "slots"), nc.vector.tensor_copy(k.mpad[:, 0:TB, 96:128], ps[:, 0:TB * 32].rearrange("p (i c) -> p i c", i=TB)))
    v.settle()
    iota = k.w("sel", "slot_iota").rearrange("p (e c) -> p e c", e=E16)
    for b in range(B):
        for i in range(TB):
            v.did(nc.vector.tensor_tensor(T.sel[:, b * TB + i, :].rearrange("p (e c) -> p e c", e=E16),
                                          bc(k.mpad[:, i, 96 + b * E16:96 + (b + 1) * E16], 2, [E16, CAP2]), iota, ALU.is_equal),
                  k.gather_sel)
    for b in range(B):
        for half in range(2):
            k.filled(v.eng, ("L2f", "xg", b, half))
    for kk in range(E16 // 2):
        for e in (2 * kk, 2 * kk + 1):
            ps = k.filled(v.eng, ("L2f", "gu", e))
            v.eng.wait_ge(k.act_copied, e + 1)
            if e >= 4:
                k.filled(v.eng, ("L2f", "eo", (e - 4) // 2))
            v.drain(("L2f", "gu", e), nc.vector.tensor_tensor(T.h[:, e % 4, :, :].rearrange("p f c -> p (f c)"), T.ge[:, e % 2, :],
                                                              ps[:, 256:512], ALU.mult))
        for b in range(B):
            ps = k.filled(v.eng, ("L2f", "bs", kk, b, 0))
            k.drained(v.eng, ("L2f", "bs", kk, b, 1))
            v.drain(("L2f", "bs", kk, b, 0), nc.vector.scalar_tensor_tensor(
                out=T.selw[:, kk, b, :], in0=ps[:, :], scalar=k.w("const", "slot_no"), in1=T.scb[:, b, :], op0=ALU.is_equal, op1=ALU.mult))


def l2f_scalar(k, a):
    nc, T = k.nc, L2f(k)
    softmax_scalar(k, a, "L2f", E16)
    for turn, (c, b) in enumerate(SHARED2):
        if turn >= 2:
            k.drained(a.eng, ("L2f", "su", *SHARED2[turn - 2]))
        ps = k.filled(a.eng, ("L2f", "sg", c, b))
        a.drain(("L2f", "sg", c, b), nc.scalar.activation(T.sg[:, turn % 2, :], ps[:, :], ACT.Gelu))
    ps = k.filled(a.eng, ("L2f", "stT"))
    a.drain(("L2f", "stT"), nc.scalar.activation(T.stT, ps[:, :].bitcast(BF16)[:, 0:S], ACT.Copy))
    for b in range(B):
        for half in range(2):
            ps = k.filled(a.eng, ("L2f", "xg", b, half))
            a.drain(("L2f", "xg", b, half), nc.scalar.activation(
                T.xgT[:, half * 8:(half + 1) * 8, b, :], ps[:, :].rearrange("p (e c) -> p e c", e=8), ACT.Copy))
    for kk in range(E16 // 2):
        for e in (2 * kk, 2 * kk + 1):
            ps = k.filled(a.eng, ("L2f", "gu", e))
            if e >= 2:
                k.drained(a.eng, ("L2f", "gu", e - 2))
            a.did(nc.scalar.activation(T.ge[:, e % 2, :], ps[:, 0:256], ACT.Gelu), k.act_copied)
        for b in range(B):
            if kk:
                k.drained(a.eng, ("L2f", "bs", kk - 1, b, 0))
            ps = k.filled(a.eng, ("L2f", "bs", kk, b, 1))
            a.drain(("L2f", "bs", kk, b, 1), nc.scalar.activation(T.scb[:, b, :], ps[:, :], ACT.Copy))
        if kk:
            eo_scalar(k, a, T, kk - 1)
    eo_scalar(k, a, T, E16 // 2 - 1)


def eo_scalar(k, a, T, kk):
    ps = k.filled(a.eng, ("L2f", "eo", kk))
    a.drain(("L2f", "eo", kk), k.nc.scalar.activation(T.eo[:, kk, :, :], ps[:, 0:2 * D].rearrange("p (b d) -> p b d", b=B), ACT.Copy))


def l2f_tensor(k, pe):
    nc, T = k.nc, L2f(k)
    logits_tensor(k, pe, "L2f", 5, E16)
    ps = k.open(pe, ("L2f", "pT"))
    pe.wait_ge(k.w_ready, 3)
    for i in range(TB):
        last = nc.tensor.transpose(ps[0:32, i * P:(i + 1) * P], k.rt[:, 2, 32 * i:32 * (i + 1)], k.w("const", "ident"))
    k.fill(("L2f", "pT"), last)
    for c, b in SHARED2:
        for kind in ("sg", "su"):
            ps = k.open(pe, ("L2f", kind, c, b))
            k.fill(("L2f", kind, c, b), nc.tensor.matmul(ps[:, :], k.w("L2f", kind)[:, c * P:(c + 1) * P], k.xnT[:, b * S:(b + 1) * S],
                                                         start=True, stop=True))
    open_acc(k, pe, 5)
    for b in range(B):
        for c in range(2):
            k.drained(pe, ("L2f", "su", c, b))
        for i in range(TB):
            t = b * TB + i
            for c in range(2):
                nc.tensor.matmul(k.acc[b][:, i * D:(i + 1) * D], T.hs[:, c, t * P:(t + 1) * P], k.w("L2f", "sd")[:, c * D:(c + 1) * D],
                                 start=(c == 0 and i == 0), stop=False, skip_group_check=True)
    ps = k.open(pe, ("L2f", "slots"))
    pe.wait_ge(k.slots_ready, 2)
    for i in range(TB):
        last = nc.tensor.transpose(ps[:, 32 * i:32 * (i + 1)], T.work[:, i * P:(i + 1) * P], k.w("const", "ident")[0:32, 0:32])
    k.fill(("L2f", "slots"), last)
    ps = k.open(pe, ("L2f", "stT"))
    k.drained(pe, ("L2f", "slots"))
    for i in range(TB):
        last = nc.tensor.transpose(ps[:, :].bitcast(BF16)[:, i * P:(i + 1) * P], k.mpad[:, i, :], k.w("sel", "ident"))
    k.fill(("L2f", "stT"), last)
    pe.wait_ge(k.parts_ready, 2)
    for b in range(B):
        for half in range(2):
            ps = k.open(pe, ("L2f", "xg", b, half))
            for i in range(TB):
                t = b * TB + i
                pe.wait_ge(k.gather_sel, t + 1)
                for part in range(3):
                    last = nc.tensor.matmul(ps[:, :], T.xp[:, part, t * D:(t + 1) * D], T.sel[:, t, half * 512:(half + 1) * 512],
                                            start=(i == 0 and part == 0), stop=(i == TB - 1 and part == 2))
            k.fill(("L2f", "xg", b, half), last)
    k.drained(pe, ("L2f", "stT"))

    def down(kk):
        ps = k.open(pe, ("L2f", "eo", kk))
        for e2 in range(2):
            e = 2 * kk + e2
            k.drained(pe, ("L2f", "gu", e))
            for b in range(B):
                for f in range(2):
                    last = nc.tensor.matmul(ps[64 * e2:64 * (e2 + 1), b * D:(b + 1) * D], T.h[:, e % 4, f, b * CAP2:(b + 1) * CAP2],
                                            k.w("L2f", "d")[:, (2 * e + f) * D:(2 * e + f + 1) * D], start=(f == 0), stop=(f == 1))
        k.fill(("L2f", "eo", kk), last)

    for kk in range(E16 // 2):
        for e in (2 * kk, 2 * kk + 1):
            ps = k.open(pe, ("L2f", "gu", e))
            for b in range(B):
                k.drained(pe, ("L2f", "xg", b, e // 8))
            for j, name in enumerate(("g", "g", "u", "u")):
                at = e * 256 + (j % 2) * P
                last = nc.tensor.matmul(ps[:, j * P:(j + 1) * P], k.w("L2f", name)[:, at:at + P],
                                        T.xgT[:, e, :, :].rearrange("p b c -> p (b c)"), start=True, stop=True)
            k.fill(("L2f", "gu", e), last)
        for b in range(B):
            for x, name in enumerate(("slot", "score")):
                ps = k.open(pe, ("L2f", "bs", kk, b, x))
                at = (b * 8 + kk) * P
                k.fill(("L2f", "bs", kk, b, x), nc.tensor.matmul(ps[:, :], k.w("sel", name)[:, at:at + P], T.stT, start=True, stop=True))
        if kk:
            down(kk - 1)
    down(E16 // 2 - 1)
    for b in range(B):
        for kk in range(E16 // 2):
            k.drained(pe, ("L2f", "bs", kk, b, 0))
            k.drained(pe, ("L2f", "eo", kk))
        for i in range(TB):
            t = b * TB + i
            out = k.acc[b][:, i * D:(i + 1) * D]
            for kk in range(E16 // 2):
                last = nc.tensor.matmul(out, T.selw[:, kk, b, i * P:(i + 1) * P], T.eo[:, kk, b, :], start=False,
                                        stop=(kk == 7 and i == TB - 1), skip_group_check=True)
        last.then_inc(k.acc_filled, 1)


def build(nc, dram, x_in, out):
    with ExitStack() as ctx:
        k = Core(nc, ctx, dram, out)
        block = ctx.enter_context(nc.Block())
        A0, A2 = Attention8(k, "L0x", 0), Attention8(k, "L2x", 4)
        A3 = Attention64(k)
        T1 = L1f(k)
        M0 = Moe(k, "L0f", 1, 6, 4)
        M3 = Moe(k, "L3f", 7, 8, 6)

        @block.sync
        def _(sp):
            def load(*groups):
                for g in groups:
                    dst = k.packed[g][:, :] if g in ("const", "ctx", "sel", "rows") else k.packed[g]
                    src = dram[g].to_broadcast([P, WIDTH[g]]) if g == "rows" else dram[g]
                    sp.dma_start(dst, src).then_inc(k.loaded[g], 16)

            sp.dma_start(k.x[:, :, :], x_in.rearrange("(t p) d -> p t d", p=P)).then_inc(k.x_loaded, 16)
            load("const", "ctx", "L0x", "rows")
            stack_keys_sync(k, sp, A0)
            stack_queries_sync(k, sp, A0, 0)
            load("sel")
            stack_queries_sync(k, sp, A0, 1)
            load("L0f", "L1x")
            stack_maxima_sync(k, sp, A0)
            load("L1f")
            l1f_zero_sync(k, sp)
            sp.wait_ge(k.x_ready, 1)
            load("L3x")
            load("L2x")
            sp.wait_ge(k.scattered, 16 * NT)
            sp.dma_start(T1.xg, k.slots[0:NSLOT, :].rearrange("(j p) d -> p j d", p=P)).then_inc(k.slots_loaded, 16)
            stack_keys_sync(k, sp, A2)
            folded_store_sync(k, sp, A3)
            l1f_sync(k, sp)
            for b in range(B):
                stack_queries_sync(k, sp, A2, b)
            stack_maxima_sync(k, sp, A2)
            load("L2f")
            sp.wait_ge(k.x_ready, 6)
            folded_load_sync(k, sp, A3)
            load("L3f")
            sp.wait_ge(k.x_ready, SUBLAYERS)
            sp.dma_start(out.rearrange("(t p) d -> p t d", p=P), k.x[:, :, :]).then_inc(k.out_stored, 16)
            sp.wait_ge(k.out_stored, 16)

        @block.gpsimd
        def _(eng):
            g = Chain(k, eng, k.pool_step)
            l1f_zero_pool(k, g)
            attention8_prep_pool(k, g, A0)
            eng.wait_ge(k.loaded["const"], 16)
            for b in range(B):
                norm_pool(k, g, 0, b)
            g.settle()
            l1x_keys_pool(k, g)
            for b in range(B):
                norm_pool(k, g, 1, b)
            for b in range(B):
                norm_pool(k, g, 2, b)
            l1x_pool(k, g)
            for b in range(B):
                norm_pool(k, g, 3, b)
            eng.wait_ge(k.acc_filled, 2 * acc_use(2) + 2)
            fold64_pool(k, g, A3)
            attention8_prep_pool(k, g, A2)
            l1f_pool(k, g)
            for b in range(B):
                norm_pool(k, g, 4, b)
            for b in range(B):
                norm_pool(k, g, 5, b)
            l2f_pool(k, g)
            for b in range(B):
                norm_pool(k, g, 6, b)
            attention64_pool(k, g, A3)
            for b in range(B):
                norm_pool(k, g, 7, b)

        @block.scalar
        def _(eng):
            a = Chain(k, eng, k.scalar_step)
            eng.wait_ge(k.loaded["rows"], 16)
            a.did(nc.scalar.activation(k.gates[:, :], k.w("rows", "g"), ACT.Tanh), k.gates_ready)
            attention8_scalar(k, a, A0)
            moe_scalar(k, a, M0)
            preload(k, a, ACT.Exp)
            for b in range(B):
                norm_scalar(k, a, 2, b)
            l1x_scalar(k, a)
            preload(k, a, ACT.Exp)
            for b in range(B):
                norm_scalar(k, a, 3, b)
            l1f_scalar(k, a, A3)
            preload(k, a, ACT.Exp)
            attention8_scalar(k, a, A2)
            for b in range(B):
                norm_scalar(k, a, 5, b)
            l2f_scalar(k, a)
            preload(k, a, ACT.Exp)
            attention64_scalar(k, a, A3)
            moe_scalar(k, a, M3)

        @block.vector
        def _(eng):
            v = Chain(k, eng, k.vector_step)

            def between(n, residual, bias=None):
                for b in range(B):
                    residual(b)
                    if b == B - 1:
                        done(k, v)
                    if n + 1 < SUBLAYERS:
                        norm_vector(k, v, n + 1, b, bias)
                if n + 1 == A2.n and n + 1 < SUBLAYERS:
                    attention8_queries_vector(k, v, A2, 0)

            v.did(nc.vector.memset(A0.ks[:, :, :, :], 0.0))
            v.did(nc.vector.memset(k.mpad[:, :, :], 0.0))
            eng.wait_ge(k.x_loaded, 16)
            eng.wait_ge(k.loaded["const"], 16)
            norm_vector(k, v, 0, 0)
            attention8_keys_vector(k, v, A0)
            attention8_values_vector(k, v, A0)
            attention8_queries_vector(k, v, A0, 0)
            norm_vector(k, v, 0, 1)
            eng.wait_ge(k.gates_ready, 1)
            for b in range(B):
                output_bias_vector(k, v, 0, b, k.w("rows", "L0_b2"))
            attention8_vector(k, v, A0)
            between(0, lambda b: residual_vector(k, v, 0, b, k.xb))
            moe_vector(k, v, M0)
            between(1, lambda b: residual_vector(k, v, 1, b, k.x), k.w("rows", "L1_bf2"))
            l1x_vector(k, v)
            between(2, lambda b: residual_vector(k, v, 2, b, k.xb, k.comb[:, 7:8]))
            l1f_vector(k, v, A2, A3)
            between(3, lambda b: l1f_residual_vector(k, v, b), k.w("rows", "L2_bo"))
            attention8_vector(k, v, A2)
            between(4, lambda b: residual_vector(k, v, 4, b, k.xb))
            l2f_vector(k, v)
            between(5, lambda b: residual_vector(k, v, 5, b, k.x), k.w("rows", "L3_bo"))
            attention64_vector(k, v, A3)
            between(6, lambda b: residual_vector(k, v, 6, b, k.xb))
            moe_vector(k, v, M3)
            between(7, lambda b: residual_vector(k, v, 7, b, k.x))

        @block.tensor
        def _(pe):
            pe.wait_ge(k.loaded["const"], 16)
            attention8_prep_tensor(k, pe, A0)
            attention8_tensor(k, pe, A0)
            moe_tensor(k, pe, M0)
            for b in range(B):
                norm_tensor(k, pe, 2, b)
            l1x_tensor(k, pe)
            for b in range(B):
                norm_tensor(k, pe, 3, b)
            l1f_tensor(k, pe, A2, A3)
            attention8_tensor(k, pe, A2)
            for b in range(B):
                norm_tensor(k, pe, 5, b)
            l2f_tensor(k, pe)
            attention64_tensor(k, pe, A3)
            moe_tensor(k, pe, M3)


def layout(np, i, bf16):
    def rows(a):
        out = np.zeros((P, a.shape[1]), a.dtype)
        out[:a.shape[0]] = a
        return out

    def chunked(a, n=P):
        return rows(a.reshape(-1, n, a.shape[1]).transpose(1, 0, 2).reshape(n, -1))

    def units(arrays):
        a = np.concatenate(arrays, axis=1).T
        return np.concatenate([a, np.zeros((1024 - a.shape[0], D), a.dtype)])

    def col(a, n=P):
        return rows(np.ascontiguousarray(a.reshape(-1, n).T))

    f32 = np.float32
    x = i["x"].reshape(N, D)
    ctxT = i["ctx_768"].reshape(NK, DC).T
    rem = np.zeros((DC, B, HG, HP), f32)
    for b in range(B):
        rem[:, b, :, :MR] = ctxT[:, None, b * M + P:(b + 1) * M]
    r = np.arange(P)[:, None]
    e = np.arange(8)
    dup = lambda w: np.concatenate([w.T, w.T], axis=1)
    kv = i["L2_xattn_Wkv"].reshape(H, 2, 8, DC)
    bkv = i["L2_xattn_bkv"].reshape(H, 2, 8)
    w1_3 = i["L3_ffn_W1"].transpose(2, 0, 1)
    s1_3 = i["L3_ffn_Ws1"].T
    w_2_1 = i["L1_ffn_w2"].reshape(8, 4, P, D).transpose(2, 0, 1, 3).reshape(P, -1)
    d_2 = i["L2_ffn_Wd"].transpose(0, 2, 1).reshape(16, 2, P, D).transpose(2, 0, 1, 3).reshape(P, -1)
    wq_3 = np.zeros((8, 2, 2, 64, D), f32)
    for odd in range(2):
        wq_3[:, odd, odd] = i["L3_xattn_Wq"].T.reshape(8, 2, 64, D)[:, odd]
    wq_3 = wq_3.reshape(16, P, D).transpose(1, 0, 2).reshape(P, -1)
    stacked = np.arange(P).reshape(8, 2, 8).transpose(1, 2, 0).reshape(P)
    parts = {
        "const": dict(
            ident=np.eye(P), ones=np.ones((P, P)),
            rem_rows=(r // HP == np.arange(HG)) & (r % HP < MR),
            earlier=np.broadcast_to((e[None, :] < e[:, None]).reshape(1, 64), (P, 64)),
            slot_no=r % CAP2 + 1, neg_half=np.full((P, 8), -0.5),
            expert_base=np.broadcast_to(np.tile(e * CAP - 1.0, 8), (P, 64)), dummy_row=NSLOT + r + P * e),
        "ctx": dict(ctxT=rows(ctxT), ctx_rem=rows(rem.reshape(DC, -1))),
        "L0x": dict(Wk=rows(i["L0_xattn_Wk"][:, stacked]), Wv=rows(i["L0_xattn_Wv"]), Wq=i["L0_xattn_Wq"][:, stacked], W1=i["L0_xattn_W1"],
                    W2=chunked(i["L0_xattn_W2"]), bq=col(i["L0_xattn_bq"][stacked]), bk=col(i["L0_xattn_bk"][stacked]), b1=col(i["L0_xattn_b1"])),
        "L0f": dict(Wr=i["L0_ffn_router_w"], gate=i["L0_ffn_gate_w"].transpose(1, 0, 2).reshape(D, -1),
                    up=i["L0_ffn_up_w"].transpose(1, 0, 2).reshape(D, -1), sgate=i["L0_ffn_s_gate_w"], sup=i["L0_ffn_s_up_w"],
                    down=chunked(i["L0_ffn_down_w"].reshape(512, D)), sdown=chunked(i["L0_ffn_s_down_w"])),
        "L1x": dict(d2v=rows(i["L1_xattn_W_d2v"].T), img=i["L1_xattn_W_img"].T, att0=dup(i["L1_xattn_W_att0"]),
                    att1=dup(i["L1_xattn_W_att1"]), txt=i["L1_xattn_W_txt"].T, f1=chunked(i["L1_xattn_W_f1"].T),
                    f2=chunked(i["L1_xattn_W_f2"].T), b_d2v=col(i["L1_xattn_b_d2v"]), b_img=col(i["L1_xattn_b_img"]),
                    b_att0=col(np.tile(i["L1_xattn_b_att0"], 2)), b_att1=col(np.tile(i["L1_xattn_b_att1"], 2)),
                    b_txt=col(i["L1_xattn_b_txt"]), b_f1=col(i["L1_xattn_b_f1"])),
        "L1f": dict(Wr=i["L1_ffn_router_w"].T, w1=i["L1_ffn_w1"].transpose(1, 0, 2).reshape(D, -1), w2=w_2_1,
                    b1=i["L1_ffn_b1"].reshape(8, 4, P).transpose(2, 0, 1).reshape(P, -1)),
        "L2x": dict(Wk=rows(kv[:, 0].reshape(P, DC)[stacked].T), Wv=rows(kv[:, 1].reshape(P, DC).T), Wq=i["L2_xattn_Wq"][stacked].T,
                    Wo=i["L2_xattn_Wo"].T, bq=col(i["L2_xattn_bq"][stacked]), bk=col(bkv[:, 0].reshape(P)[stacked])),
        "L2f": dict(Wr=i["L2_ffn_gate_w"].T, sg=i["L2_ffn_Ws_g"].T, su=i["L2_ffn_Ws_u"].T, sd=chunked(i["L2_ffn_Ws_d"].T),
                    g=i["L2_ffn_Wg"].transpose(2, 0, 1).reshape(D, -1), u=i["L2_ffn_Wu"].transpose(2, 0, 1).reshape(D, -1),
                    d=d_2),
        "L3x": dict(Wk=rows(i["L3_xattn_Wk"]), Wv=rows(i["L3_xattn_Wv"]), WqT=wq_3, Wo=chunked(i["L3_xattn_Wo"])),
        "L3f": dict(Wr=i["L3_ffn_gate_w"].T,
                    gate=units([w1_3[:, :, 96:].reshape(D, -1), s1_3[:, 192:]]).T,
                    up=units([w1_3[:, :, :96].reshape(D, -1), s1_3[:, :192]]).T,
                    down=chunked(units([i["L3_ffn_W2"].transpose(1, 0, 2).reshape(D, -1), i["L3_ffn_Ws2"]]))),
        "rows": dict(g=np.stack([i["g_xattn"], i["g_ffn"]], axis=1).reshape(1, 8), rb=i["L0_ffn_router_bias"].reshape(1, 1),
                     L0_bv=i["L0_xattn_bv"], L0_b2=i["L0_xattn_b2"], L1_bf2=i["L1_xattn_b_f2"], L1_b2=i["L1_ffn_b2"],
                     L2_bv=bkv[:, 1], L2_bo=i["L2_xattn_bo"], L3_bo=i["L3_xattn_bo"]),
    }
    m = np.arange(P)
    c = np.arange(4)
    mm = np.zeros((P, 16, P))
    for h in range(16):
        mm[h, h] = mm[16 + h, h] = 1
    s0, s3 = np.zeros((P, 4, P)), np.zeros((P, 6, P))
    slot, score = np.zeros((P, B, 8, P)), np.zeros((P, B, 8, P))
    for part in range(3):
        for q in range(8):
            s0[part * 8 + q, q // 2, (q % 2) * 64:(q % 2) * 64 + 64] = 1
            s3.reshape(P, -1)[part * 8 + q, 96 * q:96 * (q + 1)] = 1
        for b in range(B):
            for q in range(16):
                cs = slice((q % 2) * 64, (q % 2) * 64 + 64)
                score[part * 32 + b * 16 + q, b, q // 2, cs] = 1
                slot[96 + b * 16 + q, b, q // 2, cs] = 1
    parts["sel"] = dict(ident=np.eye(P), ones=np.ones((P, P)), upto=(r <= m), minus_max=mm, L0f=s0, L3f=s3, slot=slot,
                        score=score, slot_iota=np.broadcast_to(np.tile(np.arange(CAP2) + 1, 16), (P, 1024)))
    ones = np.zeros((4, H, B, 160), np.float32)
    for row in range(4):
        ones[row, row % 2::2, :, :M] = 1
    packed = {"maxrows": ones.reshape(4, -1).astype(bf16)}
    for group, items in PACK.items():
        n = 1 if group == "rows" else P
        dt = bf16 if group == "sel" else f32
        cols = [np.asarray(parts[group][name], dt).reshape(n, width) for name, width in items]
        packed[group] = np.ascontiguousarray(np.concatenate(cols, axis=1))
    return x, packed


def kernel(**inputs):
    import numpy as np
    import concourse.bacc as bacc
    from concourse.bass_utils import run_bass_kernel_spmd

    i = {name: np.asarray(a) for name, a in inputs.items()}
    x, packed = layout(np, i, mybir.dt.np(BF16))
    nc = bacc.Bacc("TRN2", target_bir_lowering=False, num_devices=1)
    arrays = {"x_in": np.ascontiguousarray(x)}
    dram = {}
    x_ap = nc.dram_tensor("x_in", x.shape, F32, kind="ExternalInput").ap()
    for group, a in packed.items():
        arrays[f"in_{group}"] = a
        dram[group] = nc.dram_tensor(f"in_{group}", a.shape, mybir.dt.from_np(a.dtype), kind="ExternalInput").ap()
    out = nc.dram_tensor("x_out", (N, D), F32, kind="ExternalOutput").ap()
    build(nc, dram, x_ap, out)
    r = run_bass_kernel_spmd(nc, [arrays], core_ids=[0])
    return r.results[0]["x_out"].reshape(B, S, D)
```
